# Optimizing a Trainium2 kernel written in Bass

```python
import numpy as np
import jax
import jax.numpy as jnp

def _softmax(x, axis=-1):
    return jax.nn.softmax(x, axis=axis)

def _gelu(x):
    return jax.nn.gelu(x, approximate=True)

def _silu(x):
    return jax.nn.silu(x)

def _sigmoid(x):
    return jax.nn.sigmoid(x)

def _layernorm(x, axis=-1, eps=1e-05):
    m = jnp.mean(x, axis=axis, keepdims=True)
    v = jnp.var(x, axis=axis, keepdims=True)
    return (x - m) / jnp.sqrt(v + eps)

def _scatter_add(tgt, idx, src, axis=0):
    return tgt.at[idx].add(src)

def _segment_sum(src, seg, n):
    return jax.ops.segment_sum(src, seg, n)
kernel_name = 'mk_gps_d2_gnn_r64_0820ae'

def setup_inputs(seed: int=0):
    np.random.seed(seed)
    _w = jnp.asarray

    def _rec_inputs():
        import jax
        import jax.numpy as jnp
        _gk = jax.random.key(seed)
        x = -8.776e-05 + 1 * jax.random.normal(jax.random.fold_in(_gk, 1), (20000, 256), jnp.float32)
        _s = jax.random.randint(jax.random.fold_in(_gk, 2), (5000,), 0, 20000, jnp.int32)
        _d = jax.random.randint(jax.random.fold_in(_gk, 3), (5000,), 0, 20000, jnp.int32)
        _loop = jnp.arange(20000, dtype=jnp.int32)
        src = jnp.concatenate([_s, _d, _loop])
        dst = jnp.concatenate([_d, _s, _loop])
        _o = jnp.argsort(dst, stable=True)
        src = src[_o]
        dst = dst[_o]
        return (x, src, dst)
    x, src, dst = _rec_inputs()

    def _L0_gnn_setup():
        import jax, jax.numpy as jnp
        import numpy as np
        N_NODES = 20000
        key = jax.random.key(seed)
        k1, k2, k3, k4 = jax.random.split(key, 4)
        d = 256
        E = 5000
        x = jax.random.normal(k1, (N_NODES, d), dtype=jnp.float32)
        edge_index = jax.random.randint(k2, (2, E), 0, N_NODES, dtype=jnp.int64)
        limit = float(np.sqrt(6.0 / (d + d)))
        W_l = jax.random.uniform(k3, (d, d), dtype=jnp.float32, minval=-limit, maxval=limit)
        W_r = jax.random.uniform(k4, (d, d), dtype=jnp.float32, minval=-limit, maxval=limit)
        b_r = jnp.zeros((d,), dtype=jnp.float32)
        return {'x': x, 'edge_index': edge_index, 'W_l': W_l, 'W_r': W_r, 'b_r': b_r}
    _L0_gnn_all = _L0_gnn_setup()
    _L0_gnn_in = {k: v for k, v in _L0_gnn_all.items() if k in ('W_l', 'W_r', 'b_r')}
    del _L0_gnn_all

    def _L0_mix_setup():
        import jax, jax.numpy as jnp
        import numpy as np
        HEADS = 8
        EPS = 1e-05

        def _ln(t, w, b, headc):
            m = jnp.mean(t, axis=-1, keepdims=True)
            d = t - m
            std = jnp.sqrt(jnp.sum(d * d, axis=-1, keepdims=True) / (headc - 1))
            return w * (d / (std + EPS)) + b
        key = jax.random.key(seed)
        B, N, C = (32, 64, 256)
        headc = C // HEADS
        x = jax.random.normal(key, (B, N, C), dtype=jnp.float32)
        return {'x': x, 'kln_weight': jnp.ones((HEADS, 1, headc), dtype=jnp.float32), 'kln_bias': jnp.zeros((HEADS, 1, headc), dtype=jnp.float32), 'vln_weight': jnp.ones((HEADS, 1, headc), dtype=jnp.float32), 'vln_bias': jnp.zeros((HEADS, 1, headc), dtype=jnp.float32)}
    _L0_mix_all = _L0_mix_setup()
    _L0_mix_in = {k: v for k, v in _L0_mix_all.items() if k in ('kln_weight', 'kln_bias', 'vln_weight', 'vln_bias')}
    del _L0_mix_all

    def _L0_ffn_setup():
        import math
        import jax, jax.numpy as jnp
        import numpy as np
        CAPACITY_FACTOR = 1.25
        key = jax.random.key(seed)
        ks = jax.random.split(key, 5)
        B, L, D, F, E = (8, 128, 256, 1024, 8)
        h = jax.random.normal(ks[0], (B, L, D), dtype=jnp.float32)
        gate_w = jax.random.normal(ks[1], (D, E), dtype=jnp.float32) * 0.02
        gate_b = jnp.zeros((E,), dtype=jnp.float32)
        w1 = jax.random.normal(ks[2], (E, D, F), dtype=jnp.float32) * (1.0 / math.sqrt(D))
        b1 = jnp.zeros((E, F), dtype=jnp.float32)
        w2 = jax.random.normal(ks[3], (E, F, D), dtype=jnp.float32) * (1.0 / math.sqrt(F))
        b2 = jnp.zeros((E, D), dtype=jnp.float32)
        return {'h': h, 'gate_w': gate_w, 'gate_b': gate_b, 'w1': w1, 'b1': b1, 'w2': w2, 'b2': b2}
    _L0_ffn_all = _L0_ffn_setup()
    _L0_ffn_in = {k: v for k, v in _L0_ffn_all.items() if k in ('gate_w', 'gate_b', 'w1', 'b1', 'w2', 'b2')}
    del _L0_ffn_all

    def _L1_gnn_setup():
        import jax, jax.numpy as jnp
        import numpy as np
        N = 50000
        E_RAND = 12500
        IN, HID, H, OUT = (256, 64, 4, 256)
        NEG_SLOPE = 0.2

        def gat_layer(h, W, a_src, a_dst, src, dst, concat):
            n = h.shape[0]
            nh, nf = a_src.shape
            hp = (h @ W.T).reshape(n, nh, nf)
            e = (hp[src] * a_src).sum(-1) + (hp[dst] * a_dst).sum(-1)
            e = jnp.where(e > 0, e, NEG_SLOPE * e)
            e_max = jax.ops.segment_max(e, dst, num_segments=n)
            ex = jnp.exp(e - e_max[dst])
            e_sum = jax.ops.segment_sum(ex, dst, num_segments=n)
            alpha = ex / (e_sum[dst] + 1e-16)
            out = jax.ops.segment_sum(hp[src] * alpha[..., None], dst, num_segments=n)
            return out.reshape(n, nh * nf) if concat else out.mean(axis=1)
        key = jax.random.key(seed)
        ks = jax.random.split(key, 8)
        x = jax.random.normal(ks[0], (N, IN), dtype=jnp.float32)
        er = jax.random.randint(ks[1], (2, E_RAND), 0, N, dtype=jnp.int32)
        loops = jnp.arange(N, dtype=jnp.int32)
        edge_index = jnp.concatenate([er, jnp.stack([loops, loops])], axis=1)
        W1 = jax.random.normal(ks[2], (H * HID, IN), jnp.float32) * (2.0 / (IN + H * HID)) ** 0.5
        a1_src = jax.random.normal(ks[3], (H, HID), jnp.float32) * 0.1
        a1_dst = jax.random.normal(ks[4], (H, HID), jnp.float32) * 0.1
        W2 = jax.random.normal(ks[5], (OUT, H * HID), jnp.float32) * (2.0 / (H * HID + OUT)) ** 0.5
        a2_src = jax.random.normal(ks[6], (1, OUT), jnp.float32) * 0.1
        a2_dst = jax.random.normal(ks[7], (1, OUT), jnp.float32) * 0.1
        return {'x': x, 'edge_index': edge_index, 'W1': W1, 'a1_src': a1_src, 'a1_dst': a1_dst, 'W2': W2, 'a2_src': a2_src, 'a2_dst': a2_dst}
    _L1_gnn_all = _L1_gnn_setup()
    _L1_gnn_in = {k: v for k, v in _L1_gnn_all.items() if k in ('W1', 'a1_src', 'a1_dst', 'W2', 'a2_src', 'a2_dst')}
    del _L1_gnn_all

    def _L1_mix_setup():
        import jax, jax.numpy as jnp
        import numpy as np
        D_MODEL = 256
        NUM_HEADS = 8
        DEPTH = D_MODEL // NUM_HEADS
        B, L = (32, 64)

        def _feature_map(x):
            return jax.nn.elu(x) + 1.0
        key = jax.random.key(seed)
        ks = jax.random.split(key, 9)
        sc = 1.0 / np.sqrt(D_MODEL)
        return {'x': jax.random.normal(ks[0], (B, L, D_MODEL), dtype=jnp.float32), 'wq': jax.random.normal(ks[1], (D_MODEL, D_MODEL), dtype=jnp.float32) * sc, 'bq': jnp.zeros((D_MODEL,), dtype=jnp.float32), 'wk': jax.random.normal(ks[2], (D_MODEL, D_MODEL), dtype=jnp.float32) * sc, 'bk': jnp.zeros((D_MODEL,), dtype=jnp.float32), 'wv': jax.random.normal(ks[3], (D_MODEL, D_MODEL), dtype=jnp.float32) * sc, 'bv': jnp.zeros((D_MODEL,), dtype=jnp.float32), 'wo': jax.random.normal(ks[4], (D_MODEL, D_MODEL), dtype=jnp.float32) * sc, 'bo': jnp.zeros((D_MODEL,), dtype=jnp.float32)}
    _L1_mix_all = _L1_mix_setup()
    _L1_mix_in = {k: v for k, v in _L1_mix_all.items() if k in ('wq', 'bq', 'wk', 'bk', 'wv', 'bv', 'wo', 'bo')}
    del _L1_mix_all

    def _L1_ffn_setup():
        import jax, jax.numpy as jnp
        import numpy as np
        B, S, D = (8, 64, 256)
        H = 4 * D
        CAPACITY = 0.5
        key = jax.random.key(seed)
        ks = jax.random.split(key, 6)
        x = jax.random.normal(ks[0], (B, S, D), dtype=jnp.float32)
        attention_mask = jnp.zeros((B, 1, 1, S), dtype=jnp.float32)
        wr = jax.random.normal(ks[1], (D, 1), dtype=jnp.float32) * 0.02
        br = jnp.zeros((1,), dtype=jnp.float32)
        w1 = jax.random.normal(ks[2], (D, H), dtype=jnp.float32) * 0.02
        b1 = jnp.zeros((H,), dtype=jnp.float32)
        w2 = jax.random.normal(ks[3], (H, D), dtype=jnp.float32) * 0.02
        b2 = jnp.zeros((D,), dtype=jnp.float32)
        return {'x': x, 'attention_mask': attention_mask, 'wr': wr, 'br': br, 'w1': w1, 'b1': b1, 'w2': w2, 'b2': b2}
    _L1_ffn_all = _L1_ffn_setup()
    _L1_ffn_in = {k: v for k, v in _L1_ffn_all.items() if k in ('attention_mask', 'wr', 'br', 'w1', 'b1', 'w2', 'b2')}
    del _L1_ffn_all
    return {'x': x, 'src': src, 'dst': dst, 'L0_gnn_W_l': _L0_gnn_in['W_l'], 'L0_gnn_W_r': _L0_gnn_in['W_r'], 'L0_gnn_b_r': _L0_gnn_in['b_r'], 'L0_mix_kln_weight': _L0_mix_in['kln_weight'], 'L0_mix_kln_bias': _L0_mix_in['kln_bias'], 'L0_mix_vln_weight': _L0_mix_in['vln_weight'], 'L0_mix_vln_bias': _L0_mix_in['vln_bias'], 'L0_ffn_gate_w': _L0_ffn_in['gate_w'], 'L0_ffn_gate_b': _L0_ffn_in['gate_b'], 'L0_ffn_w1': _L0_ffn_in['w1'], 'L0_ffn_b1': _L0_ffn_in['b1'], 'L0_ffn_w2': _L0_ffn_in['w2'], 'L0_ffn_b2': _L0_ffn_in['b2'], 'L1_gnn_W1': _L1_gnn_in['W1'], 'L1_gnn_a1_src': _L1_gnn_in['a1_src'], 'L1_gnn_a1_dst': _L1_gnn_in['a1_dst'], 'L1_gnn_W2': _L1_gnn_in['W2'], 'L1_gnn_a2_src': _L1_gnn_in['a2_src'], 'L1_gnn_a2_dst': _L1_gnn_in['a2_dst'], 'L1_mix_wq': _L1_mix_in['wq'], 'L1_mix_bq': _L1_mix_in['bq'], 'L1_mix_wk': _L1_mix_in['wk'], 'L1_mix_bk': _L1_mix_in['bk'], 'L1_mix_wv': _L1_mix_in['wv'], 'L1_mix_bv': _L1_mix_in['bv'], 'L1_mix_wo': _L1_mix_in['wo'], 'L1_mix_bo': _L1_mix_in['bo'], 'L1_ffn_attention_mask': _L1_ffn_in['attention_mask'], 'L1_ffn_wr': _L1_ffn_in['wr'], 'L1_ffn_br': _L1_ffn_in['br'], 'L1_ffn_w1': _L1_ffn_in['w1'], 'L1_ffn_b1': _L1_ffn_in['b1'], 'L1_ffn_w2': _L1_ffn_in['w2'], 'L1_ffn_b2': _L1_ffn_in['b2']}

def reference(x, src, dst, L0_gnn_W_l, L0_gnn_W_r, L0_gnn_b_r, L0_mix_kln_weight, L0_mix_kln_bias, L0_mix_vln_weight, L0_mix_vln_bias, L0_ffn_gate_w, L0_ffn_gate_b, L0_ffn_w1, L0_ffn_b1, L0_ffn_w2, L0_ffn_b2, L1_gnn_W1, L1_gnn_a1_src, L1_gnn_a1_dst, L1_gnn_W2, L1_gnn_a2_src, L1_gnn_a2_dst, L1_mix_wq, L1_mix_bq, L1_mix_wk, L1_mix_bk, L1_mix_wv, L1_mix_bv, L1_mix_wo, L1_mix_bo, L1_ffn_attention_mask, L1_ffn_wr, L1_ffn_br, L1_ffn_w1, L1_ffn_b1, L1_ffn_w2, L1_ffn_b2):
    import jax
    import jax.numpy as jnp

    def _L0_gnn_ref(x, edge_index, W_l, W_r, b_r):
        import jax, jax.numpy as jnp
        import numpy as np
        N_NODES = 20000
        src, dst = (edge_index[0], edge_index[1])
        messages = x[src]
        sums = jax.ops.segment_sum(messages, dst, num_segments=N_NODES)
        counts = jax.ops.segment_sum(jnp.ones_like(dst, dtype=x.dtype), dst, num_segments=N_NODES)
        aggr = sums / jnp.maximum(counts, 1.0)[:, None]
        out = aggr @ W_l.T + x @ W_r.T + b_r
        return out

    def _L0_mix_ref(x, kln_weight, kln_bias, vln_weight, vln_bias):
        import jax, jax.numpy as jnp
        import numpy as np
        HEADS = 8
        EPS = 1e-05

        def _ln(t, w, b, headc):
            m = jnp.mean(t, axis=-1, keepdims=True)
            d = t - m
            std = jnp.sqrt(jnp.sum(d * d, axis=-1, keepdims=True) / (headc - 1))
            return w * (d / (std + EPS)) + b
        B, N, C = x.shape
        headc = C // HEADS
        qkv = x.reshape(B, N, HEADS, headc).transpose(0, 2, 1, 3)
        k = _ln(qkv, kln_weight, kln_bias, headc)
        v = _ln(qkv, vln_weight, vln_bias, headc)
        kv = jnp.einsum('bhnd,bhne->bhde', k, v) / N
        out = jnp.einsum('bhnd,bhde->bhne', qkv, kv)
        out = out.transpose(0, 2, 1, 3).reshape(B, N, C)
        return out + x

    def _L0_ffn_ref(h, gate_w, gate_b, w1, b1, w2, b2):
        import math
        import jax, jax.numpy as jnp
        import numpy as np
        CAPACITY_FACTOR = 1.25
        B, L, D = h.shape
        E = gate_w.shape[1]
        T = B * L
        C = max(1, math.ceil(CAPACITY_FACTOR * T / E))
        x = h.reshape(T, D)
        logits = x @ gate_w + gate_b
        probs = jax.nn.softmax(logits, axis=-1)
        idx = jnp.argmax(probs, axis=-1)
        prb = jnp.take_along_axis(probs, idx[:, None], axis=1)[:, 0]
        one_hot = jax.nn.one_hot(idx, E, dtype=jnp.float32)
        pos = (jnp.cumsum(one_hot, axis=0) * one_hot).sum(-1).astype(jnp.int32) - 1
        kept = pos < C
        pos_safe = jnp.where(kept, pos, C)
        buf = jnp.zeros((E, C, D), dtype=h.dtype).at[idx, pos_safe].set(x, mode='drop')
        hmid = jax.nn.relu(jnp.einsum('ecd,edf->ecf', buf, w1) + b1[:, None, :])
        ybuf = jnp.einsum('ecf,efd->ecd', hmid, w2) + b2[:, None, :]
        pos_g = jnp.minimum(pos, C - 1)
        y_tok = ybuf[idx, pos_g] * (prb * kept)[:, None]
        y = y_tok.reshape(B, L, D)
        y = jnp.nan_to_num(y, nan=0.0, posinf=10000.0, neginf=-10000.0)
        return y

    def _L1_gnn_ref(x, edge_index, W1, a1_src, a1_dst, W2, a2_src, a2_dst):
        import jax, jax.numpy as jnp
        import numpy as np
        N = 50000
        E_RAND = 12500
        IN, HID, H, OUT = (256, 64, 4, 256)
        NEG_SLOPE = 0.2

        def gat_layer(h, W, a_src, a_dst, src, dst, concat):
            n = h.shape[0]
            nh, nf = a_src.shape
            hp = (h @ W.T).reshape(n, nh, nf)
            e = (hp[src] * a_src).sum(-1) + (hp[dst] * a_dst).sum(-1)
            e = jnp.where(e > 0, e, NEG_SLOPE * e)
            e_max = jax.ops.segment_max(e, dst, num_segments=n)
            ex = jnp.exp(e - e_max[dst])
            e_sum = jax.ops.segment_sum(ex, dst, num_segments=n)
            alpha = ex / (e_sum[dst] + 1e-16)
            out = jax.ops.segment_sum(hp[src] * alpha[..., None], dst, num_segments=n)
            return out.reshape(n, nh * nf) if concat else out.mean(axis=1)
        src, dst = (edge_index[0], edge_index[1])
        h = jax.nn.relu(gat_layer(x, W1, a1_src, a1_dst, src, dst, True))
        return gat_layer(h, W2, a2_src, a2_dst, src, dst, False)

    def _L1_mix_ref(x, wq, bq, wk, bk, wv, bv, wo, bo):
        import jax, jax.numpy as jnp
        import numpy as np
        D_MODEL = 256
        NUM_HEADS = 8
        DEPTH = D_MODEL // NUM_HEADS
        B, L = (32, 64)

        def _feature_map(x):
            return jax.nn.elu(x) + 1.0
        b, l, _ = x.shape
        q = (x @ wq + bq).reshape(b, l, NUM_HEADS, DEPTH)
        k = (x @ wk + bk).reshape(b, l, NUM_HEADS, DEPTH)
        v = (x @ wv + bv).reshape(b, l, NUM_HEADS, DEPTH)
        q = _feature_map(q)
        k = _feature_map(k)
        kv = jnp.einsum('blhd,blhe->bhde', k, v)
        k_sum = jnp.sum(k, axis=1)
        qkv = jnp.einsum('blhd,bhde->blhe', q, kv)
        normalizer = jnp.einsum('blhd,bhd->blh', q, k_sum) + 1e-06
        out = qkv / normalizer[..., None]
        out = out.reshape(b, l, D_MODEL)
        return out @ wo + bo

    def _L1_ffn_ref(x, attention_mask, wr, br, w1, b1, w2, b2):
        import jax, jax.numpy as jnp
        import numpy as np
        B, S, D = (8, 64, 256)
        H = 4 * D
        CAPACITY = 0.5
        b, s, d = x.shape
        weights = (jnp.einsum('bsd,do->bso', x, wr) + br)[..., 0]
        k = max(1, int(CAPACITY * s))
        kk = k - 1 if k > 1 else 1
        _, idx = jax.lax.top_k(weights, k)
        sel_idx = idx[:, :kk]
        sel = jnp.take_along_axis(x, sel_idx[:, :, None], axis=1)
        h = jax.nn.gelu(jnp.einsum('bkd,dh->bkh', sel, w1) + b1)
        y = jnp.einsum('bkh,hd->bkd', h, w2) + b2
        w_sel = jnp.take_along_axis(weights, sel_idx, axis=1)
        y = y * w_sel[..., None]
        batch_idx = jnp.arange(b)[:, None]
        processed = jnp.zeros_like(x).at[batch_idx, sel_idx].set(y)
        return processed + x
    edge_index = jnp.stack([src, dst])
    xn = _layernorm(x, axis=-1)
    x = x + _L0_gnn_ref(xn, edge_index, L0_gnn_W_l, L0_gnn_W_r, L0_gnn_b_r) + _L0_mix_ref(xn[None], L0_mix_kln_weight, L0_mix_kln_bias, L0_mix_vln_weight, L0_mix_vln_bias)[0]
    x = x + _L0_ffn_ref(_layernorm(x, axis=-1)[None], L0_ffn_gate_w, L0_ffn_gate_b, L0_ffn_w1, L0_ffn_b1, L0_ffn_w2, L0_ffn_b2)[0]
    xn = _layernorm(x, axis=-1)
    x = x + _L1_gnn_ref(xn, edge_index, L1_gnn_W1, L1_gnn_a1_src, L1_gnn_a1_dst, L1_gnn_W2, L1_gnn_a2_src, L1_gnn_a2_dst) + _L1_mix_ref(xn[None], L1_mix_wq, L1_mix_bq, L1_mix_wk, L1_mix_bk, L1_mix_wv, L1_mix_bv, L1_mix_wo, L1_mix_bo)[0]
    x = x + _L1_ffn_ref(_layernorm(x, axis=-1)[None], L1_ffn_attention_mask, L1_ffn_wr, L1_ffn_br, L1_ffn_w1, L1_ffn_b1, L1_ffn_w2, L1_ffn_b2)[0]
    return x

_drawn_inputs = setup_inputs


def setup_inputs(seed=0):
    import zlib

    import numpy as np

    out = dict(_drawn_inputs(seed))
    spreads = {'L0_gnn_b_r': (0.0, 0.1),
     'L0_mix_kln_weight': (1.0, 0.2),
     'L0_mix_kln_bias': (0.0, 0.49),
     'L0_mix_vln_weight': (1.0, 0.2),
     'L0_mix_vln_bias': (0.0, 0.495),
     'L0_ffn_gate_b': (0.0, 0.276),
     'L0_ffn_b1': (0.0, 0.8),
     'L0_ffn_b2': (0.0, 0.8),
     'L1_mix_bq': (0.0, 0.8),
     'L1_mix_bk': (0.0, 0.8),
     'L1_mix_bv': (0.0, 0.1),
     'L1_mix_bo': (0.0, 0.1),
     'L1_ffn_b1': (0.0, 0.8),
     'L1_ffn_b2': (0.0, 0.8)}
    factors = {'L1_gnn_a1_dst': 8.0,
     'L1_gnn_a2_src': 8.0,
     'L1_gnn_a2_dst': 8.0,
     'L1_mix_wq': 8.0,
     'L1_mix_wk': 8.0,
     'L1_mix_wv': 5.925,
     'L1_ffn_wr': 8.0,
     'L1_ffn_w1': 8.0,
     'L1_ffn_w2': 8.0}
    for name, (base, spread) in spreads.items():
        noise = np.random.default_rng([zlib.crc32(name.encode()), seed]).standard_normal(out[name].shape)
        drawn = base * np.exp(spread * noise) if base else spread * noise
        out[name] = jnp.asarray(drawn.astype(out[name].dtype))
    for name, factor in factors.items():
        out[name] = (out[name] * factor).astype(out[name].dtype)
    return out
```

```python
from contextlib import ExitStack

import numpy as np

import concourse.bass as bass
from concourse import mybir

F32 = mybir.dt.float32
I32 = mybir.dt.int32
ALU = mybir.AluOpType
ACT = mybir.ActivationFunctionType
AX = mybir.AxisListType

P = 128
D = 256
KC = D // P
N = 20000
J = 4
GROUP = P * J
G = -(-N // GROUP)
G += G % 2
NP = G * GROUP
FULL_G, LAST_P = N // GROUP, (N % GROUP) // J
E = 30000
ET = -(-E // P)
EP = ET * P
EU = 5
HEADS, HC = 8, 32
LN_EPS = 1e-5
EXPERTS, FF = 8, 1024
CAP = 3125
MB = 7
MT = 112
MROWS = MT * J * MB
GH = 4
SEL = N // 2 - 1
SB = 20
SW = 2 * D + 2
FAR = 1.0e6
BIG = 1.0e30


def sb(c, nc, name, shape, dt=F32):
    return c.enter_context(nc.sbuf_tensor(name, shape, dt))


def ps(c, nc, name, shape, dt=F32):
    return c.enter_context(nc.psum_tensor(name, shape, dt))


def sem(c, nc, name):
    handle = nc.alloc_semaphore(name)
    c.semaphores.append(handle)
    return handle


class Stage(ExitStack):

    def __init__(self, nc):
        super().__init__()
        self.nc, self.semaphores = nc, []

    def __exit__(self, *error):
        super().__exit__(*error)
        if error[0] is None:
            self.nc.clear_and_free_semaphores(self.semaphores)
            self.nc.all_engine_barrier()


def rows(dram, g):
    return dram[bass.ds(g * GROUP, GROUP), :].rearrange("(p j) d -> p j d", j=J)


def wait_all(eng, tick, *waits):
    for s, v in waits:
        eng.wait_ge(s, v)
    eng.sem_inc(tick, 1)


class Steps:

    def __init__(self, eng, semaphore, turn=0, per=0):
        self.eng, self.sem, self.base, self.per, self.k = eng, semaphore, turn * per, per, 0

    def then(self, instruction, tick=None):
        self.k += 1
        instruction.then_inc(self.sem, 1)
        self.eng.wait_ge(self.sem, self.base + self.k)
        if tick is not None:
            self.eng.sem_inc(tick, 1)

    def end(self):
        assert self.k == self.per, (self.k, self.per)


def row_mean_var(v, step, tick, x, stats, mv, ve):
    for j in range(J):
        i = v.bn_stats(stats[:, j, :], x[:, j, :])
    step.then(i, tick)
    for j in range(J):
        i = v.bn_aggr(mv[:, j, :], stats[:, j, :])
    step.then(i)
    return v.tensor_scalar(ve, mv[:, :, 1], LN_EPS, None, ALU.add)


def inverse_root(v, step, rs, ve, nt):
    step.then(v.tensor_scalar(rs[:, :].bitcast(I32), ve[:, :].bitcast(I32), -0.5, float(0x5F3759DF), ALU.mult, ALU.add))
    for n in range(3):
        step.then(v.tensor_tensor(nt[:, :], rs[:, :], rs[:, :], ALU.mult))
        step.then(v.scalar_tensor_tensor(nt[:, :], nt[:, :], -0.5, ve[:, :], ALU.mult, ALU.mult))
        step.then(v.scalar_tensor_tensor(rs[:, :], nt[:, :], 1.5, rs[:, :], ALU.add, ALU.mult))


def norm_and_gram(nc, T, C):
    with Stage(nc) as c:
        x_t = sb(c, nc, "a_x", [P, 2, J, D])
        xn_t = sb(c, nc, "a_xn", [P, 2, J, D])
        d_t = sb(c, nc, "a_d", [P, J, D])
        sq_t = sb(c, nc, "a_sq", [P, J, D])
        z_t = sb(c, nc, "a_z", [P, 2, J, KC, P + 1])
        stats = sb(c, nc, "a_stats", [P, J, 6])
        mv = sb(c, nc, "a_mv", [P, J, 2])
        ve = sb(c, nc, "a_ve", [P, J])
        sd = sb(c, nc, "a_sd", [P, J])
        rs = sb(c, nc, "a_rs", [P, J])
        hm = sb(c, nc, "a_hm", [P, J * HEADS])
        hv = sb(c, nc, "a_hv", [P, J * HEADS])
        hsd = sb(c, nc, "a_hsd", [P, J * HEADS])
        hr = sb(c, nc, "a_hr", [P, J * HEADS])
        zero = sb(c, nc, "a_zero", [P, 512])
        gram = sb(c, nc, "a_gram", [P, KC, P + 1])
        sdiag = sb(c, nc, "a_sdiag", [P, KC, P])
        srow = sb(c, nc, "a_srow", [P, KC, P])
        kcol = sb(c, nc, "a_kcol", [P, 2, KC])
        vrow = sb(c, nc, "a_vrow", [P, 2, D])
        kv = sb(c, nc, "a_kv", [P, KC, P])
        t1 = sb(c, nc, "a_t1", [P, P])
        t2 = sb(c, nc, "a_t2", [P, P])
        cs = sb(c, nc, "a_cs", [P, 1])
        zf = sb(c, nc, "a_zf", [P, 2560])
        pg = ps(c, nc, "a_pg", [P, KC, 256])
        pr = ps(c, nc, "a_pr", [P, KC, 256])
        x_in = [sem(c, nc, f"a_x_in{b}") for b in range(2)]
        xn_out = [sem(c, nc, f"a_xn_out{b}") for b in range(2)]
        s_step = sem(c, nc, "a_step")
        s_fin = sem(c, nc, "a_fin")
        s_var = sem(c, nc, "a_var")
        s_std = sem(c, nc, "a_std")
        s_xn = sem(c, nc, "a_s_xn")
        s_d = sem(c, nc, "a_s_d")
        s_sq = sem(c, nc, "a_s_sq")
        s_hv = sem(c, nc, "a_s_hv")
        s_hsd = sem(c, nc, "a_s_hsd")
        s_z = sem(c, nc, "a_s_z")
        z_free = sem(c, nc, "a_z_free")
        s_gram = sem(c, nc, "a_s_gram")
        s_diag = sem(c, nc, "a_s_diag")
        s_srow = sem(c, nc, "a_s_srow")
        s_zero = sem(c, nc, "a_s_zero")
        s_par = sem(c, nc, "a_s_par")
        s_fill = sem(c, nc, "a_s_fill")
        s_zf = sem(c, nc, "a_s_zf")
        tick = sem(c, nc, "a_tick")
        block = c.enter_context(nc.Block())
        per = 6

        @block.sync
        def _(sp):
            sp.dma_start(kcol[:, 0, :], T["kln_weight"]).then_inc(s_par, 16)
            sp.dma_start(kcol[:, 1, :], T["kln_bias"]).then_inc(s_par, 16)
            sp.dma_start(vrow[:, 0, :], T["vln_weight"].partition_broadcast(P)).then_inc(s_par, 16)
            sp.dma_start(vrow[:, 1, :], T["vln_bias"].partition_broadcast(P)).then_inc(s_par, 16)
            for b in range(2):
                sp.dma_start(x_t[:, b], rows(T["x"], b)).then_inc(x_in[b], 16)
            with sp.Fori(0, G // 2 - 1) as u:
                for b in range(2):
                    g = u * 2 + b
                    sp.wait_ge(s_xn, g + 1)
                    sp.dma_start(x_t[:, b], rows(T["x"], g + 2)).then_inc(x_in[b], 16)
                    sp.dma_start(rows(T["xn"], g), xn_t[:, b]).then_inc(xn_out[b], 16)
            for b in range(2):
                sp.wait_ge(s_xn, G - 1 + b)
                sp.dma_start(rows(T["xn"], G - 2 + b), xn_t[:, b]).then_inc(xn_out[b], 16)
            for b in range(2):
                sp.wait_ge(xn_out[b], 16 * (G // 2))

        @block.gpsimd
        def _(pool):
            pool.memset(zf[:, :], 0.0).then_inc(s_zf, 1)
            pool.wait_ge(s_zf, 1)
            n = 0
            for dram, count in ((T["agg"], NP * D // P), (T["slots"], (EXPERTS * MB + 1) * MT * J * D // P)):
                w = dram.rearrange("r d -> (r d)").rearrange("(p n) -> p n", p=P)
                for a in range(0, count, 2560):
                    k = min(2560, count - a)
                    pool.dma_start(w[:, a:a + k], zf[:, 0:k]).then_inc(s_fill, 16)
                    n += 1
            pool.wait_ge(s_fill, 16 * n)

        @block.scalar
        def _(act):
            with act.Fori(0, G) as g:
                act.wait_ge(s_var, g + 1)
                act.activation(sd[:, :], ve[:, :], ACT.Sqrt).then_inc(s_std, 1)
                act.wait_ge(s_d, g + 1)
                act.activation(sq_t[:, :, :], d_t[:, :, :], ACT.Square).then_inc(s_sq, 1)
                act.wait_ge(s_hv, g + 1)
                act.activation(hsd[:, :], hv[:, :], ACT.Sqrt, scale=1.0 / (HC - 1)).then_inc(s_hsd, 1)

        @block.tensor
        def _(pe):
            pe.wait_ge(s_zero, 1)
            pe.matmul(pg[:, :, :], zero[:, 0:P], zero[:, :], start=True, stop=False, skip_group_check=True)
            pe.sem_inc(z_free, 2)
            with pe.Fori(0, G // 2) as u:
                for b in range(2):
                    pe.wait_ge(s_z, u * 2 + b + 1)
                    for j in range(J):
                        for h in range(KC):
                            i = pe.matmul(pg[:, h, 0:P + 1], z_t[:, b, j, h, 0:P], z_t[:, b, j, h, :],
                                          start=False, stop=False, skip_group_check=True)
                    i.then_inc(z_free, 1)
            pe.matmul(pg[:, :, :], zero[:, 0:P], zero[:, :], start=False, stop=True,
                      skip_group_check=True).then_inc(s_gram, 1)
            pe.wait_ge(s_diag, 1)
            for h in range(KC):
                i = pe.matmul(pr[:, h, 0:P], C["ones"][:, :], sdiag[:, h, :], start=(h == 0), stop=True,
                              skip_group_check=True)
            i.then_inc(s_srow, 1)

        @block.vector
        def _(v):
            v.memset(zero[:, :], 0.0).then_inc(s_zero, 1)
            for b in range(2):
                i = v.memset(z_t[:, b, :, :, P:P + 1], 1.0)
            i.then_inc(s_fin, 1)
            v.wait_ge(s_fin, 1)
            with v.Fori(0, G // 2) as u:
                for b in range(2):
                    g = u * 2 + b
                    step = Steps(v, s_step, g, per)
                    x, xn, z = x_t[:, b], xn_t[:, b], z_t[:, b]
                    v.wait_ge(x_in[b], u * 16 + 16)
                    row_mean_var(v, step, tick, x, stats, mv, ve[:, :]).then_inc(s_var, 1)
                    v.wait_ge(s_std, g + 1)
                    step.then(v.reciprocal(rs[:, :], sd[:, :]))
                    v.wait_ge(xn_out[b], u * 16)
                    for j in range(J):
                        i = v.tensor_scalar(xn[:, j, :], x[:, j, :], mv[:, j, 0:1], rs[:, j:j + 1],
                                            ALU.subtract, ALU.mult)
                    i.then_inc(s_xn, 1)
                    v.wait_ge(s_xn, g + 1)
                    heads = xn.rearrange("p j (h k) -> p (j h) k", k=HC)
                    step.then(v.tensor_reduce(hm[:, :], heads, AX.X, ALU.add))
                    dh = d_t[:, :, :].rearrange("p j (h k) -> p (j h) k", k=HC)
                    v.scalar_tensor_tensor(dh, hm[:, :].unsqueeze(2).to_broadcast([P, J * HEADS, HC]), -1.0 / HC,
                                           heads, ALU.mult, ALU.add).then_inc(s_d, 1)
                    v.wait_ge(s_sq, g + 1)
                    v.tensor_reduce(hv[:, :], sq_t[:, :, :].rearrange("p j (h k) -> p (j h) k", k=HC), AX.X,
                                    ALU.add).then_inc(s_hv, 1)
                    v.wait_ge(s_hsd, g + 1)
                    step.then(v.tensor_scalar(hr[:, :], hsd[:, :], 1e-5, None, ALU.add))
                    step.then(v.reciprocal(hr[:, :], hr[:, :]))
                    v.wait_ge(z_free, g + 1)
                    v.tensor_tensor(z[:, :, :, 0:P].rearrange("p j c (h k) -> p (j c) h k", k=HC),
                                    d_t[:, :, :].rearrange("p j (c h k) -> p (j c) h k", c=KC, k=HC),
                                    hr[:, :].rearrange("p (a h) -> p a h", h=HEADS // KC).unsqueeze(3)
                                    .to_broadcast([P, J * KC, HEADS // KC, HC]), ALU.mult).then_inc(s_z, 1)
                    step.end()
            step = Steps(v, s_fin)
            step.k = 1
            v.wait_ge(s_gram, 1)
            step.then(v.tensor_copy(gram[:, :, :], pg[:, :, 0:P + 1]))
            for h in range(KC):
                i = v.tensor_scalar(sdiag[:, h, :], C["ident"][:, :], gram[:, h, P:P + 1], None, ALU.mult)
            i.then_inc(s_diag, 1)
            v.wait_ge(s_srow, 1)
            step.then(v.tensor_copy(srow[:, :, :], pr[:, :, 0:P]))
            v.wait_ge(s_par, 64)
            for h in range(KC):
                wv, bv = vrow[:, 0, h * P:(h + 1) * P], vrow[:, 1, h * P:(h + 1) * P]
                wk, bk = kcol[:, 0, h:h + 1], kcol[:, 1, h:h + 1]
                step.then(v.scalar_tensor_tensor(t1[:, :], gram[:, h, 0:P], wk, wv, ALU.mult, ALU.mult))
                step.then(v.tensor_tensor(cs[:, :], gram[:, h, P:P + 1], wk, ALU.mult))
                step.then(v.scalar_tensor_tensor(t1[:, :], bv, cs[:, 0:1], t1[:, :], ALU.mult, ALU.add))
                step.then(v.tensor_tensor(t2[:, :], srow[:, h, :], wv, ALU.mult))
                step.then(v.scalar_tensor_tensor(t2[:, :], bv, float(N), t2[:, :], ALU.mult, ALU.add))
                step.then(v.scalar_tensor_tensor(t1[:, :], t2[:, :], bk, t1[:, :], ALU.mult, ALU.add))
                step.then(v.scalar_tensor_tensor(kv[:, h, :], t1[:, :], 1.0 / N, C["heads"][:, :], ALU.mult, ALU.mult))
                step.then(v.tensor_tensor(kv[:, h, :], kv[:, h, :], C["ident"][:, :], ALU.add))
                w = C["wr"][:, h, h * P:(h + 1) * P]
                step.then(v.tensor_tensor(w, w, kv[:, h, :], ALU.add))


def load_constants(nc, T, C):
    with Stage(nc) as c:
        s_in = sem(c, nc, "c_in")
        s_step = sem(c, nc, "c_step")
        di = sb(c, nc, "c_dst_i", [P, ET], I32)
        ni = sb(c, nc, "c_next_i", [P, ET], I32)
        li = sb(c, nc, "c_lane_i", [P, 3, ET], I32)
        nf = sb(c, nc, "c_next_f", [P, ET])
        lf = sb(c, nc, "c_lane_f", [P, 3, ET])
        lt = sb(c, nc, "c_last", [P, 2])
        tick = sem(c, nc, "c_tick")
        block = c.enter_context(nc.Block())
        loads = [
            (C["ident"][:, :], T["c_ident"]), (C["tri"][:, :], T["c_tri"]), (C["heads"][:, :], T["c_heads"]),
            (lt[:, :], T["c_last"]), (C["valid"][:, :], T["c_valid"]),
            (C["valid_cols"][:, :], T["c_valid_cols"]), (C["ids"][:, :], T["c_ids"]),
            (C["wl"][:, :, :], T["W_l_t"].rearrange("(c p) n -> p c n", p=P)),
            (C["wr"][:, :, :], T["W_r_t"].rearrange("(c p) n -> p c n", p=P)),
            (di[:, :], T["dst_tile"]), (ni[:, :], T["next_tile"]), (C["src_i"][:, :], T["src_tile"]),
            (C["lane_i"][:, :, :], T["lane_i"]),
            (li[:, 0, :], T["key_lane"]), (li[:, 1, :], T["prev_lane"]), (li[:, 2, :], T["next_lane"]),
        ]

        @block.sync
        def _(sp):
            for out, in_ in loads:
                sp.dma_start(out, in_).then_inc(s_in, 16)

        @block.vector
        def _(v):
            step = Steps(v, s_step)
            step.then(v.memset(C["ones"][:, :], 1.0))
            v.wait_ge(s_in, 16 * len(loads))
            step.then(v.tensor_copy(C["dst_f"][:, :], di[:, :]))
            step.then(v.tensor_copy(nf[:, :], ni[:, :]))
            step.then(v.tensor_tensor(nf[:, :], nf[:, :], C["dst_f"][:, :], ALU.is_equal))
            step.then(v.scalar_tensor_tensor(nf[:, :], nf[:, :], FAR, C["dst_f"][:, :], ALU.mult, ALU.add))
            step.then(v.tensor_copy(C["out_i"][:, :], nf[:, :]))
            step.then(v.memset(C["carry_f"][:, :], -5.0))
            step.then(v.tensor_scalar(C["carry_f"][:, 1:ET], C["dst_f"][:, 0:ET - 1], lt[:, 0:1], lt[:, 1:2],
                                      ALU.mult, ALU.add))
            step.then(v.tensor_copy(lf[:, :, :], li[:, :, :]))
            step.then(v.tensor_tensor(C["same_prev"][:, :], lf[:, 0, :], lf[:, 1, :], ALU.is_equal))
            step.then(v.tensor_tensor(C["same_next"][:, :], lf[:, 0, :], lf[:, 2, :], ALU.is_equal))
            step.then(v.tensor_scalar(C["cut_prev"][:, :], C["same_prev"][:, :], 1.0, BIG, ALU.subtract, ALU.mult))
            step.then(v.tensor_scalar(C["cut_next"][:, :], C["same_next"][:, :], -1.0, 1.0, ALU.mult, ALU.add))
            step.then(v.tensor_reduce(C["all_prev"][:, :], C["same_prev"][:, :], AX.X, ALU.min))
            step.then(v.tensor_scalar(C["cut_whole"][:, :], C["all_prev"][:, :], 1.0, BIG, ALU.subtract, ALU.mult))
            step.then(v.tensor_reduce(C["all_next"][:, :], C["same_next"][:, :], AX.X, ALU.min))


class Segments:

    def __init__(self, c, nc, T, C, name, heads):
        self.T, self.C, self.h = T, C, heads
        self.f = sb(c, nc, name + "_scan", [P, heads, ET])
        self.g = sb(c, nc, name + "_back", [P, heads, ET])
        self.ends = sb(c, nc, name + "_ends", [P, 2, heads])
        self.row = sb(c, nc, name + "_row", [1, 2, heads, P])
        self.out = sb(c, nc, name + "_out", [1, heads, P + 1])
        self.start = sb(c, nc, name + "_start", [P, heads])
        self.s_ends = sem(c, nc, name + "_s_ends")
        self.s_row = sem(c, nc, name + "_s_row")
        self.s_out = sem(c, nc, name + "_s_out")
        self.s_start = sem(c, nc, name + "_s_start")
        self.s_hop = sem(c, nc, name + "_s_hop")
        self.n = 0

    def carry(self, sp, passes):
        hop = 0
        for n in range(passes):
            ends_d, out_d = self.T["ends"], self.T["starts"]
            h = self.h
            sp.wait_ge(self.s_ends, n + 1)
            sp.dma_start(ends_d[0:2 * h, :].rearrange("a p -> p a"), self.ends[:, :, :].rearrange("p a h -> p (a h)"),
                         allow_slow_non_contiguous=True).then_inc(self.s_hop, 16)
            hop += 16
            sp.wait_ge(self.s_hop, hop)
            sp.dma_start(self.row[:, :, :, :].rearrange("o a h p -> o (a h p)"),
                         ends_d[0:2 * h, :].rearrange("a p -> (a p)").unsqueeze(0)).then_inc(self.s_row, 16)
            sp.wait_ge(self.s_out, n + 1)
            sp.dma_start(out_d[0:h, :].rearrange("a p -> (a p)").unsqueeze(0),
                         self.out[:, :, :].rearrange("o h p -> o (h p)")).then_inc(self.s_hop, 16)
            hop += 16
            sp.wait_ge(self.s_hop, hop)
            o = 0 if n % 2 == 0 else 1
            sp.dma_start(self.start[:, :], out_d[0:h, o:o + P].rearrange("a p -> p a"),
                         allow_slow_non_contiguous=True).then_inc(self.s_start, 16)

    def scan(self, v, step, out, data0, data1, op0, op1, back, whole, first):
        h = self.h
        flip = (lambda a: a[:, ::-1]) if back else (lambda a: a)
        for k in range(h):
            i = v.tensor_tensor_scan(flip(out[:, k, :]), flip(data0), flip(data1[:, k, :]), first, op0, op1)
        step.then(i)
        for k in range(h):
            v.tensor_copy(self.ends[:, 0, k:k + 1], out[:, k, 0:1] if back else out[:, k, ET - 1:ET])
            i = v.tensor_copy(self.ends[:, 1, k:k + 1], whole)
        i.then_inc(self.s_ends, 1)
        n = self.n
        v.wait_ge(self.s_row, 16 * (n + 1))
        step.then(v.memset(self.out[:, :, :], first))
        for k in range(h):
            o = self.out[:, k, 0:P] if back else self.out[:, k, 1:P + 1]
            i = v.tensor_tensor_scan(flip(o), flip(self.row[:, 1, k, :]), flip(self.row[:, 0, k, :]), first, op0, op1)
        i.then_inc(self.s_out, 1)
        v.wait_ge(self.s_start, 16 * (n + 1))
        for k in range(h):
            i = v.tensor_tensor_scan(flip(out[:, k, :]), flip(data0), flip(data1[:, k, :]), self.start[:, k:k + 1],
                                     op0, op1)
        step.then(i)
        self.n += 1

    def total(self, v, step, x, largest):
        C = self.C
        if largest:
            self.scan(v, step, self.f, C["cut_prev"][:, :], x, ALU.add, ALU.max, False, C["cut_whole"][:, :], -BIG)
        else:
            self.scan(v, step, self.f, C["same_prev"][:, :], x, ALU.mult, ALU.add, False, C["all_prev"][:, :], 0.0)
        cut = C["cut_next"][:, :].unsqueeze(1).to_broadcast([P, self.h, ET])
        step.then(v.tensor_tensor(self.f[:, :, :], self.f[:, :, :], cut, ALU.mult))
        self.scan(v, step, self.g, C["same_next"][:, :], self.f, ALU.mult, ALU.add, True, C["all_next"][:, :], 0.0)


def spread_weights(nc, T, C, h, block, w, w_tile, s_w, names):
    rows_t, pt, s_wd, s_wr, s_pt = names
    low = ET - P

    def load(sp):
        sp.wait_ge(s_w, 1)
        sp.dma_start(T["w_edges"][0:h, :].rearrange("h (p c) -> p h c", p=P), w[:, :, :]).then_inc(s_wd, 16)
        sp.wait_ge(s_wd, 16)
        view = T["w_edges"][0:h, :].rearrange("h (i e) -> i h e", e=P)
        sp.dma_start(rows_t[:, 0, :, :], view[0:P]).then_inc(s_wr, 16)
        sp.dma_start(rows_t[0:low, 1, :, :], view[P:ET]).then_inc(s_wr, 16)

    def turn(pe):
        pe.wait_ge(s_wr, 32)
        for k in range(h):
            pe.transpose(pt[:, k, 0:P], rows_t[:, 0, k, :], C["ident"][:, :])
            i = pe.transpose(pt[:, k, P:ET], rows_t[0:low, 1, k, :], C["ident"][0:low, 0:low])
        i.then_inc(s_pt, 1)

    def land(v):
        v.wait_ge(s_pt, 1)
        return v.tensor_copy(w_tile[:, :, :].rearrange("p i h -> p h i"), pt[:, 0:h, 0:ET])

    return load, turn, land


def weight_buffers(c, nc, name, h):
    return (sb(c, nc, name + "_rows", [P, 2, h, P]), ps(c, nc, name + "_pt", [P, h, 256]),
            sem(c, nc, name + "_s_wd"), sem(c, nc, name + "_s_wr"), sem(c, nc, name + "_s_pt"))


def mean_weights(nc, T, C, w_tile):
    with Stage(nc) as c:
        ones_e = sb(c, nc, "m_ones", [P, 1, ET])
        seg = Segments(c, nc, T, C, "m_seg", 1)
        names = weight_buffers(c, nc, "m", 1)
        s_step = sem(c, nc, "m_step")
        s_w = sem(c, nc, "m_s_w")
        tick = sem(c, nc, "m_tick")
        block = c.enter_context(nc.Block())
        load, turn, land = spread_weights(nc, T, C, 1, block, ones_e, w_tile, s_w, names)

        @block.sync
        def _(sp):
            seg.carry(sp, 2)
            load(sp)

        @block.tensor
        def _(pe):
            turn(pe)

        @block.vector
        def _(v):
            step = Steps(v, s_step)
            step.then(v.memset(ones_e[:, :, :], 1.0))
            seg.total(v, step, ones_e, False)
            v.reciprocal(ones_e[:, :, :], seg.g[:, :, :]).then_inc(s_w, 1)
            step.then(land(v))


def edge_softmax(nc, T, C, name, table, h, w_tile):
    with Stage(nc) as c:
        ig = sb(c, nc, name + "_ig", [P, EU, 2], I32)
        gs = sb(c, nc, name + "_gs", [P, EU, 2 * h])
        gd = sb(c, nc, name + "_gd", [P, EU, 2 * h])
        e = sb(c, nc, name + "_e", [P, h, ET])
        w = sb(c, nc, name + "_w", [P, h, ET])
        seg = Segments(c, nc, T, C, name + "_seg", h)
        names = weight_buffers(c, nc, name, h)
        g_in = [sem(c, nc, f"{name}_g_in{k}") for k in range(EU)]
        s_ig = sem(c, nc, name + "_s_ig")
        e_free = sem(c, nc, name + "_e_free")
        s_go = sem(c, nc, name + "_s_go")
        s_step = sem(c, nc, name + "_step")
        s_arg = sem(c, nc, name + "_s_arg")
        s_exp = sem(c, nc, name + "_s_exp")
        s_w = sem(c, nc, name + "_s_w")
        tick = sem(c, nc, name + "_tick")
        block = c.enter_context(nc.Block())
        load, turn, land = spread_weights(nc, T, C, h, block, w, w_tile, s_w, names)

        @block.sync
        def _(sp):
            seg.carry(sp, 4)
            load(sp)

        @block.tensor
        def _(pe):
            turn(pe)

        @block.gpsimd
        def _(pool):
            with pool.Fori(0, ET // EU) as t:
                for k in range(EU):
                    wait_all(pool, tick, (s_ig, t * EU + k + 1), (e_free, t * EU + k + 1))
                    for n, buf in ((0, gs), (1, gd)):
                        pool.indirect_dma_start(buf[:, k, :], None, table, bass.IndirectOffsetOnAxis(ap=ig[:, k, n:n + 1], axis=0),
                                                bounds_check=NP - 1, oob_is_err=False).then_inc(g_in[k], 16)

        @block.scalar
        def _(act):
            act.sem_inc(s_go, 1)
            with act.Fori(0, ET // EU) as t:
                for k in range(EU):
                    act.wait_ge(g_in[k], t * 32)
                    act.copy(ig[:, k, :], C["lane_i"][:, bass.ds(t * EU + k, 1), :].rearrange("p o n -> p (o n)")).then_inc(s_ig, 1)
            act.wait_ge(s_arg, 1)
            act.activation(w[:, :, :], w[:, :, :], ACT.Exp).then_inc(s_exp, 1)

        @block.vector
        def _(v):
            v.sem_inc(e_free, EU)
            with v.Fori(0, ET // EU) as t:
                for k in range(EU):
                    v.wait_ge(g_in[k], t * 32 + 32)
                    v.tensor_tensor(e[:, :, bass.ds(t * EU + k, 1)].rearrange("p h o -> p (h o)"), gs[:, k, 0:h],
                                    gd[:, k, h:2 * h], ALU.add).then_inc(e_free, 1)
            v.wait_ge(e_free, ET + EU)
            step = Steps(v, s_step)
            step.then(v.scalar_tensor_tensor(e[:, :, :], e[:, :, :], 0.2, e[:, :, :], ALU.mult, ALU.max))
            seg.total(v, step, e, True)
            v.tensor_tensor(w[:, :, :], e[:, :, :], seg.g[:, :, :], ALU.subtract).then_inc(s_arg, 1)
            v.wait_ge(s_exp, 1)
            seg.total(v, step, w, False)
            step.then(v.tensor_scalar(seg.g[:, :, :], seg.g[:, :, :], 1e-16, None, ALU.add))
            step.then(v.reciprocal(seg.g[:, :, :], seg.g[:, :, :]))
            v.tensor_tensor(w[:, :, :], w[:, :, :], seg.g[:, :, :], ALU.mult).then_inc(s_w, 1)
            step.then(land(v))


def aggregate(nc, T, C, name, table, h, w_tile):
    AHEAD = 3
    with Stage(nc) as c:
        keys = sb(c, nc, name + "_keys", [P, EU, P], I32)
        ig = sb(c, nc, name + "_ig", [P, EU], I32)
        io = sb(c, nc, name + "_io", [P, EU], I32)
        msg = sb(c, nc, name + "_msg", [P, EU, D])
        m = sb(c, nc, name + "_m", [P, EU, P])
        cm = sb(c, nc, name + "_cm", [P, EU, P])
        res = sb(c, nc, name + "_res", [P, EU, D])
        pa = [ps(c, nc, f"{name}_pa{k}", [P, 512]) for k in range(EU)]
        k_in = [sem(c, nc, f"{name}_k_in{k}") for k in range(EU)]
        g_in = [sem(c, nc, f"{name}_g_in{k}") for k in range(EU)]
        r_out = [sem(c, nc, f"{name}_r_out{k}") for k in range(EU)]
        s_ig = sem(c, nc, name + "_s_ig")
        s_io = sem(c, nc, name + "_s_io")
        s_m = sem(c, nc, name + "_s_m")
        s_sum = sem(c, nc, name + "_s_sum")
        s_res = sem(c, nc, name + "_s_res")
        s_zero = sem(c, nc, name + "_s_zero")
        tick = sem(c, nc, name + "_tick")
        block = c.enter_context(nc.Block())
        turns = ET // EU

        @block.sync
        def _(sp):
            sp.wait_ge(s_zero, 1)
            with sp.Fori(0, turns) as t:
                for k in range(EU):
                    sp.wait_ge(s_m, t * EU + k + 1)
                    sp.dma_start(keys[:, k, :], T["keys"][bass.ds((t * EU + k) * P, P)].partition_broadcast(P))\
                        .then_inc(k_in[k], 16)

        @block.gpsimd
        def _(pool):
            def gather(k, i):
                wait_all(pool, tick, (s_ig, i + 1), (s_sum, i + 1))
                pool.indirect_dma_start(msg[:, k, :], None, table, bass.IndirectOffsetOnAxis(ap=ig[:, k:k + 1], axis=0),
                                        bounds_check=NP - 1, oob_is_err=False).then_inc(g_in[k], 16)

            for i in range(AHEAD):
                gather(i, i)
            with pool.Fori(0, turns) as t:
                for k in range(EU):
                    gather((k + AHEAD) % EU, t * EU + k + AHEAD)
                    wait_all(pool, tick, (s_res, t * EU + k + 1))
                    pool.indirect_dma_start(T["agg"], bass.IndirectOffsetOnAxis(ap=io[:, k:k + 1], axis=0), res[:, k, :], None,
                                            bounds_check=NP - 1, oob_is_err=False).then_inc(r_out[k], 16)
            for k in range(EU):
                pool.wait_ge(r_out[k], 16 * turns)
                pool.wait_ge(g_in[k], 16 * (turns + (k < AHEAD)))

        @block.scalar
        def _(act):
            def sources(k, i, uses):
                act.wait_ge(g_in[k], uses)
                act.copy(ig[:, k:k + 1], C["src_i"][:, bass.ds(i, 1)]).then_inc(s_ig, 1)

            for i in range(AHEAD):
                sources(i, i, 0)
            with act.Fori(0, turns) as t:
                for k in range(EU):
                    sources((k + AHEAD) % EU, t * EU + k + AHEAD, (t + (k + AHEAD) // EU) * 16)
                    act.wait_ge(r_out[k], t * 16)
                    act.copy(io[:, k:k + 1], C["out_i"][:, bass.ds(t * EU + k, 1)])
                    act.wait_ge(s_sum, t * EU + k + 1 + EU)
                    act.copy(res[:, k, :], pa[k][:, 0:D]).then_inc(s_res, 1)

        @block.tensor
        def _(pe):
            pe.wait_ge(s_zero, 1)
            pe.sem_inc(s_sum, EU)
            with pe.Fori(0, turns) as t:
                for k in range(EU):
                    i = t * EU + k
                    pe.wait_ge(g_in[k], t * 16 + 16)
                    pe.wait_ge(s_m, i + 1 + EU)
                    pe.matmul(pa[k][:, 0:D], m[:, k, :], msg[:, k, :], start=True, stop=False)
                    pe.wait_ge(s_res, i)
                    pe.matmul(pa[k][:, 0:D], cm[:, k, :], res[:, (k - 1) % EU, :], start=False, stop=True).then_inc(s_sum, 1)

        @block.vector
        def _(v):
            v.memset(res[:, EU - 1, :], 0.0).then_inc(s_zero, 1)
            v.sem_inc(s_m, EU)
            with v.Fori(0, turns) as t:
                for k in range(EU):
                    i = t * EU + k
                    v.wait_ge(k_in[k], t * 16 + 16)
                    v.wait_ge(s_sum, i + 1)
                    if h == 1:
                        v.tensor_scalar(m[:, k, :], keys[:, k, :], C["dst_f"][:, bass.ds(i, 1)],
                                        w_tile[:, bass.ds(i, 1), :].rearrange("p o h -> p (o h)"), ALU.is_equal, ALU.mult)
                    else:
                        v.tensor_scalar(m[:, k, :], keys[:, k, :], C["dst_f"][:, bass.ds(i, 1)], None, ALU.is_equal)
                        v.wait_ge(g_in[k], t * 16 + 16)
                        rows_k = msg[:, k, :].rearrange("p (h f) -> p h f", h=h)
                        v.tensor_tensor(rows_k, rows_k, w_tile[:, bass.ds(i, 1), :].rearrange("p o h -> p (o h)")
                                        .unsqueeze(2).to_broadcast([P, h, D // h]), ALU.mult)
                    v.tensor_scalar(cm[:, k, :], keys[:, k, :], C["carry_f"][:, bass.ds(i, 1)], None, ALU.is_equal)\
                        .then_inc(s_m, 1)


def piped(eng, first, second):
    first(0, 0, 0)
    with eng.Fori(0, G // 2 - 1) as u:
        first(u * 2 + 1, 1, u)
        second(u * 2, 0, u, P)
        first(u * 2 + 2, 0, u + 1)
        second(u * 2 + 1, 1, u, P)
    first(G - 1, 1, G // 2 - 1)
    second(G - 2, 0, G // 2 - 1, P)
    second(G - 1, 1, G // 2 - 1, LAST_P)


def ahead(eng, start, body, begun=None):
    start(0, 0, 0)
    start(1, 1, 0)
    if begun is not None:
        begun()
    with eng.Fori(0, G // 2 - 1) as u:
        for b in range(2):
            start(u * 2 + b + 2, b, u + 1)
            body(u * 2 + b, b, u, P)
    for b in range(2):
        body(G - 2 + b, b, G // 2 - 1, (P, LAST_P)[b])


def staggered(update, middle, finish, eng):
    update(0, 0, 0)
    update(1, 1, 0)
    middle(0, 0)
    with eng.Fori(0, G // 2 - 1) as u:
        for b in range(2):
            g = u * 2 + b
            update(g + 2, b, u + 1, g)
            middle(g + 1, 1 - b)
    finish(G - 2)
    middle(G - 1, 1)
    finish(G - 1)


def cols(tile, g):
    return tile[:, bass.ds(g * J, J)]


def update_and_gate(nc, T, C):
    with Stage(nc) as c:
        x_t = sb(c, nc, "b_x", [P, 2, J, D])
        xn_t = sb(c, nc, "b_xn", [P, 2, J, D])
        ag_t = sb(c, nc, "b_ag", [P, 2, J, D])
        x1_t = sb(c, nc, "b_x1", [P, 2, J, D])
        xl_t = sb(c, nc, "b_xl", [P, 2, J, D])
        tr_t = sb(c, nc, "b_tr", [P, 2, 4, P])
        lt_t = sb(c, nc, "b_lt", [P, 2, 4, P])
        gate = sb(c, nc, "b_gate", [P, KC, EXPERTS])
        gb = sb(c, nc, "b_gb", [P, EXPERTS])
        br = sb(c, nc, "b_br", [P, D])
        ev = sb(c, nc, "b_ev", [P, 2, EXPERTS])
        stats = sb(c, nc, "b_stats", [P, J, 6])
        mv = sb(c, nc, "b_mv", [P, J, 2])
        ve = sb(c, nc, "b_ve", [P, J])
        nt = sb(c, nc, "b_nt", [P, J])
        rs = sb(c, nc, "b_rs", [P, J])
        lg = sb(c, nc, "b_lg", [P, J, EXPERTS])
        rk = sb(c, nc, "b_rk", [P, J, EXPERTS])
        oh = sb(c, nc, "b_oh", [P, J, EXPERTS])
        cum = sb(c, nc, "b_cum", [P, J + 1, EXPERTS])
        run = sb(c, nc, "b_run", [P, EXPERTS])
        m4 = sb(c, nc, "b_m4", [P, 5, J])
        io = sb(c, nc, "b_io", [P, 2, J], I32)
        pt = [ps(c, nc, f"b_pt{n}", [P, 4, P]) for n in range(2)]
        px = [ps(c, nc, f"b_px{b}", [P, J, D]) for b in range(2)]
        pl = ps(c, nc, "b_pl", [P, 4, P])
        pg = ps(c, nc, "b_pg", [P, 512])
        pgate = pg[:, 0:J * EXPERTS].rearrange("p (j e) -> p j e", e=EXPERTS)
        ppre = pg[:, 64:64 + EXPERTS]
        ins = [sem(c, nc, f"b_ins{b}") for b in range(2)]
        outs = [sem(c, nc, f"b_outs{b}") for b in range(2)]
        sent = [sem(c, nc, f"b_sent{b}") for b in range(2)]
        s_par = sem(c, nc, "b_par")
        s_pt = sem(c, nc, "b_s_pt")
        s_tr = sem(c, nc, "b_s_tr")
        s_mm = sem(c, nc, "b_s_mm")
        s_px = sem(c, nc, "b_s_px")
        s_x1 = sem(c, nc, "b_s_x1")
        s_xl = sem(c, nc, "b_s_xl")
        s_pl = sem(c, nc, "b_s_pl")
        s_lt = sem(c, nc, "b_s_lt")
        s_gate = sem(c, nc, "b_s_gate")
        s_tot = sem(c, nc, "b_s_tot")
        s_pre = sem(c, nc, "b_s_pre")
        s_io = sem(c, nc, "b_s_io")
        s_init = sem(c, nc, "b_s_init")
        st1 = sem(c, nc, "b_step1")
        st2 = sem(c, nc, "b_step2")
        st3 = sem(c, nc, "b_step3")
        tick = sem(c, nc, "b_tick")
        block = c.enter_context(nc.Block())

        @block.sync
        def _(sp):
            sp.dma_start(gate[:, :, :], T["gate_w"].rearrange("(c p) e -> p c e", p=P)).then_inc(s_par, 16)
            sp.dma_start(gb[:, :], T["gate_b"].partition_broadcast(P)).then_inc(s_par, 16)
            sp.dma_start(br[:, :], T["b_r"].partition_broadcast(P)).then_inc(s_par, 16)
            sp.dma_start(ev[:, :, :], T["c_experts"]).then_inc(s_par, 16)

            def load(g, b, u):
                sp.wait_ge(s_x1, g + 1)
                for t, name in ((x_t, "x"), (xn_t, "xn"), (ag_t, "agg")):
                    sp.dma_start(t[:, b], rows(T[name], g)).then_inc(ins[b], 16)

            def store(g, b, u, used):
                sp.wait_ge(s_x1, g + 3)
                sp.dma_start(rows(T["x1"], g), x1_t[:, b]).then_inc(outs[b], 16)

            ahead(sp, load, store)
            for b in range(2):
                sp.wait_ge(outs[b], 16 * (G // 2))

        @block.gpsimd
        def _(pool):
            def second(g, b, u, used):
                wait_all(pool, tick, (s_io, g + 1))
                for j in range(J):
                    pool.indirect_dma_start(T["slots"], bass.IndirectOffsetOnAxis(ap=io[:, b, j:j + 1], axis=0),
                                            xl_t[:, b, j, :], None, bounds_check=EXPERTS * MROWS - 1,
                                            oob_is_err=False).then_inc(sent[b], 16)

            piped(pool, lambda *a: None, second)
            for b in range(2):
                pool.wait_ge(sent[b], 16 * J * (G // 2))

        @block.tensor
        def _(pe):
            pe.wait_ge(s_par, 64)
            pe.sem_inc(s_mm, 2)

            def update(g, b, u, counted=None):
                pe.wait_ge(ins[b], u * 48 + 48)
                pe.wait_ge(s_x1, g + 1)
                for j in range(J + 1):
                    if j < J:
                        pe.wait_ge(s_tr, g * J + j + 1)
                        for k in range(4):
                            src = (xn_t, ag_t)[k // 2]
                            i = pe.transpose(pt[j % 2][:, k, :], src[:, b, j, (k % 2) * P:(k % 2 + 1) * P],
                                             C["ident"][:, :])
                        i.then_inc(s_pt, 1)
                    if j > 0:
                        pe.wait_ge(s_tr, g * J + j + 2)
                        for k in range(4):
                            w = (C["wr"], C["wl"])[k // 2]
                            i = pe.matmul(px[b][:, j - 1, :], tr_t[:, (j - 1) % 2, k, :], w[:, k % 2, :],
                                          start=(k == 0), stop=(k == 3))
                        i.then_inc(s_mm, 1)
                    if j == 2 and counted is not None:
                        before(counted)

            def before(g):
                pe.wait_ge(s_tot, g + 1)
                pe.matmul(ppre, C["tri"][:, :], cum[:, J, :], start=True, stop=False)
                pe.matmul(ppre, C["ones"][:, :], run[:, :], start=False, stop=True).then_inc(s_pre, 1)

            def logits(g, b):
                pe.wait_ge(s_xl, g + 1)
                pe.wait_ge(s_io, g)
                for h in range(2):
                    pe.wait_ge(s_lt, g * 2 + h + 1)
                    for k in range(4):
                        i = pe.transpose(pl[:, k, :], xl_t[:, b, 2 * h + k // 2, (k % 2) * P:(k % 2 + 1) * P],
                                         C["ident"][:, :])
                    i.then_inc(s_pl, 1)
                    pe.wait_ge(s_lt, g * 2 + h + 2)
                    for k in range(4):
                        i = pe.matmul(pgate[:, 2 * h + k // 2, :], lt_t[:, h, k, :], gate[:, k % 2, :],
                                      start=(k % 2 == 0), stop=(k % 2 == 1))
                i.then_inc(s_gate, 1)

            staggered(update, logits, lambda g: before(g), pe)

        @block.scalar
        def _(act):
            act.sem_inc(s_tr, 2)
            act.sem_inc(s_lt, 1)

            def update(g, b, u, counted=None):
                for j in range(J):
                    act.wait_ge(s_pt, g * J + j + 1)
                    act.wait_ge(s_mm, g * J + j + 1)
                    act.copy(tr_t[:, j % 2], pt[j % 2][:, :, :]).then_inc(s_tr, 1)

            def logits(g, b):
                for h in range(2):
                    act.wait_ge(s_pl, g * 2 + h + 1)
                    act.copy(lt_t[:, h], pl[:, :, :]).then_inc(s_lt, 1)

            staggered(update, logits, lambda g: None, act)

        @block.vector
        def _(v):
            step = Steps(v, s_init)
            step.then(v.memset(cum[:, :, :], 0.0))
            step.then(v.memset(run[:, :], 0.0))
            v.wait_ge(s_par, 64)
            v.sem_inc(s_x1, 2)

            def update(g, b, u, counted=None):
                if counted is not None:
                    places(counted, b)
                step = Steps(v, st1, g, 4 + 10)
                x1, xl = x1_t[:, b], xl_t[:, b]
                v.wait_ge(s_mm, g * J + J + 2)
                v.wait_ge(outs[b], u * 16)
                step.then(v.tensor_tensor(x1, px[b][:, :, :], x_t[:, b], ALU.add))
                v.tensor_tensor(x1, x1, br[:, :].unsqueeze(1).to_broadcast([P, J, D]), ALU.add).then_inc(s_x1, 1)
                v.wait_ge(s_x1, g + 3)
                step.then(row_mean_var(v, step, tick, x1, stats, mv, ve[:, :]))
                inverse_root(v, step, rs, ve, nt)
                v.wait_ge(sent[b], u * 16 * J)
                for j in range(J):
                    i = v.tensor_scalar(xl[:, j, :], x1[:, j, :], mv[:, j, 0:1], rs[:, j:j + 1],
                                        ALU.subtract, ALU.mult)
                i.then_inc(s_xl, 1)
                step.end()

            wide = [P, J, EXPERTS]
            pos, base, kept, slot, far = (m4[:, n, :] for n in range(5))

            def choose(g, b):
                step = Steps(v, st2, g, 10)
                v.wait_ge(s_gate, g + 1)
                step.then(v.tensor_tensor(lg[:, :, :], pgate, gb[:, :].unsqueeze(1).to_broadcast(wide), ALU.add))
                step.then(v.tensor_reduce(pos, lg[:, :, :], AX.X, ALU.max))
                step.then(v.tensor_tensor(lg[:, :, :], lg[:, :, :], pos.unsqueeze(2).to_broadcast(wide), ALU.subtract))
                v.tensor_copy(C["gap"][:, bass.ds(g * J, J), :], lg[:, :, :])
                step.then(v.scalar_tensor_tensor(rk[:, :, :], lg[:, :, :], 0.0, ev[:, 0, :].unsqueeze(1).to_broadcast(wide),
                                                 ALU.is_equal, ALU.mult))
                step.then(v.tensor_reduce(base, rk[:, :, :], AX.X, ALU.max))
                step.then(v.tensor_tensor(oh[:, :, :], rk[:, :, :], base.unsqueeze(2).to_broadcast(wide), ALU.is_equal))
                step.then(v.tensor_scalar(oh[:, :, :], oh[:, :, :], C["valid"][:, bass.ds(g, 1)], None, ALU.mult))
                for j in range(J - 1):
                    step.then(v.tensor_tensor(cum[:, j + 1, :], cum[:, j, :], oh[:, j, :], ALU.add))
                v.tensor_tensor(cum[:, J, :], cum[:, J - 1, :], oh[:, J - 1, :], ALU.add).then_inc(s_tot, 1)
                step.end()

            def places(g, b):
                step = Steps(v, st3, g, 6)
                v.wait_ge(s_pre, g + 1)
                v.tensor_tensor(run[:, :], run[:, :], cum[:, J, :], ALU.add)
                step.then(v.tensor_tensor(rk[:, :, :], cum[:, 0:J, :], ppre.unsqueeze(1).to_broadcast(wide), ALU.add))
                step.then(v.tensor_tensor(rk[:, :, :], rk[:, :, :], oh[:, :, :], ALU.mult))
                v.tensor_reduce(pos, rk[:, :, :], AX.X, ALU.add)
                step.then(v.tensor_tensor(lg[:, :, :], oh[:, :, :], ev[:, 1, :].unsqueeze(1).to_broadcast(wide), ALU.mult))
                step.then(v.tensor_reduce(base, lg[:, :, :], AX.X, ALU.add))
                step.then(v.tensor_scalar(kept, pos, float(CAP), C["valid"][:, bass.ds(g, 1)], ALU.is_lt, ALU.mult))
                v.tensor_tensor(slot, pos, base, ALU.add)
                v.tensor_copy(cols(C["kept"], g), kept)
                step.then(v.tensor_scalar(far, kept, -FAR, FAR, ALU.mult, ALU.add))
                v.tensor_tensor(cols(C["from"], g), slot, kept, ALU.mult)
                v.tensor_tensor(io[:, b, :], slot, far, ALU.add).then_inc(s_io, 1)
                step.end()

            staggered(update, choose, lambda g: places(g, g % 2), v)


def two_layers(nc, T, C, name, experts, pairs, tail_block, r, width, source, w1_d, b1_d, w2_d, b2_d, func, store, out_d):
    n_blocks = 2 * pairs + tail_block
    total = experts * n_blocks
    assert total % 2 == 0
    slots_w = min(experts, 2)
    FC = FF // P
    with Stage(nc) as c:
        xe = sb(c, nc, name + "_xe", [r, 2, J, width])
        w1 = sb(c, nc, name + "_w1", [P, slots_w, KC, FF])
        w2 = sb(c, nc, name + "_w2", [P, slots_w, FC, D])
        b1 = sb(c, nc, name + "_b1", [P, slots_w, FC])
        b2 = sb(c, nc, name + "_b2", [P, slots_w, D])
        xt = sb(c, nc, name + "_xt", [P, KC, J * r])
        ht = sb(c, nc, name + "_ht", [P, FC, J * r])
        yt = sb(c, nc, name + "_yt", [r, 2, J, D])
        io = sb(c, nc, name + "_io", [r, 2, J], I32)
        pxt = ps(c, nc, name + "_pxt", [P, KC, 512])
        ph = [ps(c, nc, f"{name}_ph{n}", [P, 512]) for n in range(2)]
        py = [ps(c, nc, f"{name}_py{b}", [P, J, D]) for b in range(2)]
        w_in = [sem(c, nc, f"{name}_w_in{n}") for n in range(slots_w)]
        x_in = [sem(c, nc, f"{name}_x_in{b}") for b in range(2)]
        y_out = [sem(c, nc, f"{name}_y_out{b}") for b in range(2)]
        s_pt = sem(c, nc, name + "_s_pt")
        s_xt = sem(c, nc, name + "_s_xt")
        s_h = sem(c, nc, name + "_s_h")
        s_ht = sem(c, nc, name + "_s_ht")
        s_y = sem(c, nc, name + "_s_y")
        s_yt = sem(c, nc, name + "_s_yt")
        s_go = sem(c, nc, name + "_s_go")
        s_step = sem(c, nc, name + "_step")
        tick = sem(c, nc, name + "_tick")
        block = c.enter_context(nc.Block())
        block_rows = J * r

        def blocks(eng, body):
            if experts == 1:
                with eng.Fori(0, pairs) as i:
                    for s in range(2):
                        body(i * 2 + s, s, i, 0, 0)
                return
            with eng.Fori(0, experts // 2) as ep:
                for par in range(2):
                    def at(i, s):
                        k = n_blocks * par + s
                        body(ep * (2 * n_blocks) + i * 2 + k, k % 2, ep * n_blocks + i + k // 2, par, ep)
                    with eng.Fori(0, pairs) as i:
                        for s in range(2):
                            at(i, s)
                    if tail_block:
                        at(pairs, 0)

        def source_rows(n):
            return source[bass.ds(n * block_rows, block_rows), :].rearrange("(p j) d -> p j d", j=J)

        def load_weights(eng, e, slot):
            for out, in_ in ((w1[:, slot], w1_d[e].rearrange("(c p) f -> p c f", p=P)),
                             (w2[:, slot], w2_d[e].rearrange("(c p) d -> p c d", p=P)),
                             (b1[:, slot], b1_d[e]), (b2[:, slot], b2_d[e].partition_broadcast(P))):
                eng.dma_start(out, in_).then_inc(w_in[slot], 16)

        @block.sync
        def _(sp):
            sp.dma_start(xe[:, 0], source_rows(0)).then_inc(x_in[0], 16)

            def body(n, b, u, slot, e):
                if store:
                    sp.wait_ge(s_pt, n)
                else:
                    sp.wait_ge(s_yt, n + 2)
                o = 1 - b
                sp.dma_start(xe[:, o], source_rows(n + 1)).then_inc(x_in[o], 16)
                if store:
                    sp.wait_ge(s_yt, n + 3)
                    sp.dma_start(out_d[bass.ds(n * block_rows, block_rows), :].rearrange("(p j) d -> p j d", j=J), yt[:, b])\
                        .then_inc(y_out[b], 16)

            blocks(sp, body)
            sp.wait_ge(x_in[0], 16 * (total // 2 + 1))
            if store:
                for b in range(2):
                    sp.wait_ge(y_out[b], 16 * (total // 2))

        @block.gpsimd
        def _(pool):
            for n in range(slots_w):
                load_weights(pool, n, n)
            if experts > 1:
                with pool.Fori(0, experts // 2 - 1) as ep:
                    for par in range(2):
                        done = ep * (2 * n_blocks) + n_blocks * (par + 1)
                        wait_all(pool, tick, (s_y, done), (s_yt, done + 2))
                        e = ep * 2 + par + 2
                        for out, in_ in ((w1[:, par], w1_d[bass.ds(e, 1)].rearrange("o (c p) f -> p (o c) f", p=P)),
                                         (w2[:, par], w2_d[bass.ds(e, 1)].rearrange("o (c p) d -> p (o c) d", p=P)),
                                         (b1[:, par], b1_d[bass.ds(e, 1)].rearrange("o p f -> p (o f)")),
                                         (b2[:, par], b2_d[bass.ds(e, 1)].rearrange("o d -> (o d)").partition_broadcast(P))):
                            pool.dma_start(out, in_).then_inc(w_in[par], 16)
            if not store:
                def body(n, b, u, slot, e):
                    wait_all(pool, tick, (s_yt, n + 3))
                    for j in range(J):
                        pool.indirect_dma_start(out_d, bass.IndirectOffsetOnAxis(ap=io[:, b, j:j + 1], axis=0), yt[:, b, j, :],
                                                None, bounds_check=NP - 1, oob_is_err=False).then_inc(y_out[b], 16)

                blocks(pool, body)
                for b in range(2):
                    pool.wait_ge(y_out[b], 16 * J * (total // 2))

        @block.tensor
        def _(pe):
            def turn(b):
                for k in range(KC):
                    for j in range(J):
                        i = pe.transpose(pxt[:, k, j * r:(j + 1) * r], xe[:, b, j, k * P:(k + 1) * P], C["ident"][0:r, 0:r])
                i.then_inc(s_pt, 1)

            pe.wait_ge(x_in[0], 16)
            turn(0)

            def body(n, b, u, slot, e):
                pe.wait_ge(s_xt, n + 1)
                pe.wait_ge(w_in[slot], e * 64 + 64 if experts > 1 else 64)
                for f in range(FC):
                    pe.wait_ge(s_ht, n * FC + f + 1)
                    for k in range(KC):
                        i = pe.matmul(ph[f % 2][:, 0:J * r], w1[:, slot, k, f * P:(f + 1) * P], xt[:, k, :],
                                      start=(k == 0), stop=(k == KC - 1))
                    i.then_inc(s_h, 1)
                pe.wait_ge(x_in[1 - b], (u + b) * 16 + 16)
                turn(1 - b)
                pe.wait_ge(s_yt, n + 1)
                for j in range(J):
                    for f in range(FC):
                        if j == 0:
                            pe.wait_ge(s_ht, n * FC + f + 3)
                        i = pe.matmul(py[b][0:r, j, :], ht[:, f, j * r:(j + 1) * r], w2[:, slot, f, :],
                                      start=(f == 0), stop=(f == FC - 1))
                i.then_inc(s_y, 1)

            blocks(pe, body)

        @block.scalar
        def _(act):
            act.sem_inc(s_ht, 2)
            act.sem_inc(s_go, 1)

            def body(n, b, u, slot, e):
                act.wait_ge(s_pt, n + 1)
                act.copy(xt[:, :, :], pxt[:, :, 0:J * r]).then_inc(s_xt, 1)
                for f in range(FC):
                    act.wait_ge(s_h, n * FC + f + 1)
                    if f == 0:
                        act.wait_ge(s_y, n)
                    act.activation(ht[:, f, :], ph[f % 2][:, 0:J * r], func, bias=b1[:, slot, f:f + 1]).then_inc(s_ht, 1)

            blocks(act, body)

        @block.vector
        def _(v):
            v.sem_inc(s_yt, 2)

            def body(n, b, u, slot, e):
                y = yt[:, b]
                v.wait_ge(s_y, n + 1)
                v.wait_ge(y_out[b], u * 16 * (1 if store else J))
                bias = b2[0:r, slot, :].unsqueeze(1).to_broadcast([r, J, D])
                if store:
                    v.tensor_tensor(y, py[b][0:r, :, :], bias, ALU.add).then_inc(s_yt, 1)
                else:
                    step = Steps(v, s_step, n, 1)
                    step.then(v.tensor_tensor(y, py[b][0:r, :, :], bias, ALU.add))
                    for j in range(J):
                        v.scalar_tensor_tensor(y[:, j, :], y[:, j, :], xe[:, b, j, 2 * D:2 * D + 1], xe[:, b, j, D:2 * D],
                                               ALU.mult, ALU.add)
                    v.tensor_copy(io[:, b, :], xe[:, b, :, 2 * D + 1].bitcast(I32)).then_inc(s_yt, 1)

            blocks(v, body)


def combine_and_project(nc, T, C):
    QK, SC = 2 * D, 2 * GH
    with Stage(nc) as c:
        x1_t = sb(c, nc, "d_x1", [P, 2, J, D])
        yg_t = sb(c, nc, "d_yg", [P, 2, J, D])
        xl_t = sb(c, nc, "d_xl", [P, 2, J, D])
        fin = sb(c, nc, "d_fin", [P, J, D], I32)
        sg = sb(c, nc, "d_sg", [P, J, D])
        neg = sb(c, nc, "d_neg", [P, J, D])
        io = sb(c, nc, "d_io", [P, 2, J], I32)
        tr_t = sb(c, nc, "d_tr", [P, 2, KC, P])
        wqk = sb(c, nc, "d_wqk", [P, KC, QK])
        wv = sb(c, nc, "d_wv", [P, KC, D])
        wh = sb(c, nc, "d_wh", [P, KC, D + SC])
        w1n = sb(c, nc, "d_w1n", [P, KC, D])
        aa = sb(c, nc, "d_aa", [P, KC, SC])
        bqk = sb(c, nc, "d_bqk", [P, QK])
        bv = sb(c, nc, "d_bv", [P, D])
        t_t = sb(c, nc, "d_t", [P, 2, QK])
        e_t = sb(c, nc, "d_e", [P, 2, QK])
        k_t = sb(c, nc, "d_k", [P, J, D])
        q_t = sb(c, nc, "d_q", [P, 2, J, D])
        v_t = sb(c, nc, "d_v", [P, J, KC, P + 1])
        hp_t = sb(c, nc, "d_hp", [P, 2, J, D])
        sc_t = sb(c, nc, "d_sc", [P, 2, J, SC])
        zero = sb(c, nc, "d_zero", [P, 512])
        gap = C["gap"]
        stats = sb(c, nc, "d_stats", [P, J, 6])
        mv = sb(c, nc, "d_mv", [P, J, 2])
        ve = sb(c, nc, "d_ve", [P, J])
        rs = sb(c, nc, "d_rs", [P, J])
        nt = sb(c, nc, "d_nt", [P, J])
        nb = sb(c, nc, "d_nb", [P, J])
        pt = ps(c, nc, "d_pt", [P, KC, P])
        pqk = [ps(c, nc, f"d_pqk{n}", [P, 512]) for n in range(2)]
        pv = [ps(c, nc, f"d_pv{n}", [P, 512]) for n in range(2)]
        php = [ps(c, nc, f"d_php{n}", [P, 512]) for n in range(2)]
        pkv = ps(c, nc, "d_pkv", [P, KC, 256])
        ins = [sem(c, nc, f"d_ins{b}") for b in range(2)]
        got = [sem(c, nc, f"d_got{b}") for b in range(2)]
        x2o = [sem(c, nc, f"d_x2o{b}") for b in range(2)]
        pro = [sem(c, nc, f"d_pro{b}") for b in range(2)]
        s_par = sem(c, nc, "d_par")
        s_init = sem(c, nc, "d_init")
        s_aw = sem(c, nc, "d_s_aw")
        s_wh = sem(c, nc, "d_s_wh")
        s_ex = sem(c, nc, "d_s_ex")
        s_wt = sem(c, nc, "d_s_wt")
        s_io = sem(c, nc, "d_s_io")
        s_z = sem(c, nc, "d_s_z")
        s_x2 = sem(c, nc, "d_s_x2")
        s_rs = sem(c, nc, "d_s_rs")
        s_xl = sem(c, nc, "d_s_xl")
        s_pt = sem(c, nc, "d_s_pt")
        s_tr = sem(c, nc, "d_s_tr")
        s_mm = sem(c, nc, "d_s_mm")
        s_qkb = sem(c, nc, "d_s_qkb")
        s_e = sem(c, nc, "d_s_e")
        s_ph = sem(c, nc, "d_s_ph")
        s_hp = sem(c, nc, "d_s_hp")
        s_kvd = sem(c, nc, "d_s_kvd")
        st1 = sem(c, nc, "d_step1")
        st2 = sem(c, nc, "d_step2")
        tick = sem(c, nc, "d_tick")
        block = c.enter_context(nc.Block())
        n_par = 8

        @block.sync
        def _(sp):
            for out, in_ in ((wqk[:, :, 0:D], T["wq"].rearrange("(c p) n -> p c n", p=P)),
                             (wqk[:, :, D:QK], T["wk"].rearrange("(c p) n -> p c n", p=P)),
                             (wv[:, :, :], T["wv"].rearrange("(c p) n -> p c n", p=P)),
                             (wh[:, :, 0:D], T["W1_t"].rearrange("(c p) n -> p c n", p=P)),
                             (w1n[:, :, :], T["W1"].rearrange("(c p) n -> p c n", p=P)),
                             (aa[:, :, :], T["a1"].rearrange("(c p) n -> p c n", p=P)),
                             (bqk[:, :], T["b_qk"].partition_broadcast(P)),
                             (bv[:, :], T["bv"].partition_broadcast(P))):
                sp.dma_start(out, in_).then_inc(s_par, 16)

            def load(g, b, u):
                wait_all(sp, tick, (x2o[b], u * 16))
                sp.wait_ge(s_xl, g + 1)
                sp.dma_start(x1_t[:, b], rows(T["x1"], g)).then_inc(ins[b], 16)

            def store_x2(g, b):
                sp.wait_ge(s_x2, g + 3)
                sp.dma_start(rows(T["x2"], g), x1_t[:, b]).then_inc(x2o[b], 16)

            def store(g, b, u, used):
                if used == P:
                    store_x2(g + 1, 1 - b)
                sp.wait_ge(s_ph, g * J + J + 2)
                sp.dma_start(rows(T["pq"], g), q_t[:, b]).then_inc(pro[b], 16)
                sp.wait_ge(s_hp, g * J + J + 2)
                sp.dma_start(rows(T["hp"], g), hp_t[:, b]).then_inc(pro[b], 16)
                sp.dma_start(rows(T["sc1"], g), sc_t[:, b]).then_inc(pro[b], 16)

            ahead(sp, load, store, lambda: store_x2(0, 0))
            for b in range(2):
                sp.wait_ge(x2o[b], 16 * (G // 2))
                sp.wait_ge(pro[b], 48 * (G // 2))

        @block.gpsimd
        def _(pool):
            def gather(g, b, u):
                wait_all(pool, tick, (s_io, g + 1), (s_x2, g + 1))
                for j in range(J):
                    pool.indirect_dma_start(yg_t[:, b, j, :], None, T["y"], bass.IndirectOffsetOnAxis(ap=io[:, b, j:j + 1], axis=0),
                                            bounds_check=EXPERTS * MROWS - 1, oob_is_err=False).then_inc(got[b], 16)

            ahead(pool, gather, lambda *a: None)

        @block.tensor
        def _(pe):
            pe.wait_ge(s_par, 16 * n_par)
            for k in range(KC):
                for n in range(KC):
                    i = pe.matmul(php[k][:, 0:SC], w1n[:, n, k * P:(k + 1) * P], aa[:, n, :], start=(n == 0), stop=(n == KC - 1))
            i.then_inc(s_aw, 1)
            pe.wait_ge(s_wh, 1)
            pe.matmul(pkv[:, :, :], zero[:, 0:P], zero[:, :], start=True, stop=False, skip_group_check=True)
            pe.sem_inc(s_mm, 2)

            def turn(i, g, b, j):
                if j == 0:
                    pe.wait_ge(s_xl, g + 3)
                pe.wait_ge(s_tr, i + 1)
                for k in range(KC):
                    o = pe.transpose(pt[:, k, :], xl_t[:, b, j, k * P:(k + 1) * P], C["ident"][:, :])
                o.then_inc(s_pt, 1)

            def sums(i, j, used):
                pe.wait_ge(s_ph, i + 3)
                for k in range(KC):
                    o = pe.matmul(pkv[:, k, 0:P + 1], k_t[0:used, j, k * P:(k + 1) * P], v_t[0:used, j, k, :], start=False,
                                  stop=False, skip_group_check=True)

            turn(0, 0, 0, 0)

            def second(g, b, u, used):
                for j in range(J):
                    i, s = g * J + j, j % 2
                    if j < J - 1:
                        turn(i + 1, g, b, j + 1)
                    pe.wait_ge(s_tr, i + 2)
                    pe.wait_ge(s_qkb, i + 1)
                    pe.wait_ge(s_hp, i + 1)
                    for out, w, n in ((pv[s], wv, D), (pqk[s], wqk, QK), (php[s], wh, D + SC)):
                        for k in range(KC):
                            o = pe.matmul(out[:, 0:n], tr_t[:, s, k, :], w[:, k, :], start=(k == 0), stop=(k == KC - 1))
                    o.then_inc(s_mm, 1)
                    sums(i - 2, (j - 2) % J, used if j > 1 else P)
                    if j == J - 1 and used == P:
                        turn(i + 1, g + 1, 1 - b, 0)
                if used < P:
                    for j in range(J - 2, J):
                        sums(g * J + j, j, used)

            piped(pe, lambda *a: None, second)
            pe.matmul(pkv[:, :, :], zero[:, 0:P], zero[:, :], start=False, stop=True, skip_group_check=True).then_inc(s_kvd, 1)

        @block.scalar
        def _(act):
            act.activation(gap[:, :, :], gap[:, :, :], ACT.Exp).then_inc(s_ex, 1)
            act.sem_inc(s_tr, 1)
            act.sem_inc(s_hp, 2)
            act.sem_inc(s_xl, 2)

            def first(g, b, u):
                act.wait_ge(got[b], u * 16 * J)
                act.copy(io[:, b, :], cols(C["from"], g)).then_inc(s_io, 1)

            def scale(g, b, u):
                act.wait_ge(got[b], u * 16 * J + 16 * J)
                for j in range(J):
                    o = act.mul(yg_t[:, b, j], yg_t[:, b, j], C["w"][:, bass.ds(g * J + j, 1)])
                o.then_inc(s_z, 1)

            def norm(g, b):
                act.wait_ge(s_rs, g + 1)
                for j in range(J):
                    o = act.activation(xl_t[:, b, j], x1_t[:, b, j], ACT.Identity, bias=nb[:, j:j + 1], scale=rs[:, j:j + 1])
                o.then_inc(s_xl, 1)

            def turned(i, s):
                act.wait_ge(s_pt, i + 1)
                act.wait_ge(s_mm, i + 1)
                act.copy(tr_t[:, s], pt[:, :, :]).then_inc(s_tr, 1)

            def begin():
                act.wait_ge(s_wt, 1)
                scale(0, 0, 0)
                norm(0, 0)
                turned(0, 0)

            def second(g, b, u, used):
                if used == P:
                    scale(g + 1, 1 - b, u + b)
                act.wait_ge(pro[b], u * 48)
                for j in range(J):
                    i, s = g * J + j, j % 2
                    if j < J - 1:
                        turned(i + 1, 1 - s)
                    act.wait_ge(s_mm, i + 3)
                    act.copy(hp_t[:, b, j], php[s][:, 0:D])
                    act.copy(sc_t[:, b, j], php[s][:, D:D + SC]).then_inc(s_hp, 1)
                    if j == J - 1 and used == P:
                        turned(i + 1, 1 - s)
                    act.wait_ge(s_qkb, i + 3)
                    act.activation(e_t[:, s], t_t[:, s], ACT.Exp)
                    act.activation(t_t[:, s], t_t[:, s], ACT.Relu).then_inc(s_e, 1)
                    if j == J - 2 and used == P:
                        norm(g + 1, 1 - b)

            ahead(act, first, second, begin)

        @block.vector
        def _(v):
            step = Steps(v, s_init)
            step.then(v.memset(zero[:, :], 0.0))
            step.then(v.memset(k_t[:, :, :], 0.0))
            step.then(v.memset(v_t[:, :, :, :], 0.0))
            step.then(v.memset(v_t[:, :, :, P:P + 1], 1.0))
            v.sem_inc(s_qkb, 2)
            v.wait_ge(s_aw, 1)
            for k in range(KC):
                i = v.tensor_copy(wh[:, k, D:D + SC], php[k][:, 0:SC])
            i.then_inc(s_wh, 1)
            v.wait_ge(s_ex, 1)
            step.then(v.tensor_reduce(C["w"][:, :], gap[:, :, :], AX.X, ALU.add))
            step.then(v.reciprocal(C["w"][:, :], C["w"][:, :]))
            v.tensor_tensor(C["w"][:, :], C["w"][:, :], C["kept"][:, :], ALU.mult).then_inc(s_wt, 1)
            v.sem_inc(s_x2, 2)
            v.sem_inc(s_ph, 2)

            def update(g, b, u):
                step = Steps(v, st1, g, 3)
                x, y = x1_t[:, b], yg_t[:, b]
                v.wait_ge(s_z, g + 1)
                v.tensor_scalar(neg[:, :, :], y, 0.0, -1.0e4, ALU.is_lt, ALU.mult)
                v.tensor_scalar(sg[:, :, :], y, 0.0, 1.0e4, ALU.is_gt, ALU.mult)
                step.then(v.tensor_scalar(fin[:, :, :], y, 0.0, 0.0, ALU.mult, ALU.is_equal))
                step.then(v.tensor_tensor(sg[:, :, :], sg[:, :, :], neg[:, :, :], ALU.add), tick)
                step.then(v.copy_predicated(sg[:, :, :], fin[:, :, :], y))
                v.wait_ge(ins[b], u * 16 + 16)
                v.tensor_tensor(x, x, sg[:, :, :], ALU.add).then_inc(s_x2, 1)
                step.end()

            def scales(g, b, u):
                step = Steps(v, st2, g, 2 + 1 + 1 + 9)
                v.wait_ge(s_x2, g + 3)
                v.wait_ge(s_xl, g + 2)
                step.then(row_mean_var(v, step, tick, x1_t[:, b], stats, mv, ve[:, :]))
                inverse_root(v, step, rs, ve, nt)
                v.scalar_tensor_tensor(nb[:, :], mv[:, :, 0], -1.0, rs[:, :], ALU.mult, ALU.mult).then_inc(s_rs, 1)
                step.end()

            def begin():
                update(0, 0, 0)
                scales(0, 0, 0)

            def second(g, b, u, used):
                v.wait_ge(pro[b], u * 48)
                def phi(i, j):
                    s = j % 2
                    v.wait_ge(s_e, i + 1)
                    v.scalar_tensor_tensor(q_t[:, b, j], e_t[:, s, 0:D], 1.0, t_t[:, s, 0:D], ALU.min, ALU.add)
                    v.scalar_tensor_tensor(k_t[:, j], e_t[:, s, D:QK], 1.0, t_t[:, s, D:QK], ALU.min, ALU.add).then_inc(s_ph, 1)

                for j in range(J):
                    i, s = g * J + j, j % 2
                    v.wait_ge(s_mm, i + 3)
                    v.tensor_tensor(v_t[:, j, :, 0:P], pv[s][:, 0:D].rearrange("p (c n) -> p c n", c=KC),
                                    bv[:, :].rearrange("p (c n) -> p c n", c=KC), ALU.add)
                    v.wait_ge(s_ph, i + 1)
                    v.tensor_tensor(t_t[:, s], pqk[s][:, :], bqk[:, :], ALU.add).then_inc(s_qkb, 1)
                    if j > 0:
                        phi(i - 1, j - 1)
                    if used == P and j < 2:
                        (update, scales)[j](g + 1, 1 - b, u + b)
                phi(g * J + J - 1, J - 1)

            ahead(v, lambda *a: None, second, begin)
            v.wait_ge(s_kvd, 1)
            step.then(v.tensor_copy(C["kv"][:, :, :], pkv[:, :, 0:P + 1]))


def second_features(nc, T, C):
    SC = 2
    with Stage(nc) as c:
        ag_t = sb(c, nc, "f_ag", [P, 2, J, D])
        tr_t = sb(c, nc, "f_tr", [P, 2, KC, P])
        wh = sb(c, nc, "f_wh", [P, KC, D + SC])
        wn = sb(c, nc, "f_wn", [P, KC, D])
        aa = sb(c, nc, "f_aa", [P, KC, SC])
        hp_t = sb(c, nc, "f_hp", [P, 2, J, D])
        sc_t = sb(c, nc, "f_sc", [P, 2, J, SC])
        pt = [ps(c, nc, f"f_pt{n}", [P, KC, P]) for n in range(2)]
        php = [ps(c, nc, f"f_php{n}", [P, 512]) for n in range(2)]
        ins = [sem(c, nc, f"f_ins{b}") for b in range(2)]
        outs = [sem(c, nc, f"f_outs{b}") for b in range(2)]
        s_par = sem(c, nc, "f_par")
        s_aw = sem(c, nc, "f_s_aw")
        s_wh = sem(c, nc, "f_s_wh")
        s_pt = sem(c, nc, "f_s_pt")
        s_tr = sem(c, nc, "f_s_tr")
        s_mm = sem(c, nc, "f_s_mm")
        s_hp = sem(c, nc, "f_s_hp")
        tick = sem(c, nc, "f_tick")
        block = c.enter_context(nc.Block())

        def groups(eng, body):
            with eng.Fori(0, G // 2) as u:
                for b in range(2):
                    body(u * 2 + b, b, u)

        @block.sync
        def _(sp):
            for out, in_ in ((wh[:, :, 0:D], T["W2_t"].rearrange("(c p) n -> p c n", p=P)),
                             (wn[:, :, :], T["W2"].rearrange("(c p) n -> p c n", p=P)),
                             (aa[:, :, :], T["a2"].rearrange("(c p) n -> p c n", p=P))):
                sp.dma_start(out, in_).then_inc(s_par, 16)

            def load(g, b, u):
                sp.wait_ge(s_hp, g * J + 1)
                sp.dma_start(ag_t[:, b], rows(T["agg"], g)).then_inc(ins[b], 16)

            def save(g, b, u):
                sp.wait_ge(s_hp, g * J + 3 * J)
                sp.dma_start(rows(T["hp"], g), hp_t[:, b]).then_inc(outs[b], 16)
                sp.dma_start(rows(T["sc2"], g), sc_t[:, b]).then_inc(outs[b], 16)

            load(0, 0, 0)
            load(1, 1, 0)
            with sp.Fori(0, G // 2 - 1) as u:
                for b in range(2):
                    save(u * 2 + b, b, u)
                    load(u * 2 + b + 2, b, u + 1)
            for b in range(2):
                save(G - 2 + b, b, G // 2 - 1)
            for b in range(2):
                sp.wait_ge(outs[b], 32 * (G // 2))

        @block.tensor
        def _(pe):
            pe.wait_ge(s_par, 48)
            for k in range(KC):
                for n in range(KC):
                    i = pe.matmul(php[k][:, 0:SC], wn[:, n, k * P:(k + 1) * P], aa[:, n, :], start=(n == 0), stop=(n == KC - 1))
            i.then_inc(s_aw, 1)
            pe.wait_ge(s_wh, 1)

            def body(g, b, u):
                pe.wait_ge(ins[b], u * 16 + 16)
                for j in range(J + 1):
                    i = g * J + j
                    if j < J:
                        pe.wait_ge(s_tr, i + 1)
                        for k in range(KC):
                            o = pe.transpose(pt[j % 2][:, k, :], ag_t[:, b, j, k * P:(k + 1) * P], C["ident"][:, :])
                        o.then_inc(s_pt, 1)
                    if j > 0:
                        s = (j - 1) % 2
                        pe.wait_ge(s_tr, i + 2)
                        pe.wait_ge(s_hp, i - 1 + 7)
                        for k in range(KC):
                            o = pe.matmul(php[s][:, 0:D + SC], tr_t[:, s, k, :], wh[:, k, :], start=(k == 0), stop=(k == KC - 1))
                        o.then_inc(s_mm, 1)

            groups(pe, body)

        @block.scalar
        def _(act):
            act.sem_inc(s_tr, 2)

            def body(g, b, u):
                for j in range(J):
                    i = g * J + j
                    act.wait_ge(s_pt, i + 1)
                    act.wait_ge(s_mm, i + 1)
                    act.activation(tr_t[:, j % 2], pt[j % 2][:, :, :], ACT.Relu).then_inc(s_tr, 1)

            groups(act, body)

        @block.vector
        def _(v):
            v.wait_ge(s_aw, 1)
            for k in range(KC):
                i = v.tensor_copy(wh[:, k, D:D + SC], php[k][:, 0:SC])
            i.then_inc(s_wh, 1)
            v.sem_inc(s_mm, 2)
            v.sem_inc(s_hp, 2 * J)

            def body(g, b, u):
                v.wait_ge(outs[b], u * 32)
                for j in range(J):
                    i = g * J + j
                    v.wait_ge(s_mm, i + 3)
                    v.tensor_copy(hp_t[:, b, j], php[j % 2][:, 0:D])
                    v.tensor_copy(sc_t[:, b, j], php[j % 2][:, D:D + SC]).then_inc(s_hp, 1)

            groups(v, body)


def second_update(nc, T, C):
    HW_ = P + HEADS // KC
    with Stage(nc) as c:
        x2_t = sb(c, nc, "g_x2", [P, 2, J, D])
        ag_t = sb(c, nc, "g_ag", [P, 2, J, D])
        q_t = sb(c, nc, "g_q", [P, 2, J, D])
        row_t = sb(c, nc, "g_row", [P, 2, J, SW])
        tr_t = sb(c, nc, "g_tr", [P, 2, KC, P])
        o_t = sb(c, nc, "g_o", [P, 2, D])
        ot_t = sb(c, nc, "g_ot", [P, 2, KC, P])
        rc = sb(c, nc, "g_rc", [P, 2, HEADS])
        wo = sb(c, nc, "g_wo", [P, KC, D])
        bo = sb(c, nc, "g_bo", [P, D])
        wr = sb(c, nc, "g_wr", [P, D])
        br = sb(c, nc, "g_br", [P, 1])
        kvh = sb(c, nc, "g_kvh", [P, KC, HW_])
        junk = sb(c, nc, "g_junk", [P, J, D])
        stats = sb(c, nc, "g_stats", [P, J, 6])
        mv = sb(c, nc, "g_mv", [P, J, 2])
        ve = sb(c, nc, "g_ve", [P, J])
        sd = sb(c, nc, "g_sd", [P, J])
        rs = sb(c, nc, "g_rs", [P, J])
        wt = sb(c, nc, "g_wt", [P, J])
        pt = [ps(c, nc, f"g_pt{n}", [P, KC, P]) for n in range(2)]
        pq = [ps(c, nc, f"g_pq{n}", [P, 512]) for n in range(2)]
        pot = ps(c, nc, "g_pot", [P, KC, P])
        po = ps(c, nc, "g_po", [P, J, D])
        ins = [sem(c, nc, f"g_ins{b}") for b in range(2)]
        outs = [sem(c, nc, f"g_outs{b}") for b in range(2)]
        names = ("par", "init", "kv", "pt", "tr", "mq", "o", "pot", "ot", "mo", "x3", "var", "std", "row", "st1", "st2")
        S = {n: sem(c, nc, "g_s_" + n) for n in names}
        tick = sem(c, nc, "g_tick")
        block = c.enter_context(nc.Block())

        @block.sync
        def _(sp):
            for out, in_ in ((wo[:, :, :], T["wo"].rearrange("(c p) n -> p c n", p=P)),
                             (bo[:, :], T["bo"].partition_broadcast(P)),
                             (wr[:, :], T["ffn_wr"].rearrange("d o -> (d o)").partition_broadcast(P)),
                             (br[:, :], T["ffn_br"].partition_broadcast(P))):
                sp.dma_start(out, in_).then_inc(S["par"], 16)

            def first(g, b, u):
                sp.wait_ge(S["row"], g + 1)
                for t, name in ((q_t, "pq"), (x2_t, "x2"), (ag_t, "agg")):
                    sp.dma_start(t[:, b], rows(T[name], g)).then_inc(ins[b], 16)

            def second(g, b, u, used):
                sp.wait_ge(S["row"], g + 3)
                sp.dma_start(rows(T["sel"], g), row_t[:, b]).then_inc(outs[b], 16)
                sp.dma_start(rows(T["out"], g), row_t[:, b, :, D:2 * D]).then_inc(outs[b], 16)

            piped(sp, first, second)
            for b in range(2):
                sp.wait_ge(outs[b], 32 * (G // 2))

        @block.tensor
        def _(pe):
            pe.wait_ge(S["par"], 64)
            pe.wait_ge(S["kv"], 1)

            def first(g, b, u):
                pe.wait_ge(ins[b], u * 48 + 48)
                for j in range(J + 2):
                    i = g * J + j
                    if j < J:
                        pe.wait_ge(S["tr"], i + 1)
                        for k in range(KC):
                            o = pe.transpose(pt[j % 2][:, k, :], q_t[:, b, j, k * P:(k + 1) * P], C["ident"][:, :])
                        o.then_inc(S["pt"], 1)
                    if 0 < j <= J:
                        s = (j - 1) % 2
                        pe.wait_ge(S["tr"], i + 2)
                        pe.wait_ge(S["o"], i)
                        for k in range(KC):
                            o = pe.matmul(pq[s][:, k * HW_:(k + 1) * HW_], tr_t[:, s, k, :], kvh[:, k, :], start=True, stop=True)
                        o.then_inc(S["mq"], 1)
                    if j > 1:
                        s = j % 2
                        pe.wait_ge(S["o"], i + 1)
                        for k in range(KC):
                            o = pe.transpose(pot[:, k, :], o_t[:, s, k * P:(k + 1) * P], C["ident"][:, :])
                        o.then_inc(S["pot"], 1)
                        pe.wait_ge(S["ot"], i - 2 + 1)
                        if j == 2:
                            pe.wait_ge(S["x3"], g + 2)
                        for k in range(KC):
                            o = pe.matmul(po[:, j - 2, :], ot_t[:, s, k, :], wo[:, k, :], start=(k == 0), stop=(k == KC - 1))
                        o.then_inc(S["mo"], 1)

            piped(pe, first, lambda *a: None)

        @block.scalar
        def _(act):
            act.sem_inc(S["tr"], 2)

            def first(g, b, u):
                for j in range(J + 2):
                    i = g * J + j
                    if j < J:
                        act.wait_ge(S["pt"], i + 1)
                        act.wait_ge(S["mq"], i + 1)
                        act.copy(tr_t[:, j % 2], pt[j % 2][:, :, :]).then_inc(S["tr"], 1)
                    if j > 1:
                        act.wait_ge(S["pot"], i - 2 + 1)
                        act.copy(ot_t[:, j % 2], pot[:, :, :]).then_inc(S["ot"], 1)
                act.wait_ge(S["var"], g + 1)
                act.activation(sd[:, :], ve[:, :], ACT.Sqrt).then_inc(S["std"], 1)

            piped(act, first, lambda *a: None)

        @block.vector
        def _(v):
            step = Steps(v, S["init"])
            for k in range(KC):
                i = v.tensor_tensor(kvh[:, k, 0:P], C["kv"][:, k, 0:P], C["heads"][:, :], ALU.mult)
            i = v.tensor_scalar(kvh[:, :, P:HW_], C["heads"][:, 0:P:HC].unsqueeze(1).to_broadcast([P, KC, HEADS // KC]), 1.0, None,
                                ALU.mult)
            step.then(i)
            for k in range(KC):
                i = v.tensor_scalar(kvh[:, k, P:HW_], kvh[:, k, P:HW_], C["kv"][:, k, P:P + 1], None, ALU.mult)
            i.then_inc(S["kv"], 1)
            v.wait_ge(S["par"], 64)
            v.sem_inc(S["mq"], 2)
            v.sem_inc(S["o"], 2)
            v.sem_inc(S["x3"], 2)
            v.sem_inc(S["row"], 2)

            def first(g, b, u):
                step = Steps(v, S["st1"], g, 4 + 4 + 4)
                x, row = x2_t[:, b], row_t[:, b]
                for j in range(J):
                    i, s = g * J + j, j % 2
                    v.wait_ge(S["mq"], i + 3)
                    sums = pq[s][:, 0:KC * HW_].rearrange("p (k n) -> p k n", k=KC)
                    if j > 1:
                        v.wait_ge(S["pot"], i - 1)
                    step.then(v.tensor_scalar(rc[:, s, :].rearrange("p (k h) -> p k h", k=KC), sums[:, :, P:HW_], 1e-6, None, ALU.add))
                    step.then(v.reciprocal(rc[:, s, :], rc[:, s, :]))
                    for k in range(KC):
                        n = HEADS // KC
                        o = v.tensor_tensor(o_t[:, s, k * P:(k + 1) * P].rearrange("p (h e) -> p h e", h=n),
                                            sums[:, k, 0:P].rearrange("p (h e) -> p h e", h=n),
                                            rc[:, s, k * n:(k + 1) * n].unsqueeze(2).to_broadcast([P, n, HC]), ALU.mult)
                    o.then_inc(S["o"], 1)
                v.tensor_tensor(x, x, ag_t[:, b], ALU.add)
                v.wait_ge(outs[b], u * 32)
                step.then(v.tensor_copy(row[:, :, 2 * D + 1].bitcast(I32), cols(C["ids"], g)))
                v.wait_ge(S["mo"], g * J + J)
                step.then(v.tensor_tensor(x, x, po[:, :, :], ALU.add))
                v.tensor_tensor(x, x, bo[:, :].unsqueeze(1).to_broadcast([P, J, D]), ALU.add).then_inc(S["x3"], 1)
                v.wait_ge(S["x3"], g + 3)
                row_mean_var(v, step, tick, x, stats, mv, ve[:, :]).then_inc(S["var"], 1)
                step.end()

            def second(g, b, u, used):
                step = Steps(v, S["st2"], g, 5)
                x, row = x2_t[:, b], row_t[:, b]
                v.wait_ge(S["std"], g + 1)
                step.then(v.reciprocal(rs[:, :], sd[:, :]))
                for j in range(J):
                    i = v.tensor_scalar(row[:, j, 0:D], x[:, j, :], mv[:, j, 0:1], rs[:, j:j + 1], ALU.subtract, ALU.mult)
                step.then(i)
                v.tensor_tensor(row[:, :, D:2 * D], x, row[:, :, 0:D], ALU.add)
                for j in range(J):
                    i = v.scalar_tensor_tensor(junk[:, j, :], row[:, j, 0:D], 1.0, wr[:, :], ALU.mult, ALU.mult, accum_out=wt[:, j:j + 1])
                step.then(i)
                step.then(v.tensor_scalar(wt[:, :], wt[:, :], br[:, 0:1], None, ALU.add))
                step.then(v.tensor_copy(cols(C["wsel"], g), wt[:, :]))
                v.tensor_copy(row[:, :, 2 * D], wt[:, :]).then_inc(S["row"], 1)
                step.end()

            def both(g, b, u):
                first(g, b, u)
                second(g, b, u, P)

            piped(v, both, lambda *a: None)


def select_rows(nc, T, C):
    COLS = NP // P
    with Stage(nc) as c:
        u_t = sb(c, nc, "s_u", [P, COLS])
        junk = sb(c, nc, "s_junk", [P, COLS])
        eq = sb(c, nc, "s_eq", [P, COLS])
        pre = sb(c, nc, "s_pre", [P, COLS])
        sel = sb(c, nc, "s_sel", [P, COLS])
        egs = sb(c, nc, "s_egs", [P, G])
        tot = sb(c, nc, "s_tot", [P, G])
        one = sb(c, nc, "s_one", [P, COLS])
        cnt = sb(c, nc, "s_cnt", [P, 1])
        sg = sb(c, nc, "s_sg", [P, 1])
        want = sb(c, nc, "s_want", [P, 1])
        bit = sb(c, nc, "s_bit", [P, 2])
        thr = sb(c, nc, "s_thr", [P, 1], I32)
        cand = sb(c, nc, "s_cand", [P, 1], I32)
        add = sb(c, nc, "s_add", [P, 1], I32)
        rows_t = sb(c, nc, "s_rows", [P, 2, J, SW])
        io = sb(c, nc, "s_io", [P, 2, J], I32)
        pad = sb(c, nc, "s_pad", [P, SW])
        pc = ps(c, nc, "s_pc", [P, 512])
        pp = ps(c, nc, "s_pp", [P, 512])
        names = ("init", "cnt", "tot", "loop", "go", "io", "step", "pad", "padded")
        S = {n: sem(c, nc, "s_s_" + n) for n in names}
        r_in = [sem(c, nc, f"s_r_in{b}") for b in range(2)]
        sent = [sem(c, nc, f"s_sent{b}") for b in range(2)]
        tick = sem(c, nc, "s_tick")
        block = c.enter_context(nc.Block())
        BITS = 31
        last = SB * GROUP + GROUP

        @block.sync
        def _(sp):
            sp.wait_ge(S["pad"], 1)
            for n, a in enumerate(range(SEL, last, P)):
                k = min(P, last - a)
                sp.dma_start(T["packed"][a:a + k, :], pad[0:k, :]).then_inc(S["padded"], 16)
            sp.wait_ge(S["padded"], 16 * (n + 1))
            with sp.Fori(0, G // 2) as u:
                for b in range(2):
                    sp.wait_ge(sent[b], u * (16 * J))
                    sp.dma_start(rows_t[:, b], rows(T["sel"], u * 2 + b)).then_inc(r_in[b], 16)

        @block.gpsimd
        def _(pool):
            with pool.Fori(0, G // 2) as u:
                for b in range(2):
                    wait_all(pool, tick, (S["io"], u * 2 + b + 1), (r_in[b], u * 16 + 16))
                    for j in range(J):
                        pool.indirect_dma_start(T["packed"], bass.IndirectOffsetOnAxis(ap=io[:, b, j:j + 1], axis=0), rows_t[:, b, j, :],
                                                None, bounds_check=SEL - 1, oob_is_err=False).then_inc(sent[b], 16)
            for b in range(2):
                pool.wait_ge(sent[b], 16 * J * (G // 2))

        @block.tensor
        def _(pe):
            with pe.Fori(0, BITS + 2) as n:
                pe.wait_ge(S["cnt"], n + 1)
                pe.matmul(pc[:, 0:1], C["ones"][:, :], cnt[:, :], start=True, stop=True).then_inc(S["tot"], 1)
            pe.wait_ge(S["cnt"], BITS + 3)
            pe.matmul(pp[:, 0:G], C["tri"][:, :], egs[:, :], start=True, stop=True)
            pe.matmul(pp[:, 256:256 + G], C["ones"][:, :], egs[:, :], start=True, stop=True).then_inc(S["tot"], 1)
            pe.wait_ge(S["cnt"], BITS + 4)
            pe.matmul(pc[:, 0:1], C["tri"][:, :], cnt[:, :], start=True, stop=True).then_inc(S["tot"], 1)

        @block.scalar
        def _(act):
            act.wait_ge(S["go"], 1)
            with act.Fori(0, G // 2) as u:
                for b in range(2):
                    act.wait_ge(sent[b], u * (16 * J))
                    act.copy(io[:, b, :], cols(pre, u * 2 + b)).then_inc(S["io"], 1)

        @block.vector
        def _(v):
            step = Steps(v, S["step"])
            valid = C["valid_cols"]
            w = C["wsel"]
            step.then(v.memset(pad[:, :], 0.0))
            step.then(v.memset(cnt[:, :], FAR))
            v.tensor_copy(pad[:, 2 * D + 1:2 * D + 2].bitcast(I32), cnt[:, :]).then_inc(S["pad"], 1)
            v.memset(one[:, :], 1.0)
            step.then(v.tensor_scalar(junk[:, :], w[:, :], 0.0, None, ALU.is_ge))
            step.then(v.tensor_tensor(junk[:, :], junk[:, :], valid[:, :], ALU.mult))
            v.tensor_reduce(cnt[:, :], junk[:, :], AX.X, ALU.add).then_inc(S["cnt"], 1)
            v.wait_ge(S["tot"], 1)
            step.then(v.tensor_scalar(sg[:, :], pc[:, 0:1], float(SEL), None, ALU.is_ge))
            step.then(v.tensor_scalar(want[:, :], sg[:, :], float(SEL - (N - SEL + 1)), float(N - SEL + 1), ALU.mult, ALU.add))
            step.then(v.tensor_scalar(sg[:, :], sg[:, :], 2.0, -1.0, ALU.mult, ALU.add))
            step.then(v.tensor_scalar(u_t[:, :], w[:, :], sg[:, 0:1], None, ALU.mult))
            step.then(v.tensor_tensor(u_t[:, :], u_t[:, :], valid[:, :], ALU.mult))
            step.then(v.tensor_scalar(junk[:, :], valid[:, :], 1.0, 3.0e38, ALU.subtract, ALU.mult))
            step.then(v.tensor_tensor(u_t[:, :], u_t[:, :], junk[:, :], ALU.add))
            step.then(v.memset(thr[:, :], 0))
            step.then(v.memset(bit[:, 0:1], float(1 << 30)))
            per = 6
            with v.Fori(0, BITS) as n:
                turn = Steps(v, S["loop"], n, per)
                turn.then(v.tensor_copy(add[:, :], bit[:, 0:1]))
                turn.then(v.tensor_tensor(cand[:, :], thr[:, :], add[:, :], ALU.bitwise_or))
                turn.then(v.tensor_scalar(junk[:, :], u_t[:, :], cand[:, 0:1].bitcast(F32), None, ALU.is_ge))
                v.tensor_reduce(cnt[:, :], junk[:, :], AX.X, ALU.add).then_inc(S["cnt"], 1)
                v.wait_ge(S["tot"], n + 2)
                turn.then(v.tensor_scalar(bit[:, 1:2], pc[:, 0:1], want[:, 0:1], bit[:, 0:1], ALU.is_ge, ALU.mult))
                turn.then(v.tensor_copy(add[:, :], bit[:, 1:2]))
                v.tensor_scalar(bit[:, 0:1], bit[:, 0:1], 0.5, None, ALU.mult)
                turn.then(v.tensor_tensor(thr[:, :], thr[:, :], add[:, :], ALU.bitwise_or))
                turn.end()
            step.then(v.tensor_tensor(bit[:, 0:1], thr[:, :].bitcast(F32), sg[:, :], ALU.mult))
            step.then(v.tensor_scalar(sel[:, :], w[:, :], bit[:, 0:1], None, ALU.is_gt))
            step.then(v.tensor_tensor(sel[:, :], sel[:, :], valid[:, :], ALU.mult))
            v.tensor_reduce(cnt[:, :], sel[:, :], AX.X, ALU.add).then_inc(S["cnt"], 1)
            step.then(v.tensor_scalar(eq[:, :], w[:, :], bit[:, 0:1], None, ALU.is_equal))
            step.then(v.tensor_tensor(eq[:, :], eq[:, :], valid[:, :], ALU.mult))
            v.wait_ge(S["tot"], BITS + 2)
            step.then(v.tensor_scalar(want[:, :], pc[:, 0:1], -1.0, float(SEL), ALU.mult, ALU.add))
            v.tensor_reduce(egs[:, :], eq[:, :].rearrange("p (g j) -> p g j", j=J), AX.X, ALU.add).then_inc(S["cnt"], 1)
            v.wait_ge(S["tot"], BITS + 3)
            step.then(v.tensor_copy(tot[:, :], pp[:, 256:256 + G]))
            step.then(v.tensor_tensor_scan(egs[:, :], one[:, 0:G], tot[:, :], 0.0, ALU.mult, ALU.add))
            step.then(v.tensor_tensor(egs[:, :], egs[:, :], tot[:, :], ALU.subtract))
            step.then(v.tensor_tensor(egs[:, :], egs[:, :], pp[:, 0:G], ALU.add))
            p4, e4 = pre[:, :].rearrange("p (g j) -> p g j", j=J), eq[:, :].rearrange("p (g j) -> p g j", j=J)
            step.then(v.tensor_copy(p4[:, :, 0], egs[:, :]))
            for j in range(1, J):
                step.then(v.tensor_tensor(p4[:, :, j], p4[:, :, j - 1], e4[:, :, j - 1], ALU.add))
            step.then(v.scalar_tensor_tensor(pre[:, :], pre[:, :], want[:, 0:1], eq[:, :], ALU.is_lt, ALU.mult))
            step.then(v.tensor_tensor(sel[:, :], sel[:, :], pre[:, :], ALU.add))
            v.tensor_reduce(cnt[:, :], sel[:, :], AX.X, ALU.add).then_inc(S["cnt"], 1)
            step.then(v.tensor_tensor_scan(pre[:, :], one[:, :], sel[:, :], 0.0, ALU.mult, ALU.add))
            v.wait_ge(S["tot"], BITS + 4)
            step.then(v.tensor_scalar(pre[:, :], pre[:, :], pc[:, 0:1], -1.0, ALU.add, ALU.add))
            step.then(v.tensor_scalar(junk[:, :], sel[:, :], -FAR, FAR, ALU.mult, ALU.add))
            v.tensor_tensor(pre[:, :], pre[:, :], junk[:, :], ALU.add).then_inc(S["go"], 1)


def build(nc, T):
    def scratch(name, shape):
        T[name] = nc.dram_tensor("t_" + name, shape, F32).ap()

    for name in ("xn", "agg", "x1", "x2", "hp", "pq"):
        scratch(name, (NP, D))
    scratch("slots", ((EXPERTS * MB + 1) * MT * J, D))
    scratch("y", (EXPERTS * MROWS, D))
    scratch("sc1", (NP, 2 * GH))
    scratch("sc2", (NP, 2))
    scratch("sel", (NP, SW))
    scratch("packed", ((SB + 1) * GROUP, SW))
    scratch("w_edges", (GH, EP))
    scratch("ends", (2 * GH, P))
    scratch("starts", (GH, P + 1))
    with ExitStack() as c:
        C = {}
        for name, shape, dt in (
            ("ident", [P, P], F32), ("tri", [P, P], F32), ("ones", [P, P], F32), ("heads", [P, P], F32),
            ("valid", [P, G], F32), ("valid_cols", [P, NP // P], F32), ("ids", [P, NP // P], I32),
            ("wl", [P, KC, D], F32), ("wr", [P, KC, D], F32), ("kv", [P, KC, P + 1], F32),
            ("src_i", [P, ET + EU], I32), ("out_i", [P, ET], I32), ("dst_f", [P, ET], F32), ("carry_f", [P, ET], F32),
            ("lane_i", [P, ET, 2], I32), ("same_prev", [P, ET], F32), ("same_next", [P, ET], F32),
            ("cut_prev", [P, ET], F32), ("cut_next", [P, ET], F32), ("all_prev", [P, 1], F32), ("all_next", [P, 1], F32),
            ("cut_whole", [P, 1], F32), ("gap", [P, NP // P, EXPERTS], F32), ("kept", [P, NP // P], F32),
            ("from", [P, NP // P], F32), ("w", [P, NP // P], F32), ("wsel", [P, NP // P], F32),
            ("edge_w", [P, ET, GH], F32), ("edge_w1", [P, ET, 1], F32),
        ):
            C[name] = sb(c, nc, "k_" + name, shape, dt)
        stages = (
            lambda: load_constants(nc, T, C),
            lambda: norm_and_gram(nc, T, C),
            lambda: mean_weights(nc, T, C, C["edge_w1"]),
            lambda: aggregate(nc, T, C, "e0", T["xn"], 1, C["edge_w1"]),
            lambda: update_and_gate(nc, T, C),
            lambda: two_layers(nc, T, C, "m0", EXPERTS, MB // 2, MB % 2, MT, D, T["slots"], T["moe_w1"], T["moe_b1"], T["moe_w2"],
                               T["moe_b2"], ACT.Relu, True, T["y"]),
            lambda: combine_and_project(nc, T, C),
            lambda: edge_softmax(nc, T, C, "e1", T["sc1"], GH, C["edge_w"]),
            lambda: aggregate(nc, T, C, "e2", T["hp"], GH, C["edge_w"]),
            lambda: second_features(nc, T, C),
            lambda: edge_softmax(nc, T, C, "e3", T["sc2"], 1, C["edge_w1"]),
            lambda: aggregate(nc, T, C, "e4", T["hp"], 1, C["edge_w1"]),
            lambda: second_update(nc, T, C),
            lambda: select_rows(nc, T, C),
            lambda: two_layers(nc, T, C, "m1", 1, SB // 2, 0, P, SW, T["packed"], T["ffn_w1"], T["ffn_b1"], T["ffn_w2"],
                               T["ffn_b2"], ACT.Gelu_apprx_tanh, False, T["out"]),
        )
        for stage in stages:
            stage()


def layout(i):
    def f(name):
        return np.ascontiguousarray(i[name])

    x = np.zeros((NP, D), np.float32)
    x[:N] = f("x")
    src, dst = f("src").astype(np.int32, copy=False), f("dst").astype(np.int32, copy=False)

    def edges(a, before, after, shift):
        out = np.full(EP + 2, after, np.int32)
        out[0] = out[EP + 1] = before
        out[1:E + 1] = a
        return out[1 + shift:1 + shift + EP]

    far = 32767
    key, prev, nxt = (edges(dst, -1, far, s) for s in (0, -1, 1))
    src_p, dst_p = edges(src, 0, 0, 0), edges(dst, 0, 0, 0)

    def tile(a):
        return np.ascontiguousarray(a.reshape(ET, P).T)

    def lane(a):
        return np.ascontiguousarray(a.reshape(P, ET))

    def scores(a_src, a_dst):
        h, n = a_src.shape
        out = np.zeros((h * n, 2 * h), np.float32)
        for k in range(h):
            out[k * n:(k + 1) * n, k] = a_src[k]
            out[k * n:(k + 1) * n, h + k] = a_dst[k]
        return out

    p, q = np.arange(P)[:, None], np.arange(P)[None, :]
    row = (np.arange(G)[None, :, None] * GROUP + np.arange(P)[:, None, None] * J + np.arange(J)[None, None, :])
    last = np.zeros((P, 2), np.float32)
    last[:, 1] = -5.0
    last[P - 1] = (1.0, 0.0)
    ev = np.stack([np.arange(EXPERTS, 0, -1), np.arange(EXPERTS) * MROWS]).astype(np.float32)
    src_tile = np.zeros((P, ET + EU), np.int32)
    src_tile[:, :ET] = tile(src_p)
    return {
        "x": x,
        "W_l_t": np.ascontiguousarray(f("L0_gnn_W_l").T), "W_r_t": np.ascontiguousarray(f("L0_gnn_W_r").T), "b_r": f("L0_gnn_b_r"),
        "kln_weight": np.ascontiguousarray(f("L0_mix_kln_weight").reshape(KC, P).T),
        "kln_bias": np.ascontiguousarray(f("L0_mix_kln_bias").reshape(KC, P).T),
        "vln_weight": f("L0_mix_vln_weight").reshape(-1), "vln_bias": f("L0_mix_vln_bias").reshape(-1),
        "gate_w": f("L0_ffn_gate_w"), "gate_b": f("L0_ffn_gate_b"),
        "moe_w1": f("L0_ffn_w1"), "moe_w2": f("L0_ffn_w2"), "moe_b2": f("L0_ffn_b2"),
        "moe_b1": np.ascontiguousarray(f("L0_ffn_b1").reshape(EXPERTS, FF // P, P).transpose(0, 2, 1)),
        "W1_t": np.ascontiguousarray(f("L1_gnn_W1").T), "W1": f("L1_gnn_W1"), "a1": scores(f("L1_gnn_a1_src"), f("L1_gnn_a1_dst")),
        "W2_t": np.ascontiguousarray(f("L1_gnn_W2").T), "W2": f("L1_gnn_W2"), "a2": scores(f("L1_gnn_a2_src"), f("L1_gnn_a2_dst")),
        "wq": f("L1_mix_wq"), "wk": f("L1_mix_wk"), "wv": f("L1_mix_wv"), "wo": f("L1_mix_wo"),
        "b_qk": np.concatenate([f("L1_mix_bq"), f("L1_mix_bk")]), "bv": f("L1_mix_bv"), "bo": f("L1_mix_bo"),
        "ffn_wr": f("L1_ffn_wr"), "ffn_br": f("L1_ffn_br"), "ffn_w1": f("L1_ffn_w1")[None], "ffn_w2": f("L1_ffn_w2")[None],
        "ffn_b1": np.ascontiguousarray(f("L1_ffn_b1").reshape(1, FF // P, P).transpose(0, 2, 1)), "ffn_b2": f("L1_ffn_b2")[None],
        "keys": key, "dst_tile": tile(key), "next_tile": tile(nxt), "src_tile": src_tile,
        "lane_i": np.ascontiguousarray(np.stack([lane(src_p), lane(dst_p)], axis=2)),
        "key_lane": lane(key), "prev_lane": lane(prev), "next_lane": lane(nxt),
        "c_ident": np.eye(P, dtype=np.float32), "c_tri": (p < q).astype(np.float32),
        "c_heads": (p // HC == q // HC).astype(np.float32), "c_last": last,
        "c_valid": (row[:, :, 0] < N).astype(np.float32), "c_valid_cols": (row < N).reshape(P, -1).astype(np.float32),
        "c_ids": np.where(row < N, row, int(FAR)).reshape(P, -1).astype(np.int32),
        "c_experts": np.ascontiguousarray(np.broadcast_to(ev, (P, 2, EXPERTS))),
    }


def kernel(**inputs):
    import concourse.bacc as bacc
    from concourse.bass_utils import run_bass_kernel_spmd

    nc = bacc.Bacc("TRN2", target_bir_lowering=False, num_devices=1)
    arrays, T = {}, {}
    for name, a in layout(inputs).items():
        arrays["in_" + name] = a
        T[name] = nc.dram_tensor("in_" + name, a.shape, mybir.dt.from_np(a.dtype), kind="ExternalInput").ap()
    T["out"] = nc.dram_tensor("out", (NP, D), F32, kind="ExternalOutput").ap()
    build(nc, T)
    r = run_bass_kernel_spmd(nc, [arrays], core_ids=[0])
    return r.results[0]["out"][:N]
```

```python
from contextlib import ExitStack

import numpy as np

import concourse.bass as bass
from concourse import mybir

F32 = mybir.dt.float32
I32 = mybir.dt.int32
ALU = mybir.AluOpType
ACT = mybir.ActivationFunctionType
AX = mybir.AxisListType

P = 128
D = 256
KC = D // P
N = 20000
J = 4
GROUP = P * J
G = -(-N // GROUP)
G += G % 2
NP = G * GROUP
FULL_G, LAST_P = N // GROUP, (N % GROUP) // J
E = 30000
ET = -(-E // P)
EP = ET * P
EU = 5
HEADS, HC = 8, 32
LN_EPS = 1e-5
EXPERTS, FF = 8, 1024
CAP = 3125
MB = 7
MT = 112
MROWS = MT * J * MB
GH = 4
SEL = N // 2 - 1
SB = 20
SW = 2 * D + 2
FAR = 1.0e6
BIG = 1.0e30


def sb(c, nc, name, shape, dt=F32):
    return c.enter_context(nc.sbuf_tensor(name, shape, dt))


def ps(c, nc, name, shape, dt=F32):
    return c.enter_context(nc.psum_tensor(name, shape, dt))


def sem(c, nc, name):
    handle = nc.alloc_semaphore(name)
    c.semaphores.append(handle)
    return handle


class Stage(ExitStack):

    def __init__(self, nc):
        super().__init__()
        self.nc, self.semaphores = nc, []

    def __exit__(self, *error):
        super().__exit__(*error)
        if error[0] is None:
            self.nc.clear_and_free_semaphores(self.semaphores)
            self.nc.all_engine_barrier()


def rows(dram, g):
    return dram[bass.ds(g * GROUP, GROUP), :].rearrange("(p j) d -> p j d", j=J)


def wait_all(eng, tick, *waits):
    for s, v in waits:
        eng.wait_ge(s, v)
    eng.sem_inc(tick, 1)


class Steps:

    def __init__(self, eng, semaphore, turn=0, per=0):
        self.eng, self.sem, self.base, self.per, self.k = eng, semaphore, turn * per, per, 0

    def then(self, instruction, tick=None):
        self.k += 1
        instruction.then_inc(self.sem, 1)
        self.eng.wait_ge(self.sem, self.base + self.k)
        if tick is not None:
            self.eng.sem_inc(tick, 1)

    def end(self):
        assert self.k == self.per, (self.k, self.per)


def row_mean_var(v, step, tick, x, stats, mv, ve):
    for j in range(J):
        i = v.bn_stats(stats[:, j, :], x[:, j, :])
    step.then(i, tick)
    for j in range(J):
        i = v.bn_aggr(mv[:, j, :], stats[:, j, :])
    step.then(i)
    return v.tensor_scalar(ve, mv[:, :, 1], LN_EPS, None, ALU.add)


def inverse_root(v, step, rs, ve, nt):
    step.then(v.tensor_scalar(rs[:, :].bitcast(I32), ve[:, :].bitcast(I32), -0.5, float(0x5F3759DF), ALU.mult, ALU.add))
    for n in range(3):
        step.then(v.tensor_tensor(nt[:, :], rs[:, :], rs[:, :], ALU.mult))
        step.then(v.scalar_tensor_tensor(nt[:, :], nt[:, :], -0.5, ve[:, :], ALU.mult, ALU.mult))
        step.then(v.scalar_tensor_tensor(rs[:, :], nt[:, :], 1.5, rs[:, :], ALU.add, ALU.mult))


def norm_and_gram(nc, T, C):
    with Stage(nc) as c:
        x_t = sb(c, nc, "a_x", [P, 2, J, D])
        xn_t = sb(c, nc, "a_xn", [P, 2, J, D])
        d_t = sb(c, nc, "a_d", [P, J, D])
        sq_t = sb(c, nc, "a_sq", [P, J, D])
        z_t = sb(c, nc, "a_z", [P, 2, J, KC, P + 1])
        stats = sb(c, nc, "a_stats", [P, J, 6])
        mv = sb(c, nc, "a_mv", [P, J, 2])
        ve = sb(c, nc, "a_ve", [P, J])
        sd = sb(c, nc, "a_sd", [P, J])
        rs = sb(c, nc, "a_rs", [P, J])
        hm = sb(c, nc, "a_hm", [P, J * HEADS])
        hv = sb(c, nc, "a_hv", [P, J * HEADS])
        hsd = sb(c, nc, "a_hsd", [P, J * HEADS])
        hr = sb(c, nc, "a_hr", [P, J * HEADS])
        zero = sb(c, nc, "a_zero", [P, 512])
        gram = sb(c, nc, "a_gram", [P, KC, P + 1])
        sdiag = sb(c, nc, "a_sdiag", [P, KC, P])
        srow = sb(c, nc, "a_srow", [P, KC, P])
        kcol = sb(c, nc, "a_kcol", [P, 2, KC])
        vrow = sb(c, nc, "a_vrow", [P, 2, D])
        kv = sb(c, nc, "a_kv", [P, KC, P])
        t1 = sb(c, nc, "a_t1", [P, P])
        t2 = sb(c, nc, "a_t2", [P, P])
        cs = sb(c, nc, "a_cs", [P, 1])
        zf = sb(c, nc, "a_zf", [P, 2560])
        pg = ps(c, nc, "a_pg", [P, KC, 256])
        pr = ps(c, nc, "a_pr", [P, KC, 256])
        x_in = [sem(c, nc, f"a_x_in{b}") for b in range(2)]
        xn_out = [sem(c, nc, f"a_xn_out{b}") for b in range(2)]
        s_step = sem(c, nc, "a_step")
        s_fin = sem(c, nc, "a_fin")
        s_var = sem(c, nc, "a_var")
        s_std = sem(c, nc, "a_std")
        s_xn = sem(c, nc, "a_s_xn")
        s_d = sem(c, nc, "a_s_d")
        s_sq = sem(c, nc, "a_s_sq")
        s_hv = sem(c, nc, "a_s_hv")
        s_hsd = sem(c, nc, "a_s_hsd")
        s_z = sem(c, nc, "a_s_z")
        z_free = sem(c, nc, "a_z_free")
        s_gram = sem(c, nc, "a_s_gram")
        s_diag = sem(c, nc, "a_s_diag")
        s_srow = sem(c, nc, "a_s_srow")
        s_zero = sem(c, nc, "a_s_zero")
        s_par = sem(c, nc, "a_s_par")
        s_fill = sem(c, nc, "a_s_fill")
        s_zf = sem(c, nc, "a_s_zf")
        tick = sem(c, nc, "a_tick")
        block = c.enter_context(nc.Block())
        per = 6

        @block.sync
        def _(sp):
            sp.dma_start(kcol[:, 0, :], T["kln_weight"]).then_inc(s_par, 16)
            sp.dma_start(kcol[:, 1, :], T["kln_bias"]).then_inc(s_par, 16)
            sp.dma_start(vrow[:, 0, :], T["vln_weight"].partition_broadcast(P)).then_inc(s_par, 16)
            sp.dma_start(vrow[:, 1, :], T["vln_bias"].partition_broadcast(P)).then_inc(s_par, 16)
            for b in range(2):
                sp.dma_start(x_t[:, b], rows(T["x"], b)).then_inc(x_in[b], 16)
            with sp.Fori(0, G // 2 - 1) as u:
                for b in range(2):
                    g = u * 2 + b
                    sp.wait_ge(s_xn, g + 1)
                    sp.dma_start(x_t[:, b], rows(T["x"], g + 2)).then_inc(x_in[b], 16)
                    sp.dma_start(rows(T["xn"], g), xn_t[:, b]).then_inc(xn_out[b], 16)
            for b in range(2):
                sp.wait_ge(s_xn, G - 1 + b)
                sp.dma_start(rows(T["xn"], G - 2 + b), xn_t[:, b]).then_inc(xn_out[b], 16)
            for b in range(2):
                sp.wait_ge(xn_out[b], 16 * (G // 2))

        @block.gpsimd
        def _(pool):
            pool.memset(zf[:, :], 0.0).then_inc(s_zf, 1)
            pool.wait_ge(s_zf, 1)
            n = 0
            for dram, count in ((T["agg"], NP * D // P), (T["slots"], (EXPERTS * MB + 1) * MT * J * D // P)):
                w = dram.rearrange("r d -> (r d)").rearrange("(p n) -> p n", p=P)
                for a in range(0, count, 2560):
                    k = min(2560, count - a)
                    pool.dma_start(w[:, a:a + k], zf[:, 0:k]).then_inc(s_fill, 16)
                    n += 1
            pool.wait_ge(s_fill, 16 * n)

        @block.scalar
        def _(act):
            with act.Fori(0, G) as g:
                act.wait_ge(s_var, g + 1)
                act.activation(sd[:, :], ve[:, :], ACT.Sqrt).then_inc(s_std, 1)
                act.wait_ge(s_d, g + 1)
                act.activation(sq_t[:, :, :], d_t[:, :, :], ACT.Square).then_inc(s_sq, 1)
                act.wait_ge(s_hv, g + 1)
                act.activation(hsd[:, :], hv[:, :], ACT.Sqrt, scale=1.0 / (HC - 1)).then_inc(s_hsd, 1)

        @block.tensor
        def _(pe):
            pe.wait_ge(s_zero, 1)
            pe.matmul(pg[:, :, :], zero[:, 0:P], zero[:, :], start=True, stop=False, skip_group_check=True)
            pe.sem_inc(z_free, 2)
            with pe.Fori(0, G // 2) as u:
                for b in range(2):
                    pe.wait_ge(s_z, u * 2 + b + 1)
                    for j in range(J):
                        for h in range(KC):
                            i = pe.matmul(pg[:, h, 0:P + 1], z_t[:, b, j, h, 0:P], z_t[:, b, j, h, :],
                                          start=False, stop=False, skip_group_check=True)
                    i.then_inc(z_free, 1)
            pe.matmul(pg[:, :, :], zero[:, 0:P], zero[:, :], start=False, stop=True,
                      skip_group_check=True).then_inc(s_gram, 1)
            pe.wait_ge(s_diag, 1)
            for h in range(KC):
                i = pe.matmul(pr[:, h, 0:P], C["ones"][:, :], sdiag[:, h, :], start=(h == 0), stop=True,
                              skip_group_check=True)
            i.then_inc(s_srow, 1)

        @block.vector
        def _(v):
            v.memset(zero[:, :], 0.0).then_inc(s_zero, 1)
            for b in range(2):
                i = v.memset(z_t[:, b, :, :, P:P + 1], 1.0)
            i.then_inc(s_fin, 1)
            v.wait_ge(s_fin, 1)
            with v.Fori(0, G // 2) as u:
                for b in range(2):
                    g = u * 2 + b
                    step = Steps(v, s_step, g, per)
                    x, xn, z = x_t[:, b], xn_t[:, b], z_t[:, b]
                    v.wait_ge(x_in[b], u * 16 + 16)
                    row_mean_var(v, step, tick, x, stats, mv, ve[:, :]).then_inc(s_var, 1)
                    v.wait_ge(s_std, g + 1)
                    step.then(v.reciprocal(rs[:, :], sd[:, :]))
                    v.wait_ge(xn_out[b], u * 16)
                    for j in range(J):
                        i = v.tensor_scalar(xn[:, j, :], x[:, j, :], mv[:, j, 0:1], rs[:, j:j + 1],
                                            ALU.subtract, ALU.mult)
                    i.then_inc(s_xn, 1)
                    v.wait_ge(s_xn, g + 1)
                    heads = xn.rearrange("p j (h k) -> p (j h) k", k=HC)
                    step.then(v.tensor_reduce(hm[:, :], heads, AX.X, ALU.add))
                    dh = d_t[:, :, :].rearrange("p j (h k) -> p (j h) k", k=HC)
                    v.scalar_tensor_tensor(dh, hm[:, :].unsqueeze(2).to_broadcast([P, J * HEADS, HC]), -1.0 / HC,
                                           heads, ALU.mult, ALU.add).then_inc(s_d, 1)
                    v.wait_ge(s_sq, g + 1)
                    v.tensor_reduce(hv[:, :], sq_t[:, :, :].rearrange("p j (h k) -> p (j h) k", k=HC), AX.X,
                                    ALU.add).then_inc(s_hv, 1)
                    v.wait_ge(s_hsd, g + 1)
                    step.then(v.tensor_scalar(hr[:, :], hsd[:, :], 1e-5, None, ALU.add))
                    step.then(v.reciprocal(hr[:, :], hr[:, :]))
                    v.wait_ge(z_free, g + 1)
                    v.tensor_tensor(z[:, :, :, 0:P].rearrange("p j c (h k) -> p (j c) h k", k=HC),
                                    d_t[:, :, :].rearrange("p j (c h k) -> p (j c) h k", c=KC, k=HC),
                                    hr[:, :].rearrange("p (a h) -> p a h", h=HEADS // KC).unsqueeze(3)
                                    .to_broadcast([P, J * KC, HEADS // KC, HC]), ALU.mult).then_inc(s_z, 1)
                    step.end()
            step = Steps(v, s_fin)
            step.k = 1
            v.wait_ge(s_gram, 1)
            step.then(v.tensor_copy(gram[:, :, :], pg[:, :, 0:P + 1]))
            for h in range(KC):
                i = v.tensor_scalar(sdiag[:, h, :], C["ident"][:, :], gram[:, h, P:P + 1], None, ALU.mult)
            i.then_inc(s_diag, 1)
            v.wait_ge(s_srow, 1)
            step.then(v.tensor_copy(srow[:, :, :], pr[:, :, 0:P]))
            v.wait_ge(s_par, 64)
            for h in range(KC):
                wv, bv = vrow[:, 0, h * P:(h + 1) * P], vrow[:, 1, h * P:(h + 1) * P]
                wk, bk = kcol[:, 0, h:h + 1], kcol[:, 1, h:h + 1]
                step.then(v.scalar_tensor_tensor(t1[:, :], gram[:, h, 0:P], wk, wv, ALU.mult, ALU.mult))
                step.then(v.tensor_tensor(cs[:, :], gram[:, h, P:P + 1], wk, ALU.mult))
                step.then(v.scalar_tensor_tensor(t1[:, :], bv, cs[:, 0:1], t1[:, :], ALU.mult, ALU.add))
                step.then(v.tensor_tensor(t2[:, :], srow[:, h, :], wv, ALU.mult))
                step.then(v.scalar_tensor_tensor(t2[:, :], bv, float(N), t2[:, :], ALU.mult, ALU.add))
                step.then(v.scalar_tensor_tensor(t1[:, :], t2[:, :], bk, t1[:, :], ALU.mult, ALU.add))
                step.then(v.scalar_tensor_tensor(kv[:, h, :], t1[:, :], 1.0 / N, C["heads"][:, :], ALU.mult, ALU.mult))
                step.then(v.tensor_tensor(kv[:, h, :], kv[:, h, :], C["ident"][:, :], ALU.add))
                w = C["wr"][:, h, h * P:(h + 1) * P]
                step.then(v.tensor_tensor(w, w, kv[:, h, :], ALU.add))


def load_constants(nc, T, C):
    with Stage(nc) as c:
        s_in = sem(c, nc, "c_in")
        s_step = sem(c, nc, "c_step")
        di = sb(c, nc, "c_dst_i", [P, ET], I32)
        ni = sb(c, nc, "c_next_i", [P, ET], I32)
        li = sb(c, nc, "c_lane_i", [P, 3, ET], I32)
        nf = sb(c, nc, "c_next_f", [P, ET])
        lf = sb(c, nc, "c_lane_f", [P, 3, ET])
        lt = sb(c, nc, "c_last", [P, 2])
        tick = sem(c, nc, "c_tick")
        block = c.enter_context(nc.Block())
        loads = [
            (C["ident"][:, :], T["c_ident"]), (C["tri"][:, :], T["c_tri"]), (C["heads"][:, :], T["c_heads"]),
            (lt[:, :], T["c_last"]), (C["valid"][:, :], T["c_valid"]),
            (C["valid_cols"][:, :], T["c_valid_cols"]), (C["ids"][:, :], T["c_ids"]),
            (C["wl"][:, :, :], T["W_l_t"].rearrange("(c p) n -> p c n", p=P)),
            (C["wr"][:, :, :], T["W_r_t"].rearrange("(c p) n -> p c n", p=P)),
            (di[:, :], T["dst_tile"]), (ni[:, :], T["next_tile"]), (C["src_i"][:, :], T["src_tile"]),
            (C["lane_i"][:, :, :], T["lane_i"]),
            (li[:, 0, :], T["key_lane"]), (li[:, 1, :], T["prev_lane"]), (li[:, 2, :], T["next_lane"]),
        ]

        @block.sync
        def _(sp):
            for out, in_ in loads:
                sp.dma_start(out, in_).then_inc(s_in, 16)

        @block.vector
        def _(v):
            step = Steps(v, s_step)
            step.then(v.memset(C["ones"][:, :], 1.0))
            v.wait_ge(s_in, 16 * len(loads))
            step.then(v.tensor_copy(C["dst_f"][:, :], di[:, :]))
            step.then(v.tensor_copy(nf[:, :], ni[:, :]))
            step.then(v.tensor_tensor(nf[:, :], nf[:, :], C["dst_f"][:, :], ALU.is_equal))
            step.then(v.scalar_tensor_tensor(nf[:, :], nf[:, :], FAR, C["dst_f"][:, :], ALU.mult, ALU.add))
            step.then(v.tensor_copy(C["out_i"][:, :], nf[:, :]))
            step.then(v.memset(C["carry_f"][:, :], -5.0))
            step.then(v.tensor_scalar(C["carry_f"][:, 1:ET], C["dst_f"][:, 0:ET - 1], lt[:, 0:1], lt[:, 1:2],
                                      ALU.mult, ALU.add))
            step.then(v.tensor_copy(lf[:, :, :], li[:, :, :]))
            step.then(v.tensor_tensor(C["same_prev"][:, :], lf[:, 0, :], lf[:, 1, :], ALU.is_equal))
            step.then(v.tensor_tensor(C["same_next"][:, :], lf[:, 0, :], lf[:, 2, :], ALU.is_equal))
            step.then(v.tensor_scalar(C["cut_prev"][:, :], C["same_prev"][:, :], 1.0, BIG, ALU.subtract, ALU.mult))
            step.then(v.tensor_scalar(C["cut_next"][:, :], C["same_next"][:, :], -1.0, 1.0, ALU.mult, ALU.add))
            step.then(v.tensor_reduce(C["all_prev"][:, :], C["same_prev"][:, :], AX.X, ALU.min))
            step.then(v.tensor_scalar(C["cut_whole"][:, :], C["all_prev"][:, :], 1.0, BIG, ALU.subtract, ALU.mult))
            step.then(v.tensor_reduce(C["all_next"][:, :], C["same_next"][:, :], AX.X, ALU.min))


class Segments:

    def __init__(self, c, nc, T, C, name, heads):
        self.T, self.C, self.h = T, C, heads
        self.f = sb(c, nc, name + "_scan", [P, heads, ET])
        self.g = sb(c, nc, name + "_back", [P, heads, ET])
        self.ends = sb(c, nc, name + "_ends", [P, 2, heads])
        self.row = sb(c, nc, name + "_row", [1, 2, heads, P])
        self.out = sb(c, nc, name + "_out", [1, heads, P + 1])
        self.start = sb(c, nc, name + "_start", [P, heads])
        self.s_ends = sem(c, nc, name + "_s_ends")
        self.s_row = sem(c, nc, name + "_s_row")
        self.s_out = sem(c, nc, name + "_s_out")
        self.s_start = sem(c, nc, name + "_s_start")
        self.s_hop = sem(c, nc, name + "_s_hop")
        self.n = 0

    def carry(self, sp, passes):
        hop = 0
        for n in range(passes):
            ends_d, out_d = self.T["ends"], self.T["starts"]
            h = self.h
            sp.wait_ge(self.s_ends, n + 1)
            sp.dma_start(ends_d[0:2 * h, :].rearrange("a p -> p a"), self.ends[:, :, :].rearrange("p a h -> p (a h)"),
                         allow_slow_non_contiguous=True).then_inc(self.s_hop, 16)
            hop += 16
            sp.wait_ge(self.s_hop, hop)
            sp.dma_start(self.row[:, :, :, :].rearrange("o a h p -> o (a h p)"),
                         ends_d[0:2 * h, :].rearrange("a p -> (a p)").unsqueeze(0)).then_inc(self.s_row, 16)
            sp.wait_ge(self.s_out, n + 1)
            sp.dma_start(out_d[0:h, :].rearrange("a p -> (a p)").unsqueeze(0),
                         self.out[:, :, :].rearrange("o h p -> o (h p)")).then_inc(self.s_hop, 16)
            hop += 16
            sp.wait_ge(self.s_hop, hop)
            o = 0 if n % 2 == 0 else 1
            sp.dma_start(self.start[:, :], out_d[0:h, o:o + P].rearrange("a p -> p a"),
                         allow_slow_non_contiguous=True).then_inc(self.s_start, 16)

    def scan(self, v, step, out, data0, data1, op0, op1, back, whole, first):
        h = self.h
        flip = (lambda a: a[:, ::-1]) if back else (lambda a: a)
        for k in range(h):
            i = v.tensor_tensor_scan(flip(out[:, k, :]), flip(data0), flip(data1[:, k, :]), first, op0, op1)
        step.then(i)
        for k in range(h):
            v.tensor_copy(self.ends[:, 0, k:k + 1], out[:, k, 0:1] if back else out[:, k, ET - 1:ET])
            i = v.tensor_copy(self.ends[:, 1, k:k + 1], whole)
        i.then_inc(self.s_ends, 1)
        n = self.n
        v.wait_ge(self.s_row, 16 * (n + 1))
        step.then(v.memset(self.out[:, :, :], first))
        for k in range(h):
            o = self.out[:, k, 0:P] if back else self.out[:, k, 1:P + 1]
            i = v.tensor_tensor_scan(flip(o), flip(self.row[:, 1, k, :]), flip(self.row[:, 0, k, :]), first, op0, op1)
        i.then_inc(self.s_out, 1)
        v.wait_ge(self.s_start, 16 * (n + 1))
        for k in range(h):
            i = v.tensor_tensor_scan(flip(out[:, k, :]), flip(data0), flip(data1[:, k, :]), self.start[:, k:k + 1],
                                     op0, op1)
        step.then(i)
        self.n += 1

    def total(self, v, step, x, largest):
        C = self.C
        if largest:
            self.scan(v, step, self.f, C["cut_prev"][:, :], x, ALU.add, ALU.max, False, C["cut_whole"][:, :], -BIG)
        else:
            self.scan(v, step, self.f, C["same_prev"][:, :], x, ALU.mult, ALU.add, False, C["all_prev"][:, :], 0.0)
        cut = C["cut_next"][:, :].unsqueeze(1).to_broadcast([P, self.h, ET])
        step.then(v.tensor_tensor(self.f[:, :, :], self.f[:, :, :], cut, ALU.mult))
        self.scan(v, step, self.g, C["same_next"][:, :], self.f, ALU.mult, ALU.add, True, C["all_next"][:, :], 0.0)


def spread_weights(nc, T, C, h, block, w, w_tile, s_w, names):
    rows_t, pt, s_wd, s_wr, s_pt = names
    low = ET - P

    def load(sp):
        sp.wait_ge(s_w, 1)
        sp.dma_start(T["w_edges"][0:h, :].rearrange("h (p c) -> p h c", p=P), w[:, :, :]).then_inc(s_wd, 16)
        sp.wait_ge(s_wd, 16)
        view = T["w_edges"][0:h, :].rearrange("h (i e) -> i h e", e=P)
        sp.dma_start(rows_t[:, 0, :, :], view[0:P]).then_inc(s_wr, 16)
        sp.dma_start(rows_t[0:low, 1, :, :], view[P:ET]).then_inc(s_wr, 16)

    def turn(pe):
        pe.wait_ge(s_wr, 32)
        for k in range(h):
            pe.transpose(pt[:, k, 0:P], rows_t[:, 0, k, :], C["ident"][:, :])
            i = pe.transpose(pt[:, k, P:ET], rows_t[0:low, 1, k, :], C["ident"][0:low, 0:low])
        i.then_inc(s_pt, 1)

    def land(v):
        v.wait_ge(s_pt, 1)
        return v.tensor_copy(w_tile[:, :, :].rearrange("p i h -> p h i"), pt[:, 0:h, 0:ET])

    return load, turn, land


def weight_buffers(c, nc, name, h):
    return (sb(c, nc, name + "_rows", [P, 2, h, P]), ps(c, nc, name + "_pt", [P, h, 256]),
            sem(c, nc, name + "_s_wd"), sem(c, nc, name + "_s_wr"), sem(c, nc, name + "_s_pt"))


def mean_weights(nc, T, C, w_tile):
    with Stage(nc) as c:
        ones_e = sb(c, nc, "m_ones", [P, 1, ET])
        seg = Segments(c, nc, T, C, "m_seg", 1)
        names = weight_buffers(c, nc, "m", 1)
        s_step = sem(c, nc, "m_step")
        s_w = sem(c, nc, "m_s_w")
        tick = sem(c, nc, "m_tick")
        block = c.enter_context(nc.Block())
        load, turn, land = spread_weights(nc, T, C, 1, block, ones_e, w_tile, s_w, names)

        @block.sync
        def _(sp):
            seg.carry(sp, 2)
            load(sp)

        @block.tensor
        def _(pe):
            turn(pe)

        @block.vector
        def _(v):
            step = Steps(v, s_step)
            step.then(v.memset(ones_e[:, :, :], 1.0))
            seg.total(v, step, ones_e, False)
            v.reciprocal(ones_e[:, :, :], seg.g[:, :, :]).then_inc(s_w, 1)
            step.then(land(v))


class AttentionSums:

    def __init__(self, c, nc, T, C):
        self.T, self.C, self.QK = T, C, 2 * D
        self.x_t = sb(c, nc, "q_x", [P, 2, J, D])
        self.tr_t = sb(c, nc, "q_tr", [P, 2, KC, P])
        self.wqk = sb(c, nc, "q_wqk", [P, KC, self.QK])
        self.wv = sb(c, nc, "q_wv", [P, KC, D])
        self.bqk = sb(c, nc, "q_bqk", [P, self.QK])
        self.bv = sb(c, nc, "q_bv", [P, D])
        self.t_t = sb(c, nc, "q_t", [P, 2, self.QK])
        self.e_t = sb(c, nc, "q_e", [P, 2, self.QK])
        self.k_t = sb(c, nc, "q_k", [P, J, D])
        self.q_t = sb(c, nc, "q_q", [P, 2, J, D])
        self.v_t = sb(c, nc, "q_v", [P, J, KC, P + 1])
        self.zero = sb(c, nc, "q_zero", [P, 512])
        self.pt = ps(c, nc, "q_pt", [P, KC, P])
        self.pqk = [ps(c, nc, f"q_pqk{n}", [P, 512]) for n in range(2)]
        self.pv = [ps(c, nc, f"q_pv{n}", [P, 512]) for n in range(2)]
        self.pkv = ps(c, nc, "q_pkv", [P, KC, 256])
        self.x_in = [sem(c, nc, f"q_x_in{b}") for b in range(2)]
        self.q_out = [sem(c, nc, f"q_q_out{b}") for b in range(2)]
        self.s_par, self.s_init, self.s_pt, self.s_tr, self.s_mm, self.s_qkb, self.s_e, self.s_ph, self.s_kv = (
            sem(c, nc, "q_s_" + n) for n in ("par", "init", "pt", "tr", "mm", "qkb", "e", "ph", "kv"))

    def sync(self, sp):
        T = self.T
        for out, in_ in ((self.wqk[:, :, 0:D], T["wq"].rearrange("(c p) n -> p c n", p=P)),
                         (self.wqk[:, :, D:], T["wk"].rearrange("(c p) n -> p c n", p=P)),
                         (self.wv[:, :, :], T["wv"].rearrange("(c p) n -> p c n", p=P)),
                         (self.bqk[:, :], T["b_qk"].partition_broadcast(P)),
                         (self.bv[:, :], T["bv"].partition_broadcast(P))):
            sp.dma_start(out, in_).then_inc(self.s_par, 16)

        def load(g, b, u):
            sp.wait_ge(self.s_pt, g * J + J - 1)
            sp.dma_start(self.x_t[:, b], rows(T["xn"], g)).then_inc(self.x_in[b], 16)

        def store(g, b, u, used):
            sp.wait_ge(self.s_ph, g * J + J + 2)
            sp.dma_start(rows(T["pq"], g), self.q_t[:, b]).then_inc(self.q_out[b], 16)

        ahead(sp, load, store)
        for b in range(2):
            sp.wait_ge(self.q_out[b], 16 * (G // 2))

    def tensor(self, pe):
        def turn(i, b, u, j):
            if j == 0:
                pe.wait_ge(self.x_in[b], u * 16 + 16)
            pe.wait_ge(self.s_tr, i + 1)
            for k in range(KC):
                o = pe.transpose(self.pt[:, k, :], self.x_t[:, b, j, k * P:(k + 1) * P], self.C["ident"][:, :])
            o.then_inc(self.s_pt, 1)

        def sums(i, j, used):
            pe.wait_ge(self.s_ph, i + 3)
            for k in range(KC):
                pe.matmul(self.pkv[:, k, 0:P + 1], self.k_t[0:used, j, k * P:(k + 1) * P], self.v_t[0:used, j, k, :],
                          start=False, stop=False, skip_group_check=True)

        def group(g, b, u, used):
            for j in range(J):
                i, s = g * J + j, j % 2
                if j < J - 1:
                    turn(i + 1, b, u, j + 1)
                elif used == P:
                    turn(i + 1, 1 - b, u + b, 0)
                pe.wait_ge(self.s_tr, i + 2)
                pe.wait_ge(self.s_qkb, i + 1)
                for out, w, n in ((self.pv[s], self.wv, D), (self.pqk[s], self.wqk, self.QK)):
                    for k in range(KC):
                        o = pe.matmul(out[:, 0:n], self.tr_t[:, s, k, :], w[:, k, :], start=(k == 0), stop=(k == KC - 1))
                o.then_inc(self.s_mm, 1)
                sums(i - 2, (j - 2) % J, used if j > 1 else P)
            if used < P:
                for j in range(J - 2, J):
                    sums(g * J + j, j, used)

        pe.wait_ge(self.s_par, 16 * 5)
        pe.wait_ge(self.s_init, 1)
        pe.matmul(self.pkv[:, :, :], self.zero[:, 0:P], self.zero[:, :], start=True, stop=False, skip_group_check=True)
        pe.sem_inc(self.s_mm, 2)
        pe.sem_inc(self.s_pt, 2 * J - 1)
        turn(0, 0, 0, 0)
        ahead(pe, lambda *a: None, group)
        pe.matmul(self.pkv[:, :, :], self.zero[:, 0:P], self.zero[:, :], start=False, stop=True,
                  skip_group_check=True).then_inc(self.s_kv, 1)

    def turned(self, act, i, s):
        act.wait_ge(self.s_pt, i + 2 * J)
        act.wait_ge(self.s_mm, i + 1)
        act.copy(self.tr_t[:, s], self.pt[:, :, :]).then_inc(self.s_tr, 1)

    def scalar_begin(self, act):
        act.sem_inc(self.s_tr, 1)
        self.turned(act, 0, 0)

    def scalar_tile(self, act, g, b, u, j, used):
        i, s = g * J + j, j % 2
        if j < J - 1 or used == P:
            self.turned(act, i + 1, 1 - s)
        act.wait_ge(self.s_qkb, i + 3)
        act.activation(self.e_t[:, s], self.t_t[:, s], ACT.Exp)
        act.activation(self.t_t[:, s], self.t_t[:, s], ACT.Relu).then_inc(self.s_e, 1)

    def vector_begin(self, v):
        v.memset(self.zero[:, :], 0.0)
        v.memset(self.k_t[:, :, :], 0.0)
        for k in range(KC):
            v.memset(self.v_t[:, :, k, 0:P], 0.0)
            i = v.memset(self.v_t[:, :, k, P:P + 1], 1.0)
        i.then_inc(self.s_init, 1)
        v.wait_ge(self.s_init, 1)
        v.wait_ge(self.s_par, 16 * 5)
        v.sem_inc(self.s_qkb, 2)
        v.sem_inc(self.s_ph, 2)

    def vector_tile(self, v, g, b, u, j, used):
        def phi(i, j):
            s = j % 2
            v.wait_ge(self.s_e, i + 1)
            v.scalar_tensor_tensor(self.q_t[:, b, j], self.e_t[:, s, 0:D], 1.0, self.t_t[:, s, 0:D], ALU.min, ALU.add)
            v.scalar_tensor_tensor(self.k_t[:, j], self.e_t[:, s, D:], 1.0, self.t_t[:, s, D:], ALU.min,
                                   ALU.add).then_inc(self.s_ph, 1)

        i, s = g * J + j, j % 2
        if j == 0:
            v.wait_ge(self.q_out[b], u * 16)
        v.wait_ge(self.s_mm, i + 3)
        v.tensor_tensor(self.v_t[:, j, :, 0:P], self.pv[s][:, 0:D].rearrange("p (c n) -> p c n", c=KC),
                        self.bv[:, :].rearrange("p (c n) -> p c n", c=KC), ALU.add)
        v.wait_ge(self.s_ph, i + 1)
        v.tensor_tensor(self.t_t[:, s], self.pqk[s][:, :], self.bqk[:, :], ALU.add).then_inc(self.s_qkb, 1)
        if j > 0:
            phi(i - 1, j - 1)
        if j == J - 1:
            phi(i, j)

    def vector_end(self, v):
        v.wait_ge(self.s_kv, 1)
        v.tensor_copy(self.C["kv"][:, :, :], self.pkv[:, :, 0:P + 1])


def edge_softmax(nc, T, C, name, table, h, w_tile, guest=None):
    with Stage(nc) as c:
        ig = sb(c, nc, name + "_ig", [P, EU, 2], I32)
        gs = sb(c, nc, name + "_gs", [P, EU, 2 * h])
        gd = sb(c, nc, name + "_gd", [P, EU, 2 * h])
        e = sb(c, nc, name + "_e", [P, h, ET])
        w = sb(c, nc, name + "_w", [P, h, ET])
        seg = Segments(c, nc, T, C, name + "_seg", h)
        names = weight_buffers(c, nc, name, h)
        g_in = [sem(c, nc, f"{name}_g_in{k}") for k in range(EU)]
        s_ig = sem(c, nc, name + "_s_ig")
        e_free = sem(c, nc, name + "_e_free")
        s_step = sem(c, nc, name + "_step")
        s_arg = sem(c, nc, name + "_s_arg")
        s_exp = sem(c, nc, name + "_s_exp")
        s_w = sem(c, nc, name + "_s_w")
        tick = sem(c, nc, name + "_tick")
        rows_work = guest(c, nc, T, C) if guest else None
        block = c.enter_context(nc.Block())

        def edge_tiles(eng, edge_tile, row_tile):
            if rows_work is None:
                with eng.Fori(0, ET // EU) as t:
                    for k in range(EU):
                        edge_tile(t, k)
                return

            def turn(g, b, u, used):
                for k in range(EU):
                    edge_tile(g, k)
                    if k < J:
                        row_tile(g, b, u, k, used)

            ahead(eng, lambda *a: None, turn)
            with eng.Fori(G, ET // EU) as t:
                for k in range(EU):
                    edge_tile(t, k)

        load, turn, land = spread_weights(nc, T, C, h, block, w, w_tile, s_w, names)

        @block.sync
        def _(sp):
            if rows_work:
                rows_work.sync(sp)
            seg.carry(sp, 4)
            load(sp)

        @block.tensor
        def _(pe):
            if rows_work:
                rows_work.tensor(pe)
            turn(pe)

        @block.gpsimd
        def _(pool):
            with pool.Fori(0, ET // EU) as t:
                for k in range(EU):
                    wait_all(pool, tick, (s_ig, t * EU + k + 1), (e_free, t * EU + k + 1))
                    for n, buf in ((0, gs), (1, gd)):
                        pool.indirect_dma_start(buf[:, k, :], None, table, bass.IndirectOffsetOnAxis(ap=ig[:, k, n:n + 1], axis=0),
                                                bounds_check=NP - 1, oob_is_err=False).then_inc(g_in[k], 16)

        @block.scalar
        def _(act):
            def indices(t, k):
                act.wait_ge(g_in[k], t * 32)
                act.copy(ig[:, k, :], C["lane_i"][:, bass.ds(t * EU + k, 1), :].rearrange("p o n -> p (o n)")).then_inc(s_ig, 1)

            for k in range(EU):
                indices(0, k)
            if rows_work:
                rows_work.scalar_begin(act)
            edge_tiles(act, lambda t, k: indices(t + 1, k), lambda *a: rows_work.scalar_tile(act, *a))
            act.wait_ge(s_arg, 1)
            act.activation(w[:, :, :], w[:, :, :], ACT.Exp).then_inc(s_exp, 1)

        @block.vector
        def _(v):
            v.sem_inc(e_free, EU)

            def sums(t, k):
                v.wait_ge(g_in[k], t * 32 + 32)
                v.tensor_tensor(e[:, :, bass.ds(t * EU + k, 1)].rearrange("p h o -> p (h o)"), gs[:, k, 0:h],
                                gd[:, k, h:2 * h], ALU.add).then_inc(e_free, 1)

            if rows_work:
                rows_work.vector_begin(v)
            edge_tiles(v, sums, lambda *a: rows_work.vector_tile(v, *a))
            if rows_work:
                rows_work.vector_end(v)
            v.wait_ge(e_free, ET + EU)
            step = Steps(v, s_step)
            step.then(v.scalar_tensor_tensor(e[:, :, :], e[:, :, :], 0.2, e[:, :, :], ALU.mult, ALU.max))
            seg.total(v, step, e, True)
            v.tensor_tensor(w[:, :, :], e[:, :, :], seg.g[:, :, :], ALU.subtract).then_inc(s_arg, 1)
            v.wait_ge(s_exp, 1)
            seg.total(v, step, w, False)
            step.then(v.tensor_scalar(seg.g[:, :, :], seg.g[:, :, :], 1e-16, None, ALU.add))
            step.then(v.reciprocal(seg.g[:, :, :], seg.g[:, :, :]))
            v.tensor_tensor(w[:, :, :], w[:, :, :], seg.g[:, :, :], ALU.mult).then_inc(s_w, 1)
            step.then(land(v))


def aggregate(nc, T, C, name, table, h, w_tile):
    AHEAD = 3
    with Stage(nc) as c:
        keys = sb(c, nc, name + "_keys", [P, EU, P], I32)
        ig = sb(c, nc, name + "_ig", [P, EU], I32)
        io = sb(c, nc, name + "_io", [P, EU], I32)
        msg = sb(c, nc, name + "_msg", [P, EU, D])
        m = sb(c, nc, name + "_m", [P, EU, P])
        cm = sb(c, nc, name + "_cm", [P, EU, P])
        res = sb(c, nc, name + "_res", [P, EU, D])
        pa = [ps(c, nc, f"{name}_pa{k}", [P, 512]) for k in range(EU)]
        k_in = [sem(c, nc, f"{name}_k_in{k}") for k in range(EU)]
        g_in = [sem(c, nc, f"{name}_g_in{k}") for k in range(EU)]
        r_out = [sem(c, nc, f"{name}_r_out{k}") for k in range(EU)]
        s_ig = sem(c, nc, name + "_s_ig")
        s_io = sem(c, nc, name + "_s_io")
        s_m = sem(c, nc, name + "_s_m")
        s_sum = sem(c, nc, name + "_s_sum")
        s_res = sem(c, nc, name + "_s_res")
        s_zero = sem(c, nc, name + "_s_zero")
        tick = sem(c, nc, name + "_tick")
        block = c.enter_context(nc.Block())
        turns = ET // EU

        @block.sync
        def _(sp):
            sp.wait_ge(s_zero, 1)
            with sp.Fori(0, turns) as t:
                for k in range(EU):
                    sp.wait_ge(s_m, t * EU + k + 1)
                    sp.dma_start(keys[:, k, :], T["keys"][bass.ds((t * EU + k) * P, P)].partition_broadcast(P))\
                        .then_inc(k_in[k], 16)

        @block.gpsimd
        def _(pool):
            def gather(k, i):
                wait_all(pool, tick, (s_ig, i + 1), (s_sum, i + 1))
                pool.indirect_dma_start(msg[:, k, :], None, table, bass.IndirectOffsetOnAxis(ap=ig[:, k:k + 1], axis=0),
                                        bounds_check=NP - 1, oob_is_err=False).then_inc(g_in[k], 16)

            for i in range(AHEAD):
                gather(i, i)
            with pool.Fori(0, turns) as t:
                for k in range(EU):
                    gather((k + AHEAD) % EU, t * EU + k + AHEAD)
                    wait_all(pool, tick, (s_res, t * EU + k + 1))
                    pool.indirect_dma_start(T["agg"], bass.IndirectOffsetOnAxis(ap=io[:, k:k + 1], axis=0), res[:, k, :], None,
                                            bounds_check=NP - 1, oob_is_err=False).then_inc(r_out[k], 16)
            for k in range(EU):
                pool.wait_ge(r_out[k], 16 * turns)
                pool.wait_ge(g_in[k], 16 * (turns + (k < AHEAD)))

        @block.scalar
        def _(act):
            def sources(k, i, uses):
                act.wait_ge(g_in[k], uses)
                act.copy(ig[:, k:k + 1], C["src_i"][:, bass.ds(i, 1)]).then_inc(s_ig, 1)

            for i in range(AHEAD):
                sources(i, i, 0)
            with act.Fori(0, turns) as t:
                for k in range(EU):
                    sources((k + AHEAD) % EU, t * EU + k + AHEAD, (t + (k + AHEAD) // EU) * 16)
                    act.wait_ge(r_out[k], t * 16)
                    act.copy(io[:, k:k + 1], C["out_i"][:, bass.ds(t * EU + k, 1)])
                    act.wait_ge(s_sum, t * EU + k + 1 + EU)
                    act.copy(res[:, k, :], pa[k][:, 0:D]).then_inc(s_res, 1)

        @block.tensor
        def _(pe):
            pe.wait_ge(s_zero, 1)
            pe.sem_inc(s_sum, EU)
            with pe.Fori(0, turns) as t:
                for k in range(EU):
                    i = t * EU + k
                    pe.wait_ge(g_in[k], t * 16 + 16)
                    pe.wait_ge(s_m, i + 1 + EU)
                    pe.matmul(pa[k][:, 0:D], m[:, k, :], msg[:, k, :], start=True, stop=False)
                    pe.wait_ge(s_res, i)
                    pe.matmul(pa[k][:, 0:D], cm[:, k, :], res[:, (k - 1) % EU, :], start=False, stop=True).then_inc(s_sum, 1)

        @block.vector
        def _(v):
            v.memset(res[:, EU - 1, :], 0.0).then_inc(s_zero, 1)
            v.sem_inc(s_m, EU)
            with v.Fori(0, turns) as t:
                for k in range(EU):
                    i = t * EU + k
                    v.wait_ge(k_in[k], t * 16 + 16)
                    v.wait_ge(s_sum, i + 1)
                    if h == 1:
                        v.tensor_scalar(m[:, k, :], keys[:, k, :], C["dst_f"][:, bass.ds(i, 1)],
                                        w_tile[:, bass.ds(i, 1), :].rearrange("p o h -> p (o h)"), ALU.is_equal, ALU.mult)
                    else:
                        v.tensor_scalar(m[:, k, :], keys[:, k, :], C["dst_f"][:, bass.ds(i, 1)], None, ALU.is_equal)
                        v.wait_ge(g_in[k], t * 16 + 16)
                        rows_k = msg[:, k, :].rearrange("p (h f) -> p h f", h=h)
                        v.tensor_tensor(rows_k, rows_k, w_tile[:, bass.ds(i, 1), :].rearrange("p o h -> p (o h)")
                                        .unsqueeze(2).to_broadcast([P, h, D // h]), ALU.mult)
                    v.tensor_scalar(cm[:, k, :], keys[:, k, :], C["carry_f"][:, bass.ds(i, 1)], None, ALU.is_equal)\
                        .then_inc(s_m, 1)


def piped(eng, first, second):
    first(0, 0, 0)
    with eng.Fori(0, G // 2 - 1) as u:
        first(u * 2 + 1, 1, u)
        second(u * 2, 0, u, P)
        first(u * 2 + 2, 0, u + 1)
        second(u * 2 + 1, 1, u, P)
    first(G - 1, 1, G // 2 - 1)
    second(G - 2, 0, G // 2 - 1, P)
    second(G - 1, 1, G // 2 - 1, LAST_P)


def ahead(eng, start, body, begun=None, last=None):
    start(0, 0, 0)
    start(1, 1, 0)
    if begun is not None:
        begun()
    with eng.Fori(0, G // 2 - 1) as u:
        for b in range(2):
            start(u * 2 + b + 2, b, u + 1)
            body(u * 2 + b, b, u, P)
    for b in range(2):
        (last or body)(G - 2 + b, b, G // 2 - 1, (P, LAST_P)[b])


def staggered(update, middle, finish, eng):
    update(0, 0, 0)
    update(1, 1, 0)
    middle(0, 0)
    with eng.Fori(0, G // 2 - 1) as u:
        for b in range(2):
            g = u * 2 + b
            update(g + 2, b, u + 1, g)
            middle(g + 1, 1 - b)
    finish(G - 2)
    middle(G - 1, 1)
    finish(G - 1)


def cols(tile, g):
    return tile[:, bass.ds(g * J, J)]


def update_and_gate(nc, T, C):
    with Stage(nc) as c:
        x_t = sb(c, nc, "b_x", [P, 2, J, D])
        xn_t = sb(c, nc, "b_xn", [P, 2, J, D])
        ag_t = sb(c, nc, "b_ag", [P, 2, J, D])
        x1_t = sb(c, nc, "b_x1", [P, 2, J, D])
        xl_t = sb(c, nc, "b_xl", [P, 2, J, D])
        tr_t = sb(c, nc, "b_tr", [P, 2, 4, P])
        lt_t = sb(c, nc, "b_lt", [P, 2, 4, P])
        gate = sb(c, nc, "b_gate", [P, KC, EXPERTS])
        gb = sb(c, nc, "b_gb", [P, EXPERTS])
        br = sb(c, nc, "b_br", [P, D])
        ev = sb(c, nc, "b_ev", [P, 2, EXPERTS])
        stats = sb(c, nc, "b_stats", [P, J, 6])
        mv = sb(c, nc, "b_mv", [P, J, 2])
        ve = sb(c, nc, "b_ve", [P, J])
        nt = sb(c, nc, "b_nt", [P, J])
        rs = sb(c, nc, "b_rs", [P, J])
        lg = sb(c, nc, "b_lg", [P, J, EXPERTS])
        rk = sb(c, nc, "b_rk", [P, J, EXPERTS])
        oh = sb(c, nc, "b_oh", [P, J, EXPERTS])
        cum = sb(c, nc, "b_cum", [P, J + 1, EXPERTS])
        run = sb(c, nc, "b_run", [P, EXPERTS])
        m4 = sb(c, nc, "b_m4", [P, 5, J])
        io = sb(c, nc, "b_io", [P, 2, J], I32)
        pt = [ps(c, nc, f"b_pt{n}", [P, 4, P]) for n in range(2)]
        px = [ps(c, nc, f"b_px{b}", [P, J, D]) for b in range(2)]
        pl = ps(c, nc, "b_pl", [P, 4, P])
        pg = ps(c, nc, "b_pg", [P, 512])
        pgate = pg[:, 0:J * EXPERTS].rearrange("p (j e) -> p j e", e=EXPERTS)
        ppre = pg[:, 64:64 + EXPERTS]
        ins = [sem(c, nc, f"b_ins{b}") for b in range(2)]
        outs = [sem(c, nc, f"b_outs{b}") for b in range(2)]
        sent = [sem(c, nc, f"b_sent{b}") for b in range(2)]
        s_par = sem(c, nc, "b_par")
        s_pt = sem(c, nc, "b_s_pt")
        s_tr = sem(c, nc, "b_s_tr")
        s_mm = sem(c, nc, "b_s_mm")
        s_px = sem(c, nc, "b_s_px")
        s_x1 = sem(c, nc, "b_s_x1")
        s_xl = sem(c, nc, "b_s_xl")
        s_pl = sem(c, nc, "b_s_pl")
        s_lt = sem(c, nc, "b_s_lt")
        s_gate = sem(c, nc, "b_s_gate")
        s_tot = sem(c, nc, "b_s_tot")
        s_pre = sem(c, nc, "b_s_pre")
        s_io = sem(c, nc, "b_s_io")
        s_init = sem(c, nc, "b_s_init")
        st1 = sem(c, nc, "b_step1")
        st2 = sem(c, nc, "b_step2")
        st3 = sem(c, nc, "b_step3")
        tick = sem(c, nc, "b_tick")
        block = c.enter_context(nc.Block())

        @block.sync
        def _(sp):
            sp.dma_start(gate[:, :, :], T["gate_w"].rearrange("(c p) e -> p c e", p=P)).then_inc(s_par, 16)
            sp.dma_start(gb[:, :], T["gate_b"].partition_broadcast(P)).then_inc(s_par, 16)
            sp.dma_start(br[:, :], T["b_r"].partition_broadcast(P)).then_inc(s_par, 16)
            sp.dma_start(ev[:, :, :], T["c_experts"]).then_inc(s_par, 16)

            def load(g, b, u):
                sp.wait_ge(s_x1, g + 1)
                for t, name in ((x_t, "x"), (xn_t, "xn"), (ag_t, "agg")):
                    sp.dma_start(t[:, b], rows(T[name], g)).then_inc(ins[b], 16)

            def store(g, b, u, used):
                sp.wait_ge(s_x1, g + 3)
                sp.dma_start(rows(T["x1"], g), x1_t[:, b]).then_inc(outs[b], 16)

            ahead(sp, load, store)
            for b in range(2):
                sp.wait_ge(outs[b], 16 * (G // 2))

        @block.gpsimd
        def _(pool):
            def second(g, b, u, used):
                wait_all(pool, tick, (s_io, g + 1))
                for j in range(J):
                    pool.indirect_dma_start(T["slots"], bass.IndirectOffsetOnAxis(ap=io[:, b, j:j + 1], axis=0),
                                            xl_t[:, b, j, :], None, bounds_check=EXPERTS * MROWS - 1,
                                            oob_is_err=False).then_inc(sent[b], 16)

            piped(pool, lambda *a: None, second)
            for b in range(2):
                pool.wait_ge(sent[b], 16 * J * (G // 2))

        @block.tensor
        def _(pe):
            pe.wait_ge(s_par, 64)
            pe.sem_inc(s_mm, 2)

            def update(g, b, u, counted=None):
                pe.wait_ge(ins[b], u * 48 + 48)
                pe.wait_ge(s_x1, g + 1)
                for j in range(J + 1):
                    if j < J:
                        pe.wait_ge(s_tr, g * J + j + 1)
                        for k in range(4):
                            src = (xn_t, ag_t)[k // 2]
                            i = pe.transpose(pt[j % 2][:, k, :], src[:, b, j, (k % 2) * P:(k % 2 + 1) * P],
                                             C["ident"][:, :])
                        i.then_inc(s_pt, 1)
                    if j > 0:
                        pe.wait_ge(s_tr, g * J + j + 2)
                        for k in range(4):
                            w = (C["wr"], C["wl"])[k // 2]
                            i = pe.matmul(px[b][:, j - 1, :], tr_t[:, (j - 1) % 2, k, :], w[:, k % 2, :],
                                          start=(k == 0), stop=(k == 3))
                        i.then_inc(s_mm, 1)
                    if j == 2 and counted is not None:
                        before(counted)

            def before(g):
                pe.wait_ge(s_tot, g + 1)
                pe.matmul(ppre, C["tri"][:, :], cum[:, J, :], start=True, stop=False)
                pe.matmul(ppre, C["ones"][:, :], run[:, :], start=False, stop=True).then_inc(s_pre, 1)

            def logits(g, b):
                pe.wait_ge(s_xl, g + 1)
                pe.wait_ge(s_io, g)
                for h in range(2):
                    pe.wait_ge(s_lt, g * 2 + h + 1)
                    for k in range(4):
                        i = pe.transpose(pl[:, k, :], xl_t[:, b, 2 * h + k // 2, (k % 2) * P:(k % 2 + 1) * P],
                                         C["ident"][:, :])
                    i.then_inc(s_pl, 1)
                    pe.wait_ge(s_lt, g * 2 + h + 2)
                    for k in range(4):
                        i = pe.matmul(pgate[:, 2 * h + k // 2, :], lt_t[:, h, k, :], gate[:, k % 2, :],
                                      start=(k % 2 == 0), stop=(k % 2 == 1))
                i.then_inc(s_gate, 1)

            staggered(update, logits, before, pe)
            pe.wait_ge(s_io, G)
            pe.matmul(ppre, C["ones"][:, :], run[:, :], start=True, stop=True).then_inc(s_pre, 1)

        @block.scalar
        def _(act):
            act.sem_inc(s_tr, 2)
            act.sem_inc(s_lt, 1)

            def update(g, b, u, counted=None):
                for j in range(J):
                    act.wait_ge(s_pt, g * J + j + 1)
                    act.wait_ge(s_mm, g * J + j + 1)
                    act.copy(tr_t[:, j % 2], pt[j % 2][:, :, :]).then_inc(s_tr, 1)

            def logits(g, b):
                for h in range(2):
                    act.wait_ge(s_pl, g * 2 + h + 1)
                    act.copy(lt_t[:, h], pl[:, :, :]).then_inc(s_lt, 1)

            staggered(update, logits, lambda g: None, act)

        @block.vector
        def _(v):
            step = Steps(v, s_init)
            step.then(v.memset(cum[:, :, :], 0.0))
            step.then(v.memset(run[:, :], 0.0))
            v.wait_ge(s_par, 64)
            v.sem_inc(s_x1, 2)

            def update(g, b, u, counted=None):
                if counted is not None:
                    places(counted, b)
                step = Steps(v, st1, g, 4 + 10)
                x1, xl = x1_t[:, b], xl_t[:, b]
                v.wait_ge(s_mm, g * J + J + 2)
                v.wait_ge(outs[b], u * 16)
                step.then(v.tensor_tensor(x1, px[b][:, :, :], x_t[:, b], ALU.add))
                v.tensor_tensor(x1, x1, br[:, :].unsqueeze(1).to_broadcast([P, J, D]), ALU.add).then_inc(s_x1, 1)
                v.wait_ge(s_x1, g + 3)
                step.then(row_mean_var(v, step, tick, x1, stats, mv, ve[:, :]))
                inverse_root(v, step, rs, ve, nt)
                v.wait_ge(sent[b], u * 16 * J)
                for j in range(J):
                    i = v.tensor_scalar(xl[:, j, :], x1[:, j, :], mv[:, j, 0:1], rs[:, j:j + 1],
                                        ALU.subtract, ALU.mult)
                i.then_inc(s_xl, 1)
                step.end()

            wide = [P, J, EXPERTS]
            pos, base, kept, slot, far = (m4[:, n, :] for n in range(5))

            def choose(g, b):
                step = Steps(v, st2, g, 10)
                v.wait_ge(s_gate, g + 1)
                step.then(v.tensor_tensor(lg[:, :, :], pgate, gb[:, :].unsqueeze(1).to_broadcast(wide), ALU.add))
                step.then(v.tensor_reduce(pos, lg[:, :, :], AX.X, ALU.max))
                step.then(v.tensor_tensor(lg[:, :, :], lg[:, :, :], pos.unsqueeze(2).to_broadcast(wide), ALU.subtract))
                v.tensor_copy(C["gap"][:, bass.ds(g * J, J), :], lg[:, :, :])
                step.then(v.scalar_tensor_tensor(rk[:, :, :], lg[:, :, :], 0.0, ev[:, 0, :].unsqueeze(1).to_broadcast(wide),
                                                 ALU.is_equal, ALU.mult))
                step.then(v.tensor_reduce(base, rk[:, :, :], AX.X, ALU.max))
                step.then(v.tensor_tensor(oh[:, :, :], rk[:, :, :], base.unsqueeze(2).to_broadcast(wide), ALU.is_equal))
                step.then(v.tensor_scalar(oh[:, :, :], oh[:, :, :], C["valid"][:, bass.ds(g, 1)], None, ALU.mult))
                for j in range(J - 1):
                    step.then(v.tensor_tensor(cum[:, j + 1, :], cum[:, j, :], oh[:, j, :], ALU.add))
                v.tensor_tensor(cum[:, J, :], cum[:, J - 1, :], oh[:, J - 1, :], ALU.add).then_inc(s_tot, 1)
                step.end()

            def places(g, b):
                step = Steps(v, st3, g, 6)
                v.wait_ge(s_pre, g + 1)
                v.tensor_tensor(run[:, :], run[:, :], cum[:, J, :], ALU.add)
                step.then(v.tensor_tensor(rk[:, :, :], cum[:, 0:J, :], ppre.unsqueeze(1).to_broadcast(wide), ALU.add))
                step.then(v.tensor_tensor(rk[:, :, :], rk[:, :, :], oh[:, :, :], ALU.mult))
                v.tensor_reduce(pos, rk[:, :, :], AX.X, ALU.add)
                step.then(v.tensor_tensor(lg[:, :, :], oh[:, :, :], ev[:, 1, :].unsqueeze(1).to_broadcast(wide), ALU.mult))
                step.then(v.tensor_reduce(base, lg[:, :, :], AX.X, ALU.add))
                step.then(v.tensor_scalar(kept, pos, float(CAP), C["valid"][:, bass.ds(g, 1)], ALU.is_lt, ALU.mult))
                v.tensor_tensor(slot, pos, base, ALU.add)
                v.tensor_copy(cols(C["kept"], g), kept)
                step.then(v.tensor_scalar(far, kept, -FAR, FAR, ALU.mult, ALU.add))
                v.tensor_tensor(cols(C["from"], g), slot, kept, ALU.mult)
                v.tensor_tensor(io[:, b, :], slot, far, ALU.add).then_inc(s_io, 1)
                step.end()

            staggered(update, choose, lambda g: places(g, g % 2), v)
            v.wait_ge(s_pre, G + 1)
            v.tensor_copy(C["tokens"][:, :], ppre)


def two_layers(nc, T, C, name, experts, pairs, tail_block, r, width, source, w1_d, b1_d, w2_d, b2_d, func, store, out_d):
    n_blocks = 2 * pairs + tail_block
    total = experts * n_blocks
    assert total % 2 == 0
    slots_w = min(experts, 2)
    FC = FF // P
    with Stage(nc) as c:
        xe = sb(c, nc, name + "_xe", [r, 2, J, width])
        w1 = sb(c, nc, name + "_w1", [P, slots_w, KC, FF])
        w2 = sb(c, nc, name + "_w2", [P, slots_w, FC, D])
        b1 = sb(c, nc, name + "_b1", [P, slots_w, FC])
        b2 = sb(c, nc, name + "_b2", [P, slots_w, D])
        xt = sb(c, nc, name + "_xt", [P, KC, J * r])
        ht = sb(c, nc, name + "_ht", [P, FC, J * r])
        yt = sb(c, nc, name + "_yt", [r, 2, J, D])
        io = sb(c, nc, name + "_io", [r, 2, J], I32)
        pxt = ps(c, nc, name + "_pxt", [P, KC, 512])
        ph = [ps(c, nc, f"{name}_ph{n}", [P, 512]) for n in range(2)]
        py = [ps(c, nc, f"{name}_py{b}", [P, J, D]) for b in range(2)]
        w_in = [sem(c, nc, f"{name}_w_in{n}") for n in range(slots_w)]
        x_in = [sem(c, nc, f"{name}_x_in{b}") for b in range(2)]
        y_out = [sem(c, nc, f"{name}_y_out{b}") for b in range(2)]
        s_pt = sem(c, nc, name + "_s_pt")
        s_xt = sem(c, nc, name + "_s_xt")
        s_h = sem(c, nc, name + "_s_h")
        s_ht = sem(c, nc, name + "_s_ht")
        s_y = sem(c, nc, name + "_s_y")
        s_yt = sem(c, nc, name + "_s_yt")
        s_go = sem(c, nc, name + "_s_go")
        s_step = sem(c, nc, name + "_step")
        tick = sem(c, nc, name + "_tick")
        block = c.enter_context(nc.Block())
        block_rows = J * r

        def blocks(eng, body):
            if experts == 1:
                with eng.Fori(0, pairs) as i:
                    for s in range(2):
                        body(i * 2 + s, s, i, 0, 0, i * 2 + s)
                return
            with eng.Fori(0, experts // 2) as ep:
                for par in range(2):
                    def at(i, s):
                        k = n_blocks * par + s
                        body(ep * (2 * n_blocks) + i * 2 + k, k % 2, ep * n_blocks + i + k // 2, par, ep, i * 2 + s)
                    with eng.Fori(0, pairs) as i:
                        for s in range(2):
                            at(i, s)
                    if tail_block:
                        at(pairs, 0)

        def source_rows(n):
            return source[bass.ds(n * block_rows, block_rows), :].rearrange("(p j) d -> p j d", j=J)

        def load_weights(eng, e, slot):
            for out, in_ in ((w1[:, slot], w1_d[e].rearrange("(c p) f -> p c f", p=P)),
                             (w2[:, slot], w2_d[e].rearrange("(c p) d -> p c d", p=P)),
                             (b1[:, slot], b1_d[e]), (b2[:, slot], b2_d[e].partition_broadcast(P))):
                eng.dma_start(out, in_).then_inc(w_in[slot], 16)

        @block.sync
        def _(sp):
            sp.dma_start(xe[:, 0], source_rows(0)).then_inc(x_in[0], 16)

            def body(n, b, u, slot, e, w):
                if store:
                    sp.wait_ge(s_pt, n)
                else:
                    sp.wait_ge(s_yt, n + 2)
                o = 1 - b
                sp.dma_start(xe[:, o], source_rows(n + 1)).then_inc(x_in[o], 16)
                if store:
                    sp.wait_ge(s_yt, n + 3)
                    sp.dma_start(out_d[bass.ds(n * block_rows, block_rows), :].rearrange("(p j) d -> p j d", j=J), yt[:, b])\
                        .then_inc(y_out[b], 16)

            blocks(sp, body)
            sp.wait_ge(x_in[0], 16 * (total // 2 + 1))
            if store:
                for b in range(2):
                    sp.wait_ge(y_out[b], 16 * (total // 2))

        @block.gpsimd
        def _(pool):
            for n in range(slots_w):
                load_weights(pool, n, n)
            if experts > 1:
                with pool.Fori(0, experts // 2 - 1) as ep:
                    for par in range(2):
                        done = ep * (2 * n_blocks) + n_blocks * (par + 1)
                        wait_all(pool, tick, (s_y, done), (s_yt, done + 2))
                        e = ep * 2 + par + 2
                        for out, in_ in ((w1[:, par], w1_d[bass.ds(e, 1)].rearrange("o (c p) f -> p (o c) f", p=P)),
                                         (w2[:, par], w2_d[bass.ds(e, 1)].rearrange("o (c p) d -> p (o c) d", p=P)),
                                         (b1[:, par], b1_d[bass.ds(e, 1)].rearrange("o p f -> p (o f)")),
                                         (b2[:, par], b2_d[bass.ds(e, 1)].rearrange("o d -> (o d)").partition_broadcast(P))):
                            pool.dma_start(out, in_).then_inc(w_in[par], 16)
            if not store:
                def body(n, b, u, slot, e, w):
                    wait_all(pool, tick, (s_yt, n + 3))
                    for j in range(J):
                        pool.indirect_dma_start(out_d, bass.IndirectOffsetOnAxis(ap=io[:, b, j:j + 1], axis=0), yt[:, b, j, :],
                                                None, bounds_check=NP - 1, oob_is_err=False).then_inc(y_out[b], 16)

                blocks(pool, body)
                for b in range(2):
                    pool.wait_ge(y_out[b], 16 * J * (total // 2))

        @block.tensor
        def _(pe):
            def turn(b):
                for k in range(KC):
                    for j in range(J):
                        i = pe.transpose(pxt[:, k, j * r:(j + 1) * r], xe[:, b, j, k * P:(k + 1) * P], C["ident"][0:r, 0:r])
                i.then_inc(s_pt, 1)

            def first_layer(n, slot):
                for f in range(FC):
                    pe.wait_ge(s_ht, n * FC + f + 1)
                    for k in range(KC):
                        i = pe.matmul(ph[f % 2][:, 0:J * r], w1[:, slot, k, f * P:(f + 1) * P], xt[:, k, :],
                                      start=(k == 0), stop=(k == KC - 1))
                    i.then_inc(s_h, 1)

            def second_layer(n, b, slot):
                for j in range(J):
                    for f in range(FC):
                        if j == 0:
                            pe.wait_ge(s_ht, n * FC + f + 3)
                        i = pe.matmul(py[b][0:r, j, :], ht[:, f, j * r:(j + 1) * r], w2[:, slot, f, :],
                                      start=(f == 0), stop=(f == FC - 1))
                i.then_inc(s_y, 1)

            pe.wait_ge(x_in[0], 16)
            turn(0)
            pe.wait_ge(s_go, 1)

            def body(n, b, u, slot, e, w):
                wait_all(pe, tick, (s_xt, n + 1), (w_in[slot], e * 64 + 64 if experts > 1 else 64))
                if experts > 1:
                    tokens = pe.value_load(C["tokens"][0:1, bass.ds(e * 2 + slot, 1)], min_val=0, max_val=N)
                    with pe.If(w * block_rows < tokens):
                        first_layer(n, slot)
                    with pe.Else():
                        for f in range(FC):
                            pe.wait_ge(s_ht, n * FC + f + 1)
                            pe.sem_inc(s_h, 1)
                else:
                    first_layer(n, slot)
                pe.wait_ge(x_in[1 - b], (u + b) * 16 + 16)
                turn(1 - b)
                pe.wait_ge(s_yt, n + 1)
                if experts > 1:
                    with pe.If(w * block_rows < tokens):
                        second_layer(n, b, slot)
                    with pe.Else():
                        pe.wait_ge(s_ht, n * FC + FC + 2)
                        pe.sem_inc(s_y, 1)
                else:
                    second_layer(n, b, slot)

            blocks(pe, body)

        @block.scalar
        def _(act):
            act.sem_inc(s_ht, 2)

            def body(n, b, u, slot, e, w):
                act.wait_ge(s_pt, n + 1)
                act.copy(xt[:, :, :], pxt[:, :, 0:J * r]).then_inc(s_xt, 1)
                for f in range(FC):
                    act.wait_ge(s_h, n * FC + f + 1)
                    if f == 0:
                        act.wait_ge(s_y, n)
                    act.activation(ht[:, f, :], ph[f % 2][:, 0:J * r], func, bias=b1[:, slot, f:f + 1]).then_inc(s_ht, 1)

            blocks(act, body)

        @block.vector
        def _(v):
            for t in (*ph, *py):
                i = v.memset(t[:, :] if t in ph else t[:, :, :], 0.0)
            i.then_inc(s_go, 1)
            v.sem_inc(s_yt, 2)

            def body(n, b, u, slot, e, w):
                y = yt[:, b]
                v.wait_ge(s_y, n + 1)
                v.wait_ge(y_out[b], u * 16 * (1 if store else J))
                bias = b2[0:r, slot, :].unsqueeze(1).to_broadcast([r, J, D])
                if store:
                    v.tensor_tensor(y, py[b][0:r, :, :], bias, ALU.add).then_inc(s_yt, 1)
                else:
                    step = Steps(v, s_step, n, 1)
                    step.then(v.tensor_tensor(y, py[b][0:r, :, :], bias, ALU.add))
                    for j in range(J):
                        v.scalar_tensor_tensor(y[:, j, :], y[:, j, :], xe[:, b, j, 2 * D:2 * D + 1], xe[:, b, j, D:2 * D],
                                               ALU.mult, ALU.add)
                    v.tensor_copy(io[:, b, :], xe[:, b, :, 2 * D + 1].bitcast(I32)).then_inc(s_yt, 1)

            blocks(v, body)


def combine_and_project(nc, T, C):
    SC = 2 * GH
    with Stage(nc) as c:
        x1_t = sb(c, nc, "d_x1", [P, 2, J, D])
        yg_t = sb(c, nc, "d_yg", [P, 2, J, D])
        xl_t = sb(c, nc, "d_xl", [P, 2, J, D])
        fin = sb(c, nc, "d_fin", [P, J, D], I32)
        sg = sb(c, nc, "d_sg", [P, J, D])
        neg = sb(c, nc, "d_neg", [P, J, D])
        io = sb(c, nc, "d_io", [P, 2, J], I32)
        tr_t = sb(c, nc, "d_tr", [P, 2, KC, P])
        wh = sb(c, nc, "d_wh", [P, KC, D + SC])
        w1n = sb(c, nc, "d_w1n", [P, KC, D])
        aa = sb(c, nc, "d_aa", [P, KC, SC])
        hp_t = sb(c, nc, "d_hp", [P, 2, J, D])
        sc_t = sb(c, nc, "d_sc", [P, 2, J, SC])
        gap = C["gap"]
        stats = sb(c, nc, "d_stats", [P, J, 6])
        mv = sb(c, nc, "d_mv", [P, J, 2])
        ve = sb(c, nc, "d_ve", [P, J])
        rs = sb(c, nc, "d_rs", [P, J])
        nt = sb(c, nc, "d_nt", [P, J])
        nb = sb(c, nc, "d_nb", [P, J])
        pt = ps(c, nc, "d_pt", [P, KC, P])
        php = [ps(c, nc, f"d_php{n}", [P, 512]) for n in range(2)]
        ins = [sem(c, nc, f"d_ins{b}") for b in range(2)]
        got = [sem(c, nc, f"d_got{b}") for b in range(2)]
        x2o = [sem(c, nc, f"d_x2o{b}") for b in range(2)]
        xno = [sem(c, nc, f"d_xno{b}") for b in range(2)]
        pro = [sem(c, nc, f"d_pro{b}") for b in range(2)]
        s_par = sem(c, nc, "d_par")
        s_init = sem(c, nc, "d_init")
        s_aw = sem(c, nc, "d_s_aw")
        s_wh = sem(c, nc, "d_s_wh")
        s_ex = sem(c, nc, "d_s_ex")
        s_wt = sem(c, nc, "d_s_wt")
        s_io = sem(c, nc, "d_s_io")
        s_z = sem(c, nc, "d_s_z")
        s_x2 = sem(c, nc, "d_s_x2")
        s_rs = sem(c, nc, "d_s_rs")
        s_xl = sem(c, nc, "d_s_xl")
        s_pt = sem(c, nc, "d_s_pt")
        s_tr = sem(c, nc, "d_s_tr")
        s_mm = sem(c, nc, "d_s_mm")
        s_hp = sem(c, nc, "d_s_hp")
        st1 = sem(c, nc, "d_step1")
        st2 = sem(c, nc, "d_step2")
        tick = sem(c, nc, "d_tick")
        block = c.enter_context(nc.Block())
        n_par = 3

        @block.sync
        def _(sp):
            for out, in_ in ((wh[:, :, 0:D], T["W1_t"].rearrange("(c p) n -> p c n", p=P)),
                             (w1n[:, :, :], T["W1"].rearrange("(c p) n -> p c n", p=P)),
                             (aa[:, :, :], T["a1"].rearrange("(c p) n -> p c n", p=P))):
                sp.dma_start(out, in_).then_inc(s_par, 16)

            def load(g, b, u):
                wait_all(sp, tick, (x2o[b], u * 16))
                sp.wait_ge(s_xl, g + 1)
                sp.dma_start(x1_t[:, b], rows(T["x1"], g)).then_inc(ins[b], 16)

            def store_x2(g, b):
                sp.wait_ge(s_x2, g + 3)
                sp.dma_start(rows(T["x2"], g), x1_t[:, b]).then_inc(x2o[b], 16)

            def store(g, b, u, used):
                sp.wait_ge(s_xl, g + 3)
                sp.dma_start(rows(T["xn"], g), xl_t[:, b]).then_inc(xno[b], 16)
                if used == P:
                    store_x2(g + 1, 1 - b)
                sp.wait_ge(s_hp, g * J + J + 2)
                sp.dma_start(rows(T["hp"], g), hp_t[:, b]).then_inc(pro[b], 16)
                sp.dma_start(rows(T["sc1"], g), sc_t[:, b]).then_inc(pro[b], 16)

            ahead(sp, load, store, lambda: store_x2(0, 0))
            for b in range(2):
                sp.wait_ge(x2o[b], 16 * (G // 2))
                sp.wait_ge(xno[b], 16 * (G // 2))
                sp.wait_ge(pro[b], 32 * (G // 2))

        @block.gpsimd
        def _(pool):
            def gather(g, b, u):
                wait_all(pool, tick, (s_io, g + 1), (s_x2, g + 1))
                for j in range(J):
                    pool.indirect_dma_start(yg_t[:, b, j, :], None, T["y"], bass.IndirectOffsetOnAxis(ap=io[:, b, j:j + 1], axis=0),
                                            bounds_check=EXPERTS * MROWS - 1, oob_is_err=False).then_inc(got[b], 16)

            ahead(pool, gather, lambda *a: None)

        @block.tensor
        def _(pe):
            pe.wait_ge(s_par, 16 * n_par)
            for k in range(KC):
                for n in range(KC):
                    i = pe.matmul(php[k][:, 0:SC], w1n[:, n, k * P:(k + 1) * P], aa[:, n, :], start=(n == 0), stop=(n == KC - 1))
            i.then_inc(s_aw, 1)
            pe.wait_ge(s_wh, 1)
            pe.sem_inc(s_mm, 2)

            def turn(i, g, b, j):
                if j == 0:
                    pe.wait_ge(s_xl, g + 3)
                pe.wait_ge(s_tr, i + 1)
                for k in range(KC):
                    o = pe.transpose(pt[:, k, :], xl_t[:, b, j, k * P:(k + 1) * P], C["ident"][:, :])
                o.then_inc(s_pt, 1)

            turn(0, 0, 0, 0)

            def project(g, b, u, used):
                for j in range(J):
                    i, s = g * J + j, j % 2
                    if j < J - 1:
                        turn(i + 1, g, b, j + 1)
                    pe.wait_ge(s_tr, i + 2)
                    pe.wait_ge(s_hp, i + 1)
                    for k in range(KC):
                        o = pe.matmul(php[s][:, 0:D + SC], tr_t[:, s, k, :], wh[:, k, :], start=(k == 0), stop=(k == KC - 1))
                    o.then_inc(s_mm, 1)
                    if j == J - 1 and used == P:
                        turn(i + 1, g + 1, 1 - b, 0)

            ahead(pe, lambda *a: None, project)

        @block.scalar
        def _(act):
            act.activation(gap[:, :, :], gap[:, :, :], ACT.Exp).then_inc(s_ex, 1)
            act.sem_inc(s_tr, 1)
            act.sem_inc(s_hp, 2)
            act.sem_inc(s_xl, 2)

            def first(g, b, u):
                act.wait_ge(got[b], u * 16 * J)
                act.copy(io[:, b, :], cols(C["from"], g)).then_inc(s_io, 1)

            def scale(g, b, u):
                act.wait_ge(got[b], u * 16 * J + 16 * J)
                for j in range(J):
                    o = act.mul(yg_t[:, b, j], yg_t[:, b, j], C["w"][:, bass.ds(g * J + j, 1)])
                o.then_inc(s_z, 1)

            def norm(g, b, u):
                act.wait_ge(xno[b], u * 16)
                act.wait_ge(s_rs, g + 1)
                for j in range(J):
                    o = act.activation(xl_t[:, b, j], x1_t[:, b, j], ACT.Identity, bias=nb[:, j:j + 1], scale=rs[:, j:j + 1])
                o.then_inc(s_xl, 1)

            def turned(i, s):
                act.wait_ge(s_pt, i + 1)
                act.wait_ge(s_mm, i + 1)
                act.copy(tr_t[:, s], pt[:, :, :]).then_inc(s_tr, 1)

            def begin():
                act.wait_ge(s_wt, 1)
                scale(0, 0, 0)
                scale(1, 1, 0)
                norm(0, 0, 0)
                turned(0, 0)

            def project(g, b, u, used, more=False):
                act.wait_ge(pro[b], u * 32)
                for j in range(J):
                    i, s = g * J + j, j % 2
                    if j < J - 1:
                        turned(i + 1, 1 - s)
                    act.wait_ge(s_mm, i + 3)
                    act.copy(hp_t[:, b, j], php[s][:, 0:D])
                    act.copy(sc_t[:, b, j], php[s][:, D:D + SC]).then_inc(s_hp, 1)
                if more:
                    scale(g + 2, b, u + 1)
                if used == P:
                    norm(g + 1, 1 - b, u + b)
                    turned(g * J + J, 0)

            ahead(act, first, lambda g, b, u, used: project(g, b, u, used, True), begin, project)

        @block.vector
        def _(v):
            step = Steps(v, s_init)
            v.wait_ge(s_aw, 1)
            for k in range(KC):
                i = v.tensor_copy(wh[:, k, D:D + SC], php[k][:, 0:SC])
            i.then_inc(s_wh, 1)
            v.wait_ge(s_ex, 1)
            step.then(v.tensor_reduce(C["w"][:, :], gap[:, :, :], AX.X, ALU.add))
            step.then(v.reciprocal(C["w"][:, :], C["w"][:, :]))
            v.tensor_tensor(C["w"][:, :], C["w"][:, :], C["kept"][:, :], ALU.mult).then_inc(s_wt, 1)
            v.sem_inc(s_x2, 2)

            def update(g, b, u):
                step = Steps(v, st1, g, 3)
                x, y = x1_t[:, b], yg_t[:, b]
                v.wait_ge(s_z, g + 1)
                v.tensor_scalar(neg[:, :, :], y, 0.0, -1.0e4, ALU.is_lt, ALU.mult)
                v.tensor_scalar(sg[:, :, :], y, 0.0, 1.0e4, ALU.is_gt, ALU.mult)
                step.then(v.tensor_scalar(fin[:, :, :], y, 0.0, 0.0, ALU.mult, ALU.is_equal))
                step.then(v.tensor_tensor(sg[:, :, :], sg[:, :, :], neg[:, :, :], ALU.add), tick)
                step.then(v.copy_predicated(sg[:, :, :], fin[:, :, :], y))
                v.wait_ge(ins[b], u * 16 + 16)
                v.tensor_tensor(x, x, sg[:, :, :], ALU.add).then_inc(s_x2, 1)
                step.end()

            def scales(g, b, u):
                step = Steps(v, st2, g, 2 + 1 + 1 + 9)
                v.wait_ge(s_x2, g + 3)
                v.wait_ge(s_xl, g + 2)
                step.then(row_mean_var(v, step, tick, x1_t[:, b], stats, mv, ve[:, :]))
                inverse_root(v, step, rs, ve, nt)
                v.scalar_tensor_tensor(nb[:, :], mv[:, :, 0], -1.0, rs[:, :], ALU.mult, ALU.mult).then_inc(s_rs, 1)
                step.end()

            with v.Fori(0, G // 2) as u:
                for b in range(2):
                    update(u * 2 + b, b, u)
                    scales(u * 2 + b, b, u)


def second_features(nc, T, C):
    SC = 2
    with Stage(nc) as c:
        ag_t = sb(c, nc, "f_ag", [P, 2, J, D])
        tr_t = sb(c, nc, "f_tr", [P, 2, KC, P])
        wh = sb(c, nc, "f_wh", [P, KC, D + SC])
        wn = sb(c, nc, "f_wn", [P, KC, D])
        aa = sb(c, nc, "f_aa", [P, KC, SC])
        hp_t = sb(c, nc, "f_hp", [P, 2, J, D])
        sc_t = sb(c, nc, "f_sc", [P, 2, J, SC])
        pt = [ps(c, nc, f"f_pt{n}", [P, KC, P]) for n in range(2)]
        php = [ps(c, nc, f"f_php{n}", [P, 512]) for n in range(2)]
        ins = [sem(c, nc, f"f_ins{b}") for b in range(2)]
        outs = [sem(c, nc, f"f_outs{b}") for b in range(2)]
        s_par = sem(c, nc, "f_par")
        s_aw = sem(c, nc, "f_s_aw")
        s_wh = sem(c, nc, "f_s_wh")
        s_pt = sem(c, nc, "f_s_pt")
        s_tr = sem(c, nc, "f_s_tr")
        s_mm = sem(c, nc, "f_s_mm")
        s_hp = sem(c, nc, "f_s_hp")
        tick = sem(c, nc, "f_tick")
        block = c.enter_context(nc.Block())

        def groups(eng, body):
            with eng.Fori(0, G // 2) as u:
                for b in range(2):
                    body(u * 2 + b, b, u)

        @block.sync
        def _(sp):
            for out, in_ in ((wh[:, :, 0:D], T["W2_t"].rearrange("(c p) n -> p c n", p=P)),
                             (wn[:, :, :], T["W2"].rearrange("(c p) n -> p c n", p=P)),
                             (aa[:, :, :], T["a2"].rearrange("(c p) n -> p c n", p=P))):
                sp.dma_start(out, in_).then_inc(s_par, 16)

            def load(g, b, u):
                sp.wait_ge(s_hp, g * J + 1)
                sp.dma_start(ag_t[:, b], rows(T["agg"], g)).then_inc(ins[b], 16)

            def save(g, b, u):
                sp.wait_ge(s_hp, g * J + 3 * J)
                sp.dma_start(rows(T["hp"], g), hp_t[:, b]).then_inc(outs[b], 16)
                sp.dma_start(rows(T["sc2"], g), sc_t[:, b]).then_inc(outs[b], 16)

            load(0, 0, 0)
            load(1, 1, 0)
            with sp.Fori(0, G // 2 - 1) as u:
                for b in range(2):
                    save(u * 2 + b, b, u)
                    load(u * 2 + b + 2, b, u + 1)
            for b in range(2):
                save(G - 2 + b, b, G // 2 - 1)
            for b in range(2):
                sp.wait_ge(outs[b], 32 * (G // 2))

        @block.tensor
        def _(pe):
            pe.wait_ge(s_par, 48)
            for k in range(KC):
                for n in range(KC):
                    i = pe.matmul(php[k][:, 0:SC], wn[:, n, k * P:(k + 1) * P], aa[:, n, :], start=(n == 0), stop=(n == KC - 1))
            i.then_inc(s_aw, 1)
            pe.wait_ge(s_wh, 1)

            def body(g, b, u):
                pe.wait_ge(ins[b], u * 16 + 16)
                for j in range(J + 1):
                    i = g * J + j
                    if j < J:
                        pe.wait_ge(s_tr, i + 1)
                        for k in range(KC):
                            o = pe.transpose(pt[j % 2][:, k, :], ag_t[:, b, j, k * P:(k + 1) * P], C["ident"][:, :])
                        o.then_inc(s_pt, 1)
                    if j > 0:
                        s = (j - 1) % 2
                        pe.wait_ge(s_tr, i + 2)
                        pe.wait_ge(s_hp, i - 1 + 7)
                        for k in range(KC):
                            o = pe.matmul(php[s][:, 0:D + SC], tr_t[:, s, k, :], wh[:, k, :], start=(k == 0), stop=(k == KC - 1))
                        o.then_inc(s_mm, 1)

            groups(pe, body)

        @block.scalar
        def _(act):
            act.sem_inc(s_tr, 2)

            def body(g, b, u):
                for j in range(J):
                    i = g * J + j
                    act.wait_ge(s_pt, i + 1)
                    act.wait_ge(s_mm, i + 1)
                    act.activation(tr_t[:, j % 2], pt[j % 2][:, :, :], ACT.Relu).then_inc(s_tr, 1)

            groups(act, body)

        @block.vector
        def _(v):
            v.wait_ge(s_aw, 1)
            for k in range(KC):
                i = v.tensor_copy(wh[:, k, D:D + SC], php[k][:, 0:SC])
            i.then_inc(s_wh, 1)
            v.sem_inc(s_mm, 2)
            v.sem_inc(s_hp, 2 * J)

            def body(g, b, u):
                v.wait_ge(outs[b], u * 32)
                for j in range(J):
                    i = g * J + j
                    v.wait_ge(s_mm, i + 3)
                    v.tensor_copy(hp_t[:, b, j], php[j % 2][:, 0:D])
                    v.tensor_copy(sc_t[:, b, j], php[j % 2][:, D:D + SC]).then_inc(s_hp, 1)

            groups(v, body)


def second_update(nc, T, C):
    HW = P + HEADS // KC
    with Stage(nc) as c:
        x2_t = sb(c, nc, "g_x2", [P, 2, J, D])
        ag_t = sb(c, nc, "g_ag", [P, 2, J, D])
        q_t = sb(c, nc, "g_q", [P, 2, J, D])
        row_t = sb(c, nc, "g_row", [P, 2, J, SW])
        tr_t = sb(c, nc, "g_tr", [P, 2, KC, P])
        o_t = sb(c, nc, "g_o", [P, 2, D])
        ot_t = sb(c, nc, "g_ot", [P, 2, KC, P])
        rc = sb(c, nc, "g_rc", [P, 2, HEADS])
        wo = sb(c, nc, "g_wo", [P, KC, D])
        bo = sb(c, nc, "g_bo", [P, D])
        wr = sb(c, nc, "g_wr", [P, D])
        br = sb(c, nc, "g_br", [P, 1])
        kvh = sb(c, nc, "g_kvh", [P, KC, HW])
        junk = sb(c, nc, "g_junk", [P, J, D])
        stats = sb(c, nc, "g_stats", [P, J, 6])
        mv = sb(c, nc, "g_mv", [P, J, 2])
        ve = sb(c, nc, "g_ve", [P, J])
        nt = sb(c, nc, "g_nt", [P, J])
        rs = sb(c, nc, "g_rs", [P, J])
        wt = sb(c, nc, "g_wt", [P, J])
        pt = [ps(c, nc, f"g_pt{n}", [P, KC, P]) for n in range(2)]
        pq = [ps(c, nc, f"g_pq{n}", [P, 512]) for n in range(2)]
        pot = ps(c, nc, "g_pot", [P, KC, P])
        po = ps(c, nc, "g_po", [P, J, D])
        ins = [sem(c, nc, f"g_ins{b}") for b in range(2)]
        q_in = [sem(c, nc, f"g_q_in{b}") for b in range(2)]
        outs = [sem(c, nc, f"g_outs{b}") for b in range(2)]
        names = ("par", "init", "kv", "pt", "tr", "mq", "o", "pot", "ot", "mo", "x3", "row", "st1", "st2")
        S = {n: sem(c, nc, "g_s_" + n) for n in names}
        tick = sem(c, nc, "g_tick")
        block = c.enter_context(nc.Block())

        @block.sync
        def _(sp):
            for out, in_ in ((wo[:, :, :], T["wo"].rearrange("(c p) n -> p c n", p=P)),
                             (bo[:, :], T["bo"].partition_broadcast(P)),
                             (wr[:, :], T["ffn_wr"].rearrange("d o -> (d o)").partition_broadcast(P)),
                             (br[:, :], T["ffn_br"].partition_broadcast(P))):
                sp.dma_start(out, in_).then_inc(S["par"], 16)

            def load_q(g, b, u):
                sp.wait_ge(S["pt"], g * J + J - 1)
                sp.dma_start(q_t[:, b], rows(T["pq"], g)).then_inc(q_in[b], 16)

            def load(g, b):
                for t, name in ((x2_t, "x2"), (ag_t, "agg")):
                    sp.dma_start(t[:, b], rows(T[name], g)).then_inc(ins[b], 16)

            def store(g, b, u, used):
                sp.wait_ge(S["row"], g + 1)
                sp.dma_start(rows(T["sel"], g), row_t[:, b]).then_inc(outs[b], 16)
                sp.dma_start(rows(T["out"], g), row_t[:, b, :, D:2 * D]).then_inc(outs[b], 16)

            def next_group(g, b, u, used):
                store(g, b, u, used)
                load(g + 2, b)

            def begin():
                load(0, 0)
                load(1, 1)

            ahead(sp, load_q, next_group, begin, store)
            for b in range(2):
                sp.wait_ge(outs[b], 32 * (G // 2))

        @block.tensor
        def _(pe):
            pe.wait_ge(S["par"], 64)
            pe.wait_ge(S["kv"], 1)
            pe.sem_inc(S["pot"], 2)
            pe.sem_inc(S["pt"], 2 * J - 1)

            def first(g, b, u):
                pe.wait_ge(q_in[b], u * 16 + 16)
                for j in range(J + 2):
                    i = g * J + j
                    if j < J:
                        pe.wait_ge(S["tr"], i + 1)
                        for k in range(KC):
                            o = pe.transpose(pt[j % 2][:, k, :], q_t[:, b, j, k * P:(k + 1) * P], C["ident"][:, :])
                        o.then_inc(S["pt"], 1)
                    if 0 < j <= J:
                        s = (j - 1) % 2
                        pe.wait_ge(S["tr"], i + 2)
                        pe.wait_ge(S["o"], i)
                        for k in range(KC):
                            o = pe.matmul(pq[s][:, k * HW:(k + 1) * HW], tr_t[:, s, k, :], kvh[:, k, :], start=True, stop=True)
                        o.then_inc(S["mq"], 1)
                    if j > 1:
                        s = j % 2
                        pe.wait_ge(S["o"], i + 1)
                        pe.wait_ge(S["ot"], i - 2)
                        for k in range(KC):
                            o = pe.transpose(pot[:, k, :], o_t[:, s, k * P:(k + 1) * P], C["ident"][:, :])
                        o.then_inc(S["pot"], 1)
                        pe.wait_ge(S["ot"], i - 1)
                        if j == 2:
                            pe.wait_ge(S["x3"], g + 2)
                        for k in range(KC):
                            o = pe.matmul(po[:, j - 2, :], ot_t[:, s, k, :], wo[:, k, :], start=(k == 0), stop=(k == KC - 1))
                        o.then_inc(S["mo"], 1)

            piped(pe, first, lambda *a: None)

        @block.scalar
        def _(act):
            act.sem_inc(S["tr"], 2)

            def first(g, b, u):
                for j in range(J + 2):
                    i = g * J + j
                    if j < J:
                        act.wait_ge(S["pt"], i + 2 * J)
                        act.wait_ge(S["mq"], i + 1)
                        act.copy(tr_t[:, j % 2], pt[j % 2][:, :, :]).then_inc(S["tr"], 1)
                    if j > 1:
                        act.wait_ge(S["pot"], i + 1)
                        act.copy(ot_t[:, j % 2], pot[:, :, :]).then_inc(S["ot"], 1)

            piped(act, first, lambda *a: None)

        @block.vector
        def _(v):
            step = Steps(v, S["init"])
            for k in range(KC):
                i = v.tensor_tensor(kvh[:, k, 0:P], C["kv"][:, k, 0:P], C["heads"][:, :], ALU.mult)
            i = v.tensor_scalar(kvh[:, :, P:HW], C["heads"][:, 0:P:HC].unsqueeze(1).to_broadcast([P, KC, HEADS // KC]), 1.0, None,
                                ALU.mult)
            step.then(i)
            for k in range(KC):
                i = v.tensor_scalar(kvh[:, k, P:HW], kvh[:, k, P:HW], C["kv"][:, k, P:P + 1], None, ALU.mult)
            i.then_inc(S["kv"], 1)
            v.wait_ge(S["par"], 64)
            v.sem_inc(S["mq"], 2)
            v.sem_inc(S["o"], 2)
            v.sem_inc(S["x3"], 2)

            def attend(i, j):
                step = Steps(v, S["st1"], i, 2)
                s, n = j % 2, HEADS // KC
                v.wait_ge(S["mq"], i + 3)
                sums = pq[s][:, 0:KC * HW].rearrange("p (k n) -> p k n", k=KC)
                step.then(v.tensor_scalar(rc[:, s, :].rearrange("p (k h) -> p k h", k=KC), sums[:, :, P:HW], 1e-6, None, ALU.add))
                step.then(v.reciprocal(rc[:, s, :], rc[:, s, :]))
                v.wait_ge(S["pot"], i + 1)
                for k in range(KC):
                    o = v.tensor_tensor(o_t[:, s, k * P:(k + 1) * P].rearrange("p (h e) -> p h e", h=n),
                                        sums[:, k, 0:P].rearrange("p (h e) -> p h e", h=n),
                                        rc[:, s, k * n:(k + 1) * n].unsqueeze(2).to_broadcast([P, n, HC]), ALU.mult)
                o.then_inc(S["o"], 1)
                step.end()

            def update(g, b, u, used):
                step = Steps(v, S["st2"], g, 2 + 3 + 10 + 3)
                x, row = x2_t[:, b], row_t[:, b]

                def next_tile(j):
                    if used == P:
                        attend(g * J + J + j, j)

                v.wait_ge(ins[b], u * 32 + 32)
                v.wait_ge(S["mo"], g * J + J)
                step.then(v.tensor_tensor(x, x, po[:, :, :], ALU.add))
                v.tensor_tensor(x, x, bo[:, :].unsqueeze(1).to_broadcast([P, J, D]), ALU.add).then_inc(S["x3"], 1)
                next_tile(0)
                v.wait_ge(S["x3"], g + 3)
                step.then(v.tensor_tensor(x, x, ag_t[:, b], ALU.add))
                next_tile(1)
                step.then(row_mean_var(v, step, tick, x, stats, mv, ve[:, :]))
                next_tile(2)
                inverse_root(v, step, rs, ve, nt)
                v.wait_ge(outs[b], u * 32)
                for j in range(J):
                    i = v.tensor_scalar(row[:, j, 0:D], x[:, j, :], mv[:, j, 0:1], rs[:, j:j + 1], ALU.subtract, ALU.mult)
                step.then(i)
                next_tile(3)
                v.tensor_tensor(row[:, :, D:2 * D], x, row[:, :, 0:D], ALU.add)
                for j in range(J):
                    i = v.scalar_tensor_tensor(junk[:, j, :], row[:, j, 0:D], 1.0, wr[:, :], ALU.mult, ALU.mult, accum_out=wt[:, j:j + 1])
                step.then(i)
                step.then(v.tensor_scalar(wt[:, :], wt[:, :], br[:, 0:1], None, ALU.add))
                v.tensor_copy(cols(C["wsel"], g), wt[:, :])
                v.tensor_copy(row[:, :, 2 * D + 1].bitcast(I32), cols(C["ids"], g))
                v.tensor_copy(row[:, :, 2 * D], wt[:, :]).then_inc(S["row"], 1)
                step.end()

            def begin():
                for j in range(J):
                    attend(j, j)

            ahead(v, lambda *a: None, update, begin)


def select_rows(nc, T, C):
    COLS = NP // P
    with Stage(nc) as c:
        u_t = sb(c, nc, "s_u", [P, COLS])
        junk = sb(c, nc, "s_junk", [P, COLS])
        eq = sb(c, nc, "s_eq", [P, COLS])
        pre = sb(c, nc, "s_pre", [P, COLS])
        sel = sb(c, nc, "s_sel", [P, COLS])
        egs = sb(c, nc, "s_egs", [P, G])
        tot = sb(c, nc, "s_tot", [P, G])
        one = sb(c, nc, "s_one", [P, COLS])
        cnt = sb(c, nc, "s_cnt", [P, 1])
        sg = sb(c, nc, "s_sg", [P, 1])
        want = sb(c, nc, "s_want", [P, 1])
        bit = sb(c, nc, "s_bit", [P, 2])
        thr = sb(c, nc, "s_thr", [P, 1], I32)
        cand = sb(c, nc, "s_cand", [P, 1], I32)
        add = sb(c, nc, "s_add", [P, 1], I32)
        rows_t = sb(c, nc, "s_rows", [P, 2, J, SW])
        io = sb(c, nc, "s_io", [P, 2, J], I32)
        pad = sb(c, nc, "s_pad", [P, SW])
        pc = ps(c, nc, "s_pc", [P, 512])
        pp = ps(c, nc, "s_pp", [P, 512])
        names = ("init", "cnt", "tot", "loop", "go", "io", "step", "pad", "padded")
        S = {n: sem(c, nc, "s_s_" + n) for n in names}
        r_in = [sem(c, nc, f"s_r_in{b}") for b in range(2)]
        sent = [sem(c, nc, f"s_sent{b}") for b in range(2)]
        tick = sem(c, nc, "s_tick")
        block = c.enter_context(nc.Block())
        BITS = 31
        last = SB * GROUP + GROUP

        @block.sync
        def _(sp):
            sp.wait_ge(S["pad"], 1)
            for n, a in enumerate(range(SEL, last, P)):
                k = min(P, last - a)
                sp.dma_start(T["packed"][a:a + k, :], pad[0:k, :]).then_inc(S["padded"], 16)
            sp.wait_ge(S["padded"], 16 * (n + 1))
            with sp.Fori(0, G // 2) as u:
                for b in range(2):
                    sp.wait_ge(sent[b], u * (16 * J))
                    sp.dma_start(rows_t[:, b], rows(T["sel"], u * 2 + b)).then_inc(r_in[b], 16)

        @block.gpsimd
        def _(pool):
            with pool.Fori(0, G // 2) as u:
                for b in range(2):
                    wait_all(pool, tick, (S["io"], u * 2 + b + 1), (r_in[b], u * 16 + 16))
                    for j in range(J):
                        pool.indirect_dma_start(T["packed"], bass.IndirectOffsetOnAxis(ap=io[:, b, j:j + 1], axis=0), rows_t[:, b, j, :],
                                                None, bounds_check=SEL - 1, oob_is_err=False).then_inc(sent[b], 16)
            for b in range(2):
                pool.wait_ge(sent[b], 16 * J * (G // 2))

        @block.tensor
        def _(pe):
            with pe.Fori(0, BITS + 2) as n:
                pe.wait_ge(S["cnt"], n + 1)
                pe.matmul(pc[:, 0:1], C["ones"][:, :], cnt[:, :], start=True, stop=True).then_inc(S["tot"], 1)
            pe.wait_ge(S["cnt"], BITS + 3)
            pe.matmul(pp[:, 0:G], C["tri"][:, :], egs[:, :], start=True, stop=True)
            pe.matmul(pp[:, 256:256 + G], C["ones"][:, :], egs[:, :], start=True, stop=True).then_inc(S["tot"], 1)
            pe.wait_ge(S["cnt"], BITS + 4)
            pe.matmul(pc[:, 0:1], C["tri"][:, :], cnt[:, :], start=True, stop=True).then_inc(S["tot"], 1)

        @block.scalar
        def _(act):
            act.wait_ge(S["go"], 1)
            with act.Fori(0, G // 2) as u:
                for b in range(2):
                    act.wait_ge(sent[b], u * (16 * J))
                    act.copy(io[:, b, :], cols(pre, u * 2 + b)).then_inc(S["io"], 1)

        @block.vector
        def _(v):
            step = Steps(v, S["step"])
            valid = C["valid_cols"]
            w = C["wsel"]
            step.then(v.memset(pad[:, :], 0.0))
            step.then(v.memset(cnt[:, :], FAR))
            v.tensor_copy(pad[:, 2 * D + 1:2 * D + 2].bitcast(I32), cnt[:, :]).then_inc(S["pad"], 1)
            v.memset(one[:, :], 1.0)
            step.then(v.tensor_scalar(junk[:, :], w[:, :], 0.0, None, ALU.is_ge))
            step.then(v.tensor_tensor(junk[:, :], junk[:, :], valid[:, :], ALU.mult))
            v.tensor_reduce(cnt[:, :], junk[:, :], AX.X, ALU.add).then_inc(S["cnt"], 1)
            v.wait_ge(S["tot"], 1)
            step.then(v.tensor_scalar(sg[:, :], pc[:, 0:1], float(SEL), None, ALU.is_ge))
            step.then(v.tensor_scalar(want[:, :], sg[:, :], float(SEL - (N - SEL + 1)), float(N - SEL + 1), ALU.mult, ALU.add))
            step.then(v.tensor_scalar(sg[:, :], sg[:, :], 2.0, -1.0, ALU.mult, ALU.add))
            step.then(v.tensor_scalar(u_t[:, :], w[:, :], sg[:, 0:1], None, ALU.mult))
            step.then(v.tensor_tensor(u_t[:, :], u_t[:, :], valid[:, :], ALU.mult))
            step.then(v.tensor_scalar(junk[:, :], valid[:, :], 1.0, 3.0e38, ALU.subtract, ALU.mult))
            step.then(v.tensor_tensor(u_t[:, :], u_t[:, :], junk[:, :], ALU.add))
            step.then(v.memset(thr[:, :], 0))
            step.then(v.memset(bit[:, 0:1], float(1 << 30)))
            per = 6
            with v.Fori(0, BITS) as n:
                turn = Steps(v, S["loop"], n, per)
                turn.then(v.tensor_copy(add[:, :], bit[:, 0:1]))
                turn.then(v.tensor_tensor(cand[:, :], thr[:, :], add[:, :], ALU.bitwise_or))
                turn.then(v.tensor_scalar(junk[:, :], u_t[:, :], cand[:, 0:1].bitcast(F32), None, ALU.is_ge))
                v.tensor_reduce(cnt[:, :], junk[:, :], AX.X, ALU.add).then_inc(S["cnt"], 1)
                v.wait_ge(S["tot"], n + 2)
                turn.then(v.tensor_scalar(bit[:, 1:2], pc[:, 0:1], want[:, 0:1], bit[:, 0:1], ALU.is_ge, ALU.mult))
                turn.then(v.tensor_copy(add[:, :], bit[:, 1:2]))
                v.tensor_scalar(bit[:, 0:1], bit[:, 0:1], 0.5, None, ALU.mult)
                turn.then(v.tensor_tensor(thr[:, :], thr[:, :], add[:, :], ALU.bitwise_or))
                turn.end()
            step.then(v.tensor_tensor(bit[:, 0:1], thr[:, :].bitcast(F32), sg[:, :], ALU.mult))
            step.then(v.tensor_scalar(sel[:, :], w[:, :], bit[:, 0:1], None, ALU.is_gt))
            step.then(v.tensor_tensor(sel[:, :], sel[:, :], valid[:, :], ALU.mult))
            v.tensor_reduce(cnt[:, :], sel[:, :], AX.X, ALU.add).then_inc(S["cnt"], 1)
            step.then(v.tensor_scalar(eq[:, :], w[:, :], bit[:, 0:1], None, ALU.is_equal))
            step.then(v.tensor_tensor(eq[:, :], eq[:, :], valid[:, :], ALU.mult))
            v.wait_ge(S["tot"], BITS + 2)
            step.then(v.tensor_scalar(want[:, :], pc[:, 0:1], -1.0, float(SEL), ALU.mult, ALU.add))
            v.tensor_reduce(egs[:, :], eq[:, :].rearrange("p (g j) -> p g j", j=J), AX.X, ALU.add).then_inc(S["cnt"], 1)
            v.wait_ge(S["tot"], BITS + 3)
            step.then(v.tensor_copy(tot[:, :], pp[:, 256:256 + G]))
            step.then(v.tensor_tensor_scan(egs[:, :], one[:, 0:G], tot[:, :], 0.0, ALU.mult, ALU.add))
            step.then(v.tensor_tensor(egs[:, :], egs[:, :], tot[:, :], ALU.subtract))
            step.then(v.tensor_tensor(egs[:, :], egs[:, :], pp[:, 0:G], ALU.add))
            p4, e4 = pre[:, :].rearrange("p (g j) -> p g j", j=J), eq[:, :].rearrange("p (g j) -> p g j", j=J)
            step.then(v.tensor_copy(p4[:, :, 0], egs[:, :]))
            for j in range(1, J):
                step.then(v.tensor_tensor(p4[:, :, j], p4[:, :, j - 1], e4[:, :, j - 1], ALU.add))
            step.then(v.scalar_tensor_tensor(pre[:, :], pre[:, :], want[:, 0:1], eq[:, :], ALU.is_lt, ALU.mult))
            step.then(v.tensor_tensor(sel[:, :], sel[:, :], pre[:, :], ALU.add))
            v.tensor_reduce(cnt[:, :], sel[:, :], AX.X, ALU.add).then_inc(S["cnt"], 1)
            step.then(v.tensor_tensor_scan(pre[:, :], one[:, :], sel[:, :], 0.0, ALU.mult, ALU.add))
            v.wait_ge(S["tot"], BITS + 4)
            step.then(v.tensor_scalar(pre[:, :], pre[:, :], pc[:, 0:1], -1.0, ALU.add, ALU.add))
            step.then(v.tensor_scalar(junk[:, :], sel[:, :], -FAR, FAR, ALU.mult, ALU.add))
            v.tensor_tensor(pre[:, :], pre[:, :], junk[:, :], ALU.add).then_inc(S["go"], 1)


def build(nc, T):
    def scratch(name, shape):
        T[name] = nc.dram_tensor("t_" + name, shape, F32).ap()

    for name in ("xn", "agg", "x1", "x2", "hp", "pq"):
        scratch(name, (NP, D))
    scratch("slots", ((EXPERTS * MB + 1) * MT * J, D))
    scratch("y", (EXPERTS * MROWS, D))
    scratch("sc1", (NP, 2 * GH))
    scratch("sc2", (NP, 2))
    scratch("sel", (NP, SW))
    scratch("packed", ((SB + 1) * GROUP, SW))
    scratch("w_edges", (GH, EP))
    scratch("ends", (2 * GH, P))
    scratch("starts", (GH, P + 1))
    with ExitStack() as c:
        C = {}
        for name, shape, dt in (
            ("ident", [P, P], F32), ("tri", [P, P], F32), ("ones", [P, P], F32), ("heads", [P, P], F32),
            ("valid", [P, G], F32), ("valid_cols", [P, NP // P], F32), ("ids", [P, NP // P], I32),
            ("wl", [P, KC, D], F32), ("wr", [P, KC, D], F32), ("kv", [P, KC, P + 1], F32),
            ("src_i", [P, ET + EU], I32), ("out_i", [P, ET], I32), ("dst_f", [P, ET], F32), ("carry_f", [P, ET], F32),
            ("lane_i", [P, ET + EU, 2], I32), ("same_prev", [P, ET], F32), ("same_next", [P, ET], F32),
            ("cut_prev", [P, ET], F32), ("cut_next", [P, ET], F32), ("all_prev", [P, 1], F32), ("all_next", [P, 1], F32),
            ("cut_whole", [P, 1], F32), ("gap", [P, NP // P, EXPERTS], F32), ("kept", [P, NP // P], F32),
            ("from", [P, NP // P], F32), ("w", [P, NP // P], F32), ("wsel", [P, NP // P], F32),
            ("tokens", [P, EXPERTS], I32), ("edge_w", [P, ET, GH], F32), ("edge_w1", [P, ET, 1], F32),
        ):
            C[name] = sb(c, nc, "k_" + name, shape, dt)
        stages = (
            lambda: load_constants(nc, T, C),
            lambda: norm_and_gram(nc, T, C),
            lambda: mean_weights(nc, T, C, C["edge_w1"]),
            lambda: aggregate(nc, T, C, "e0", T["xn"], 1, C["edge_w1"]),
            lambda: update_and_gate(nc, T, C),
            lambda: two_layers(nc, T, C, "m0", EXPERTS, MB // 2, MB % 2, MT, D, T["slots"], T["moe_w1"], T["moe_b1"], T["moe_w2"],
                               T["moe_b2"], ACT.Relu, True, T["y"]),
            lambda: combine_and_project(nc, T, C),
            lambda: edge_softmax(nc, T, C, "e1", T["sc1"], GH, C["edge_w"], AttentionSums),
            lambda: aggregate(nc, T, C, "e2", T["hp"], GH, C["edge_w"]),
            lambda: second_features(nc, T, C),
            lambda: edge_softmax(nc, T, C, "e3", T["sc2"], 1, C["edge_w1"]),
            lambda: aggregate(nc, T, C, "e4", T["hp"], 1, C["edge_w1"]),
            lambda: second_update(nc, T, C),
            lambda: select_rows(nc, T, C),
            lambda: two_layers(nc, T, C, "m1", 1, SB // 2, 0, P, SW, T["packed"], T["ffn_w1"], T["ffn_b1"], T["ffn_w2"],
                               T["ffn_b2"], ACT.Gelu_apprx_tanh, False, T["out"]),
        )
        for stage in stages:
            stage()


def layout(i):
    def f(name):
        return np.ascontiguousarray(i[name])

    x = np.zeros((NP, D), np.float32)
    x[:N] = f("x")
    src, dst = f("src").astype(np.int32, copy=False), f("dst").astype(np.int32, copy=False)

    def edges(a, before, after, shift):
        out = np.full(EP + 2, after, np.int32)
        out[0] = out[EP + 1] = before
        out[1:E + 1] = a
        return out[1 + shift:1 + shift + EP]

    far = 32767
    key, prev, nxt = (edges(dst, -1, far, s) for s in (0, -1, 1))
    src_p, dst_p = edges(src, 0, 0, 0), edges(dst, 0, 0, 0)

    def tile(a):
        return np.ascontiguousarray(a.reshape(ET, P).T)

    def lane(a):
        return np.ascontiguousarray(a.reshape(P, ET))

    def scores(a_src, a_dst):
        h, n = a_src.shape
        out = np.zeros((h * n, 2 * h), np.float32)
        for k in range(h):
            out[k * n:(k + 1) * n, k] = a_src[k]
            out[k * n:(k + 1) * n, h + k] = a_dst[k]
        return out

    p, q = np.arange(P)[:, None], np.arange(P)[None, :]
    row = (np.arange(G)[None, :, None] * GROUP + np.arange(P)[:, None, None] * J + np.arange(J)[None, None, :])
    last = np.zeros((P, 2), np.float32)
    last[:, 1] = -5.0
    last[P - 1] = (1.0, 0.0)
    ev = np.stack([np.arange(EXPERTS, 0, -1), np.arange(EXPERTS) * MROWS]).astype(np.float32)
    src_tile = np.zeros((P, ET + EU), np.int32)
    src_tile[:, :ET] = tile(src_p)
    return {
        "x": x,
        "W_l_t": np.ascontiguousarray(f("L0_gnn_W_l").T), "W_r_t": np.ascontiguousarray(f("L0_gnn_W_r").T), "b_r": f("L0_gnn_b_r"),
        "kln_weight": np.ascontiguousarray(f("L0_mix_kln_weight").reshape(KC, P).T),
        "kln_bias": np.ascontiguousarray(f("L0_mix_kln_bias").reshape(KC, P).T),
        "vln_weight": f("L0_mix_vln_weight").reshape(-1), "vln_bias": f("L0_mix_vln_bias").reshape(-1),
        "gate_w": f("L0_ffn_gate_w"), "gate_b": f("L0_ffn_gate_b"),
        "moe_w1": f("L0_ffn_w1"), "moe_w2": f("L0_ffn_w2"), "moe_b2": f("L0_ffn_b2"),
        "moe_b1": np.ascontiguousarray(f("L0_ffn_b1").reshape(EXPERTS, FF // P, P).transpose(0, 2, 1)),
        "W1_t": np.ascontiguousarray(f("L1_gnn_W1").T), "W1": f("L1_gnn_W1"), "a1": scores(f("L1_gnn_a1_src"), f("L1_gnn_a1_dst")),
        "W2_t": np.ascontiguousarray(f("L1_gnn_W2").T), "W2": f("L1_gnn_W2"), "a2": scores(f("L1_gnn_a2_src"), f("L1_gnn_a2_dst")),
        "wq": f("L1_mix_wq"), "wk": f("L1_mix_wk"), "wv": f("L1_mix_wv"), "wo": f("L1_mix_wo"),
        "b_qk": np.concatenate([f("L1_mix_bq"), f("L1_mix_bk")]), "bv": f("L1_mix_bv"), "bo": f("L1_mix_bo"),
        "ffn_wr": f("L1_ffn_wr"), "ffn_br": f("L1_ffn_br"), "ffn_w1": f("L1_ffn_w1")[None], "ffn_w2": f("L1_ffn_w2")[None],
        "ffn_b1": np.ascontiguousarray(f("L1_ffn_b1").reshape(1, FF // P, P).transpose(0, 2, 1)), "ffn_b2": f("L1_ffn_b2")[None],
        "keys": key, "dst_tile": tile(key), "next_tile": tile(nxt), "src_tile": src_tile,
        "lane_i": np.pad(np.stack([lane(src_p), lane(dst_p)], axis=2), ((0, 0), (0, EU), (0, 0))),
        "key_lane": lane(key), "prev_lane": lane(prev), "next_lane": lane(nxt),
        "c_ident": np.eye(P, dtype=np.float32), "c_tri": (p < q).astype(np.float32),
        "c_heads": (p // HC == q // HC).astype(np.float32), "c_last": last,
        "c_valid": (row[:, :, 0] < N).astype(np.float32), "c_valid_cols": (row < N).reshape(P, -1).astype(np.float32),
        "c_ids": np.where(row < N, row, int(FAR)).reshape(P, -1).astype(np.int32),
        "c_experts": np.ascontiguousarray(np.broadcast_to(ev, (P, 2, EXPERTS))),
    }


def kernel(**inputs):
    import concourse.bacc as bacc
    from concourse.bass_utils import run_bass_kernel_spmd

    nc = bacc.Bacc("TRN2", target_bir_lowering=False, num_devices=1)
    arrays, T = {}, {}
    for name, a in layout(inputs).items():
        arrays["in_" + name] = a
        T[name] = nc.dram_tensor("in_" + name, a.shape, mybir.dt.from_np(a.dtype), kind="ExternalInput").ap()
    T["out"] = nc.dram_tensor("out", (NP, D), F32, kind="ExternalOutput").ap()
    build(nc, T)
    r = run_bass_kernel_spmd(nc, [arrays], core_ids=[0])
    return r.results[0]["out"][:N]
```

```python
from contextlib import ExitStack

import numpy as np

import concourse.bass as bass
from concourse import mybir

F32 = mybir.dt.float32
I32 = mybir.dt.int32
ALU = mybir.AluOpType
ACT = mybir.ActivationFunctionType
AX = mybir.AxisListType

P = 128
D = 256
KC = D // P
N = 20000
J = 4
GROUP = P * J
G = -(-N // GROUP)
G += G % 2
NP = G * GROUP
LAST_P = (N % GROUP) // J
assert N // GROUP == G - 1 and N % GROUP % J == 0
E = 30000
ET = -(-E // P)
EP = ET * P
EU = 5
HEADS, HC = 8, 32
LN_EPS = 1e-5
EXPERTS, FF = 8, 1024
CAP = 3125
MB = 7
MT = 112
MROWS = MT * J * MB
GH = 4
SEL = N // 2 - 1
SB = 20
SW = 2 * D + 2
FAR = 1.0e6
BIG = 1.0e30


def sb(c, nc, name, shape, dt=F32):
    return c.enter_context(nc.sbuf_tensor(name, shape, dt))


def ps(c, nc, name, shape, dt=F32):
    return c.enter_context(nc.psum_tensor(name, shape, dt))


def sem(c, nc, name):
    handle = nc.alloc_semaphore(name)
    c.semaphores.append(handle)
    return handle


class Stage(ExitStack):

    def __init__(self, nc):
        super().__init__()
        self.nc, self.semaphores = nc, []

    def __exit__(self, *error):
        super().__exit__(*error)
        if error[0] is None:
            self.nc.clear_and_free_semaphores(self.semaphores)
            self.nc.all_engine_barrier()


def rows(dram, g):
    return dram[bass.ds(g * GROUP, GROUP), :].rearrange("(p j) d -> p j d", j=J)


def wait_all(eng, tick, *waits):
    for s, v in waits:
        eng.wait_ge(s, v)
    eng.sem_inc(tick, 1)


class Steps:

    def __init__(self, eng, semaphore, turn=0, per=0):
        self.eng, self.sem, self.base, self.per, self.k = eng, semaphore, turn * per, per, 0

    def then(self, instruction, tick=None):
        self.k += 1
        instruction.then_inc(self.sem, 1)
        self.eng.wait_ge(self.sem, self.base + self.k)
        if tick is not None:
            self.eng.sem_inc(tick, 1)

    def end(self):
        assert self.k == self.per, (self.k, self.per)


def row_mean_var(v, step, tick, x, stats, mv, ve):
    for j in range(J):
        i = v.bn_stats(stats[:, j, :], x[:, j, :])
    step.then(i, tick)
    for j in range(J):
        i = v.bn_aggr(mv[:, j, :], stats[:, j, :])
    step.then(i)
    return v.tensor_scalar(ve, mv[:, :, 1], LN_EPS, None, ALU.add)


def inverse_root(v, step, rs, ve, nt):
    step.then(v.tensor_scalar(rs[:, :].bitcast(I32), ve[:, :].bitcast(I32), -0.5, float(0x5F3759DF), ALU.mult, ALU.add))
    for n in range(3):
        step.then(v.tensor_tensor(nt[:, :], rs[:, :], rs[:, :], ALU.mult))
        step.then(v.scalar_tensor_tensor(nt[:, :], nt[:, :], -0.5, ve[:, :], ALU.mult, ALU.mult))
        step.then(v.scalar_tensor_tensor(rs[:, :], nt[:, :], 1.5, rs[:, :], ALU.add, ALU.mult))


def norm_rows(nc, T, C):
    NB = 4
    assert G % NB == 0
    with Stage(nc) as c:
        x_t = sb(c, nc, "a_x", [P, NB, J, D])
        xn_t = sb(c, nc, "a_xn", [P, NB, J, D])
        stats = sb(c, nc, "a_stats", [P, J, 6])
        mv = sb(c, nc, "a_mv", [P, 2, J, 2])
        ve = sb(c, nc, "a_ve", [P, 2, J])
        sd = sb(c, nc, "a_sd", [P, 2, J])
        rs = sb(c, nc, "a_rs", [P, J])
        zf = sb(c, nc, "a_zf", [P, 2560])
        x_in = [sem(c, nc, f"a_x_in{b}") for b in range(NB)]
        xn_out = [sem(c, nc, f"a_xn_out{b}") for b in range(NB)]
        st1 = sem(c, nc, "a_step1")
        st2 = sem(c, nc, "a_step2")
        s_var = sem(c, nc, "a_var")
        s_std = sem(c, nc, "a_std")
        s_xn = sem(c, nc, "a_s_xn")
        s_fill = sem(c, nc, "a_s_fill")
        s_zf = sem(c, nc, "a_s_zf")
        tick = sem(c, nc, "a_tick")
        block = c.enter_context(nc.Block())

        @block.sync
        def _(sp):
            def store(g, b):
                sp.wait_ge(s_xn, g + 1)
                sp.dma_start(rows(T["xn"], g), xn_t[:, b]).then_inc(xn_out[b], 16)

            for b in range(NB):
                sp.dma_start(x_t[:, b], rows(T["x"], b)).then_inc(x_in[b], 16)
            with sp.Fori(0, G // NB - 1) as u:
                for b in range(NB):
                    store(u * NB + b, b)
                    sp.dma_start(x_t[:, b], rows(T["x"], u * NB + b + NB)).then_inc(x_in[b], 16)
            for b in range(NB):
                store(G - NB + b, b)
            for b in range(NB):
                sp.wait_ge(xn_out[b], 16 * (G // NB))

        @block.gpsimd
        def _(pool):
            pool.memset(zf[:, :], 0.0).then_inc(s_zf, 1)
            pool.wait_ge(s_zf, 1)
            n = 0
            for dram, count in ((T["agg"], NP * D // P), (T["slots"], (EXPERTS * MB + 1) * MT * J * D // P)):
                w = dram.rearrange("r d -> (r d)").rearrange("(p n) -> p n", p=P)
                for a in range(0, count, 2560):
                    k = min(2560, count - a)
                    pool.dma_start(w[:, a:a + k], zf[:, 0:k]).then_inc(s_fill, 16)
                    n += 1
            pool.wait_ge(s_fill, 16 * n)

        @block.scalar
        def _(act):
            with act.Fori(0, G // 2) as u:
                for b in range(2):
                    act.wait_ge(s_var, u * 2 + b + 1)
                    act.activation(sd[:, b], ve[:, b], ACT.Sqrt).then_inc(s_std, 1)

        @block.vector
        def _(v):
            def variance(g, b, u):
                step = Steps(v, st1, g, 2)
                v.wait_ge(x_in[b], u * 16 + 16)
                row_mean_var(v, step, tick, x_t[:, b], stats, mv[:, b % 2], ve[:, b % 2]).then_inc(s_var, 1)
                step.end()

            def norm(g, b, u):
                step = Steps(v, st2, g, 1)
                v.wait_ge(s_std, g + 1)
                v.wait_ge(s_xn, g)
                step.then(v.reciprocal(rs[:, :], sd[:, b % 2]))
                v.wait_ge(xn_out[b], u * 16)
                for j in range(J):
                    i = v.tensor_scalar(xn_t[:, b, j, :], x_t[:, b, j, :], mv[:, b % 2, j, 0:1], rs[:, j:j + 1],
                                        ALU.subtract, ALU.mult)
                i.then_inc(s_xn, 1)
                step.end()

            variance(0, 0, 0)
            with v.Fori(0, G // NB - 1) as u:
                for b in range(NB):
                    variance(u * NB + b + 1, (b + 1) % NB, u + (b + 1) // NB)
                    norm(u * NB + b, b, u)
            for b in range(NB):
                if b < NB - 1:
                    variance(G - NB + b + 1, b + 1, G // NB - 1)
                norm(G - NB + b, b, G // NB - 1)


class HeadGram:

    def __init__(self, c, nc, T, C):
        self.T, self.C = T, C
        self.x_t = sb(c, nc, "h_x", [P, 2, J, D])
        self.d_t = sb(c, nc, "h_d", [P, J, D])
        self.sq_t = sb(c, nc, "h_sq", [P, J, D])
        self.z_t = sb(c, nc, "h_z", [P, 2, J, KC, P + 1])
        self.hm, self.hv, self.hsd, self.hr = (sb(c, nc, "h_" + n, [P, J * HEADS]) for n in ("hm", "hv", "hsd", "hr"))
        self.zero = sb(c, nc, "h_zero", [P, 512])
        self.gram = sb(c, nc, "h_gram", [P, KC, P + 1])
        self.sdiag = sb(c, nc, "h_sdiag", [P, KC, P])
        self.srow = sb(c, nc, "h_srow", [P, KC, P])
        self.kcol = sb(c, nc, "h_kcol", [P, 2, KC])
        self.vrow = sb(c, nc, "h_vrow", [P, 2, D])
        self.kv = sb(c, nc, "h_kv", [P, KC, P])
        self.t1 = sb(c, nc, "h_t1", [P, P])
        self.t2 = sb(c, nc, "h_t2", [P, P])
        self.cs = sb(c, nc, "h_cs", [P, 1])
        self.pg = ps(c, nc, "h_pg", [P, KC, 256])
        self.pr = ps(c, nc, "h_pr", [P, KC, 256])
        self.x_in = [sem(c, nc, f"h_x_in{b}") for b in range(2)]
        (self.s_par, self.s_init, self.s_step, self.s_d, self.s_sq, self.s_hv, self.s_hsd, self.s_z, self.z_free,
         self.s_gram, self.s_diag, self.s_srow) = (
            sem(c, nc, "h_s_" + n)
            for n in ("par", "init", "step", "d", "sq", "hv", "hsd", "z", "z_free", "gram", "diag", "srow"))

    def load(self, sp, g, b):
        sp.dma_start(self.x_t[:, b], rows(self.T["xn"], g)).then_inc(self.x_in[b], 16)

    def sync_begin(self, sp):
        T = self.T
        sp.dma_start(self.kcol[:, 0, :], T["kln_weight"]).then_inc(self.s_par, 16)
        sp.dma_start(self.kcol[:, 1, :], T["kln_bias"]).then_inc(self.s_par, 16)
        sp.dma_start(self.vrow[:, 0, :], T["vln_weight"].partition_broadcast(P)).then_inc(self.s_par, 16)
        sp.dma_start(self.vrow[:, 1, :], T["vln_bias"].partition_broadcast(P)).then_inc(self.s_par, 16)
        self.load(sp, 0, 0)
        self.load(sp, 1, 1)

    def sync_step(self, sp, g, b, u, k, more):
        if k == EU - 1 and more:
            sp.wait_ge(self.s_d, g + 1)
            self.load(sp, g + 2, b)

    def scalar_step(self, act, g, b, u, k, more):
        if k == 1:
            act.wait_ge(self.s_d, g + 1)
            act.activation(self.sq_t[:, :, :], self.d_t[:, :, :], ACT.Square).then_inc(self.s_sq, 1)
        if k == 3:
            act.wait_ge(self.s_hv, g + 1)
            act.activation(self.hsd[:, :], self.hv[:, :], ACT.Sqrt, scale=1.0 / (HC - 1)).then_inc(self.s_hsd, 1)

    def tensor_begin(self, pe):
        pe.wait_ge(self.s_init, 1)
        pe.matmul(self.pg[:, :, :], self.zero[:, 0:P], self.zero[:, :], start=True, stop=False, skip_group_check=True)
        pe.sem_inc(self.z_free, 2)

    def tensor_step(self, pe, g, b, u, k, more):
        if k == EU - 1:
            pe.wait_ge(self.s_z, g + 1)
            for j in range(J):
                for h in range(KC):
                    i = pe.matmul(self.pg[:, h, 0:P + 1], self.z_t[:, b, j, h, 0:P], self.z_t[:, b, j, h, :],
                                  start=False, stop=False, skip_group_check=True)
            i.then_inc(self.z_free, 1)

    def tensor_end(self, pe):
        pe.matmul(self.pg[:, :, :], self.zero[:, 0:P], self.zero[:, :], start=False, stop=True,
                  skip_group_check=True).then_inc(self.s_gram, 1)
        pe.wait_ge(self.s_diag, 1)
        for h in range(KC):
            i = pe.matmul(self.pr[:, h, 0:P], self.C["ones"][:, :], self.sdiag[:, h, :], start=(h == 0), stop=True,
                          skip_group_check=True)
        i.then_inc(self.s_srow, 1)

    def vector_begin(self, v):
        v.memset(self.zero[:, :], 0.0)
        for b in range(2):
            i = v.memset(self.z_t[:, b, :, :, P:P + 1], 1.0)
        i.then_inc(self.s_init, 1)
        v.wait_ge(self.s_init, 1)

    def vector_step(self, v, g, b, u, k, more):
        heads = self.x_t[:, b].rearrange("p j (h k) -> p (j h) k", k=HC)
        wide = [P, J * HEADS, HC]
        if k == 0:
            v.wait_ge(self.x_in[b], u * 16 + 16)
            v.wait_ge(self.s_z, g)
            v.tensor_reduce(self.hm[:, :], heads, AX.X, ALU.add).then_inc(self.s_step, 1)
            v.wait_ge(self.s_step, g * 3 + 1)
            v.scalar_tensor_tensor(self.d_t[:, :, :].rearrange("p j (h k) -> p (j h) k", k=HC),
                                   self.hm[:, :].unsqueeze(2).to_broadcast(wide), -1.0 / HC, heads, ALU.mult,
                                   ALU.add).then_inc(self.s_d, 1)
        if k == 2:
            v.wait_ge(self.s_sq, g + 1)
            v.tensor_reduce(self.hv[:, :], self.sq_t[:, :, :].rearrange("p j (h k) -> p (j h) k", k=HC), AX.X,
                            ALU.add).then_inc(self.s_hv, 1)
        if k == 4:
            v.wait_ge(self.s_hsd, g + 1)
            v.tensor_scalar(self.hr[:, :], self.hsd[:, :], 1e-5, None, ALU.add).then_inc(self.s_step, 1)
            v.wait_ge(self.s_step, g * 3 + 2)
            v.reciprocal(self.hr[:, :], self.hr[:, :]).then_inc(self.s_step, 1)
            v.wait_ge(self.s_step, g * 3 + 3)
            v.wait_ge(self.z_free, g + 1)
            v.tensor_tensor(self.z_t[:, b, :, :, 0:P].rearrange("p j c (h k) -> p (j c) h k", k=HC),
                            self.d_t[:, :, :].rearrange("p j (c h k) -> p (j c) h k", c=KC, k=HC),
                            self.hr[:, :].rearrange("p (a h) -> p a h", h=HEADS // KC).unsqueeze(3)
                            .to_broadcast([P, J * KC, HEADS // KC, HC]), ALU.mult).then_inc(self.s_z, 1)

    def vector_end(self, v):
        step = Steps(v, self.s_init)
        step.k = 1
        v.wait_ge(self.s_gram, 1)
        step.then(v.tensor_copy(self.gram[:, :, :], self.pg[:, :, 0:P + 1]))
        for h in range(KC):
            i = v.tensor_scalar(self.sdiag[:, h, :], self.C["ident"][:, :], self.gram[:, h, P:P + 1], None, ALU.mult)
        i.then_inc(self.s_diag, 1)
        v.wait_ge(self.s_srow, 1)
        step.then(v.tensor_copy(self.srow[:, :, :], self.pr[:, :, 0:P]))
        v.wait_ge(self.s_par, 64)
        for h in range(KC):
            wv, bv = self.vrow[:, 0, h * P:(h + 1) * P], self.vrow[:, 1, h * P:(h + 1) * P]
            wk, bk = self.kcol[:, 0, h:h + 1], self.kcol[:, 1, h:h + 1]
            step.then(v.scalar_tensor_tensor(self.t1[:, :], self.gram[:, h, 0:P], wk, wv, ALU.mult, ALU.mult))
            step.then(v.tensor_tensor(self.cs[:, :], self.gram[:, h, P:P + 1], wk, ALU.mult))
            step.then(v.scalar_tensor_tensor(self.t1[:, :], bv, self.cs[:, 0:1], self.t1[:, :], ALU.mult, ALU.add))
            step.then(v.tensor_tensor(self.t2[:, :], self.srow[:, h, :], wv, ALU.mult))
            step.then(v.scalar_tensor_tensor(self.t2[:, :], bv, float(N), self.t2[:, :], ALU.mult, ALU.add))
            step.then(v.scalar_tensor_tensor(self.t1[:, :], self.t2[:, :], bk, self.t1[:, :], ALU.mult, ALU.add))
            step.then(v.scalar_tensor_tensor(self.kv[:, h, :], self.t1[:, :], 1.0 / N, self.C["heads"][:, :], ALU.mult, ALU.mult))
            step.then(v.tensor_tensor(self.kv[:, h, :], self.kv[:, h, :], self.C["ident"][:, :], ALU.add))
            w = self.C["wr"][:, h, h * P:(h + 1) * P]
            step.then(v.tensor_tensor(w, w, self.kv[:, h, :], ALU.add))


def load_constants(nc, T, C):
    with Stage(nc) as c:
        s_in = sem(c, nc, "c_in")
        s_step = sem(c, nc, "c_step")
        di = sb(c, nc, "c_dst_i", [P, ET], I32)
        ni = sb(c, nc, "c_next_i", [P, ET], I32)
        li = sb(c, nc, "c_lane_i", [P, 3, ET], I32)
        nf = sb(c, nc, "c_next_f", [P, ET])
        lf = sb(c, nc, "c_lane_f", [P, 3, ET])
        lt = sb(c, nc, "c_last", [P, 2])
        block = c.enter_context(nc.Block())
        loads = [
            (C["ident"][:, :], T["c_ident"]), (C["tri"][:, :], T["c_tri"]), (C["heads"][:, :], T["c_heads"]),
            (lt[:, :], T["c_last"]), (C["valid"][:, :], T["c_valid"]),
            (C["valid_cols"][:, :], T["c_valid_cols"]), (C["ids"][:, :], T["c_ids"]),
            (C["wl"][:, :, :], T["W_l_t"].rearrange("(c p) n -> p c n", p=P)),
            (C["wr"][:, :, :], T["W_r_t"].rearrange("(c p) n -> p c n", p=P)),
            (di[:, :], T["dst_tile"]), (ni[:, :], T["next_tile"]), (C["src_i"][:, :], T["src_tile"]),
            (C["lane_i"][:, :, :], T["lane_i"]),
            (li[:, 0, :], T["key_lane"]), (li[:, 1, :], T["prev_lane"]), (li[:, 2, :], T["next_lane"]),
        ]

        @block.sync
        def _(sp):
            for out, in_ in loads:
                sp.dma_start(out, in_).then_inc(s_in, 16)

        @block.vector
        def _(v):
            step = Steps(v, s_step)
            step.then(v.memset(C["ones"][:, :], 1.0))
            v.wait_ge(s_in, 16 * len(loads))
            step.then(v.tensor_copy(C["dst_f"][:, :], di[:, :]))
            step.then(v.tensor_copy(nf[:, :], ni[:, :]))
            step.then(v.tensor_tensor(nf[:, :], nf[:, :], C["dst_f"][:, :], ALU.is_equal))
            step.then(v.scalar_tensor_tensor(nf[:, :], nf[:, :], FAR, C["dst_f"][:, :], ALU.mult, ALU.add))
            step.then(v.tensor_copy(C["out_i"][:, :], nf[:, :]))
            step.then(v.memset(C["carry_f"][:, :], -5.0))
            step.then(v.tensor_scalar(C["carry_f"][:, 1:ET], C["dst_f"][:, 0:ET - 1], lt[:, 0:1], lt[:, 1:2],
                                      ALU.mult, ALU.add))
            step.then(v.tensor_copy(lf[:, :, :], li[:, :, :]))
            step.then(v.tensor_tensor(C["same_prev"][:, :], lf[:, 0, :], lf[:, 1, :], ALU.is_equal))
            step.then(v.tensor_tensor(C["same_next"][:, :], lf[:, 0, :], lf[:, 2, :], ALU.is_equal))
            step.then(v.tensor_scalar(C["cut_prev"][:, :], C["same_prev"][:, :], 1.0, BIG, ALU.subtract, ALU.mult))
            step.then(v.tensor_scalar(C["cut_next"][:, :], C["same_next"][:, :], -1.0, 1.0, ALU.mult, ALU.add))
            step.then(v.tensor_reduce(C["all_prev"][:, :], C["same_prev"][:, :], AX.X, ALU.min))
            step.then(v.tensor_scalar(C["cut_whole"][:, :], C["all_prev"][:, :], 1.0, BIG, ALU.subtract, ALU.mult))
            step.then(v.tensor_reduce(C["all_next"][:, :], C["same_next"][:, :], AX.X, ALU.min))


class Segments:

    def __init__(self, c, nc, T, C, name, heads):
        self.T, self.C, self.h = T, C, heads
        self.f = sb(c, nc, name + "_scan", [P, heads, ET])
        self.g = sb(c, nc, name + "_back", [P, heads, ET])
        self.ends = sb(c, nc, name + "_ends", [P, 2, heads])
        self.row = sb(c, nc, name + "_row", [1, 2, heads, P])
        self.out = sb(c, nc, name + "_out", [1, heads, P + 1])
        self.start = sb(c, nc, name + "_start", [P, heads])
        self.s_ends = sem(c, nc, name + "_s_ends")
        self.s_row = sem(c, nc, name + "_s_row")
        self.s_out = sem(c, nc, name + "_s_out")
        self.s_start = sem(c, nc, name + "_s_start")
        self.s_hop = sem(c, nc, name + "_s_hop")
        self.n = 0

    def carry(self, sp, passes):
        hop = 0
        for n in range(passes):
            ends_d, out_d = self.T["ends"], self.T["starts"]
            h = self.h
            sp.wait_ge(self.s_ends, n + 1)
            sp.dma_start(ends_d[0:2 * h, :].rearrange("a p -> p a"), self.ends[:, :, :].rearrange("p a h -> p (a h)"),
                         allow_slow_non_contiguous=True).then_inc(self.s_hop, 16)
            hop += 16
            sp.wait_ge(self.s_hop, hop)
            sp.dma_start(self.row[:, :, :, :].rearrange("o a h p -> o (a h p)"),
                         ends_d[0:2 * h, :].rearrange("a p -> (a p)").unsqueeze(0)).then_inc(self.s_row, 16)
            sp.wait_ge(self.s_out, n + 1)
            sp.dma_start(out_d[0:h, :].rearrange("a p -> (a p)").unsqueeze(0),
                         self.out[:, :, :].rearrange("o h p -> o (h p)")).then_inc(self.s_hop, 16)
            hop += 16
            sp.wait_ge(self.s_hop, hop)
            o = 0 if n % 2 == 0 else 1
            sp.dma_start(self.start[:, :], out_d[0:h, o:o + P].rearrange("a p -> p a"),
                         allow_slow_non_contiguous=True).then_inc(self.s_start, 16)

    def scan(self, v, step, out, data0, data1, op0, op1, back, whole, first):
        h = self.h
        flip = (lambda a: a[:, ::-1]) if back else (lambda a: a)
        for k in range(h):
            i = v.tensor_tensor_scan(flip(out[:, k, :]), flip(data0), flip(data1[:, k, :]), first, op0, op1)
        step.then(i)
        for k in range(h):
            v.tensor_copy(self.ends[:, 0, k:k + 1], out[:, k, 0:1] if back else out[:, k, ET - 1:ET])
            i = v.tensor_copy(self.ends[:, 1, k:k + 1], whole)
        i.then_inc(self.s_ends, 1)
        n = self.n
        v.wait_ge(self.s_row, 16 * (n + 1))
        step.then(v.memset(self.out[:, :, :], first))
        for k in range(h):
            o = self.out[:, k, 0:P] if back else self.out[:, k, 1:P + 1]
            i = v.tensor_tensor_scan(flip(o), flip(self.row[:, 1, k, :]), flip(self.row[:, 0, k, :]), first, op0, op1)
        i.then_inc(self.s_out, 1)
        v.wait_ge(self.s_start, 16 * (n + 1))
        for k in range(h):
            i = v.tensor_tensor_scan(flip(out[:, k, :]), flip(data0), flip(data1[:, k, :]), self.start[:, k:k + 1],
                                     op0, op1)
        step.then(i)
        self.n += 1

    def total(self, v, step, x, largest):
        C = self.C
        if largest:
            self.scan(v, step, self.f, C["cut_prev"][:, :], x, ALU.add, ALU.max, False, C["cut_whole"][:, :], -BIG)
        else:
            self.scan(v, step, self.f, C["same_prev"][:, :], x, ALU.mult, ALU.add, False, C["all_prev"][:, :], 0.0)
        cut = C["cut_next"][:, :].unsqueeze(1).to_broadcast([P, self.h, ET])
        step.then(v.tensor_tensor(self.f[:, :, :], self.f[:, :, :], cut, ALU.mult))
        self.scan(v, step, self.g, C["same_next"][:, :], self.f, ALU.mult, ALU.add, True, C["all_next"][:, :], 0.0)


def spread_weights(nc, T, C, h, w, w_tile, s_w, names):
    rows_t, pt, s_wd, s_wr, s_pt = names
    low = ET - P

    def load(sp):
        sp.wait_ge(s_w, 1)
        sp.dma_start(T["w_edges"][0:h, :].rearrange("h (p c) -> p h c", p=P), w[:, :, :]).then_inc(s_wd, 16)
        sp.wait_ge(s_wd, 16)
        view = T["w_edges"][0:h, :].rearrange("h (i e) -> i h e", e=P)
        sp.dma_start(rows_t[:, 0, :, :], view[0:P]).then_inc(s_wr, 16)
        sp.dma_start(rows_t[0:low, 1, :, :], view[P:ET]).then_inc(s_wr, 16)

    def turn(pe):
        pe.wait_ge(s_wr, 32)
        for k in range(h):
            pe.transpose(pt[:, k, 0:P], rows_t[:, 0, k, :], C["ident"][:, :])
            i = pe.transpose(pt[:, k, P:ET], rows_t[0:low, 1, k, :], C["ident"][0:low, 0:low])
        i.then_inc(s_pt, 1)

    def land(v):
        v.wait_ge(s_pt, 1)
        return v.tensor_copy(w_tile[:, :, :].rearrange("p i h -> p h i"), pt[:, 0:h, 0:ET])

    return load, turn, land


def weight_buffers(c, nc, name, h):
    return (sb(c, nc, name + "_rows", [P, 2, h, P]), ps(c, nc, name + "_pt", [P, h, 256]),
            sem(c, nc, name + "_s_wd"), sem(c, nc, name + "_s_wr"), sem(c, nc, name + "_s_pt"))


def mean_weights(nc, T, C, w_tile):
    with Stage(nc) as c:
        ones_e = sb(c, nc, "m_ones", [P, 1, ET])
        seg = Segments(c, nc, T, C, "m_seg", 1)
        names = weight_buffers(c, nc, "m", 1)
        s_step = sem(c, nc, "m_step")
        s_w = sem(c, nc, "m_s_w")
        block = c.enter_context(nc.Block())
        load, turn, land = spread_weights(nc, T, C, 1, ones_e, w_tile, s_w, names)

        @block.sync
        def _(sp):
            seg.carry(sp, 2)
            load(sp)

        @block.tensor
        def _(pe):
            turn(pe)

        @block.vector
        def _(v):
            step = Steps(v, s_step)
            step.then(v.memset(ones_e[:, :, :], 1.0))
            seg.total(v, step, ones_e, False)
            v.reciprocal(ones_e[:, :, :], seg.g[:, :, :]).then_inc(s_w, 1)
            step.then(land(v))


class AttentionSums:

    def __init__(self, c, nc, T, C):
        self.T, self.C, self.QK = T, C, 2 * D
        self.x_t = sb(c, nc, "q_x", [P, 2, J, D])
        self.tr_t = sb(c, nc, "q_tr", [P, 2, KC, P])
        self.wqk = sb(c, nc, "q_wqk", [P, KC, self.QK])
        self.wv = sb(c, nc, "q_wv", [P, KC, D])
        self.bqk = sb(c, nc, "q_bqk", [P, self.QK])
        self.bv = sb(c, nc, "q_bv", [P, D])
        self.t_t = sb(c, nc, "q_t", [P, 2, self.QK])
        self.e_t = sb(c, nc, "q_e", [P, 2, self.QK])
        self.k_t = sb(c, nc, "q_k", [P, J, D])
        self.q_t = sb(c, nc, "q_q", [P, 2, J, D])
        self.v_t = sb(c, nc, "q_v", [P, J, KC, P + 1])
        self.zero = sb(c, nc, "q_zero", [P, 512])
        self.pt = ps(c, nc, "q_pt", [P, KC, P])
        self.pqk = [ps(c, nc, f"q_pqk{n}", [P, 512]) for n in range(2)]
        self.pv = [ps(c, nc, f"q_pv{n}", [P, 512]) for n in range(2)]
        self.pkv = ps(c, nc, "q_pkv", [P, KC, 256])
        self.x_in = [sem(c, nc, f"q_x_in{b}") for b in range(2)]
        self.q_out = [sem(c, nc, f"q_q_out{b}") for b in range(2)]
        self.s_par, self.s_init, self.s_pt, self.s_tr, self.s_mm, self.s_qkb, self.s_e, self.s_ph, self.s_kv = (
            sem(c, nc, "q_s_" + n) for n in ("par", "init", "pt", "tr", "mm", "qkb", "e", "ph", "kv"))

    def sync(self, sp):
        T = self.T
        for out, in_ in ((self.wqk[:, :, 0:D], T["wq"].rearrange("(c p) n -> p c n", p=P)),
                         (self.wqk[:, :, D:], T["wk"].rearrange("(c p) n -> p c n", p=P)),
                         (self.wv[:, :, :], T["wv"].rearrange("(c p) n -> p c n", p=P)),
                         (self.bqk[:, :], T["b_qk"].partition_broadcast(P)),
                         (self.bv[:, :], T["bv"].partition_broadcast(P))):
            sp.dma_start(out, in_).then_inc(self.s_par, 16)

        def load(g, b, u):
            sp.wait_ge(self.s_pt, g * J + J - 1)
            sp.dma_start(self.x_t[:, b], rows(T["xn"], g)).then_inc(self.x_in[b], 16)

        def store(g, b, u, used):
            sp.wait_ge(self.s_ph, g * J + J + 2)
            sp.dma_start(rows(T["pq"], g), self.q_t[:, b]).then_inc(self.q_out[b], 16)

        ahead(sp, load, store)
        for b in range(2):
            sp.wait_ge(self.q_out[b], 16 * (G // 2))

    def tensor(self, pe):
        def turn(i, b, u, j):
            if j == 0:
                pe.wait_ge(self.x_in[b], u * 16 + 16)
            pe.wait_ge(self.s_tr, i + 1)
            for k in range(KC):
                o = pe.transpose(self.pt[:, k, :], self.x_t[:, b, j, k * P:(k + 1) * P], self.C["ident"][:, :])
            o.then_inc(self.s_pt, 1)

        def sums(i, j, used):
            pe.wait_ge(self.s_ph, i + 3)
            for k in range(KC):
                pe.matmul(self.pkv[:, k, 0:P + 1], self.k_t[0:used, j, k * P:(k + 1) * P], self.v_t[0:used, j, k, :],
                          start=False, stop=False, skip_group_check=True)

        def group(g, b, u, used):
            for j in range(J):
                i, s = g * J + j, j % 2
                if j < J - 1:
                    turn(i + 1, b, u, j + 1)
                elif used == P:
                    turn(i + 1, 1 - b, u + b, 0)
                pe.wait_ge(self.s_tr, i + 2)
                pe.wait_ge(self.s_qkb, i + 1)
                for out, w, n in ((self.pv[s], self.wv, D), (self.pqk[s], self.wqk, self.QK)):
                    for k in range(KC):
                        o = pe.matmul(out[:, 0:n], self.tr_t[:, s, k, :], w[:, k, :], start=(k == 0), stop=(k == KC - 1))
                o.then_inc(self.s_mm, 1)
                sums(i - 2, (j - 2) % J, used if j > 1 else P)
            if used < P:
                for j in range(J - 2, J):
                    sums(g * J + j, j, used)

        pe.wait_ge(self.s_par, 16 * 5)
        pe.wait_ge(self.s_init, 1)
        pe.matmul(self.pkv[:, :, :], self.zero[:, 0:P], self.zero[:, :], start=True, stop=False, skip_group_check=True)
        pe.sem_inc(self.s_mm, 2)
        pe.sem_inc(self.s_pt, 2 * J - 1)
        turn(0, 0, 0, 0)
        ahead(pe, lambda *a: None, group)
        pe.matmul(self.pkv[:, :, :], self.zero[:, 0:P], self.zero[:, :], start=False, stop=True,
                  skip_group_check=True).then_inc(self.s_kv, 1)

    def turned(self, act, i, s):
        act.wait_ge(self.s_pt, i + 2 * J)
        act.wait_ge(self.s_mm, i + 1)
        act.copy(self.tr_t[:, s], self.pt[:, :, :]).then_inc(self.s_tr, 1)

    def scalar_begin(self, act):
        act.sem_inc(self.s_tr, 1)
        self.turned(act, 0, 0)

    def scalar_tile(self, act, g, b, u, j, used):
        if j == J:
            return
        i, s = g * J + j, j % 2
        if j < J - 1 or used == P:
            self.turned(act, i + 1, 1 - s)
        act.wait_ge(self.s_qkb, i + 3)
        act.activation(self.e_t[:, s], self.t_t[:, s], ACT.Exp)
        act.activation(self.t_t[:, s], self.t_t[:, s], ACT.Relu).then_inc(self.s_e, 1)

    def vector_begin(self, v):
        v.memset(self.zero[:, :], 0.0)
        v.memset(self.k_t[:, :, :], 0.0)
        for k in range(KC):
            v.memset(self.v_t[:, :, k, 0:P], 0.0)
            i = v.memset(self.v_t[:, :, k, P:P + 1], 1.0)
        i.then_inc(self.s_init, 1)
        v.wait_ge(self.s_init, 1)
        v.wait_ge(self.s_par, 16 * 5)
        v.sem_inc(self.s_qkb, 2)
        v.sem_inc(self.s_ph, 2)

    def vector_tile(self, v, g, b, u, j, used):
        if j == J:
            return

        def phi(i, j):
            s = j % 2
            v.wait_ge(self.s_e, i + 1)
            v.scalar_tensor_tensor(self.q_t[:, b, j], self.e_t[:, s, 0:D], 1.0, self.t_t[:, s, 0:D], ALU.min, ALU.add)
            v.scalar_tensor_tensor(self.k_t[:, j], self.e_t[:, s, D:], 1.0, self.t_t[:, s, D:], ALU.min,
                                   ALU.add).then_inc(self.s_ph, 1)

        i, s = g * J + j, j % 2
        if j == 0:
            v.wait_ge(self.q_out[b], u * 16)
        v.wait_ge(self.s_mm, i + 3)
        v.tensor_tensor(self.v_t[:, j, :, 0:P], self.pv[s][:, 0:D].rearrange("p (c n) -> p c n", c=KC),
                        self.bv[:, :].rearrange("p (c n) -> p c n", c=KC), ALU.add)
        v.wait_ge(self.s_ph, i + 1)
        v.tensor_tensor(self.t_t[:, s], self.pqk[s][:, :], self.bqk[:, :], ALU.add).then_inc(self.s_qkb, 1)
        if j > 0:
            phi(i - 1, j - 1)
        if j == J - 1:
            phi(i, j)

    def vector_end(self, v):
        v.wait_ge(self.s_kv, 1)
        v.tensor_copy(self.C["kv"][:, :, :], self.pkv[:, :, 0:P + 1])


class AttentionRows:

    HW = P + HEADS // KC

    def __init__(self, c, nc, T, C):
        self.T, self.C = T, C
        self.x_t = sb(c, nc, "r_x", [P, 2, J, D])
        self.q_t = sb(c, nc, "r_q", [P, 2, J, D])
        self.tr_t = sb(c, nc, "r_tr", [P, 2, KC, P])
        self.o_t = sb(c, nc, "r_o", [P, 2, D])
        self.ot_t = sb(c, nc, "r_ot", [P, 2, KC, P])
        self.rc = sb(c, nc, "r_rc", [P, 2, HEADS])
        self.wo = sb(c, nc, "r_wo", [P, KC, D])
        self.bo = sb(c, nc, "r_bo", [P, D])
        self.kvh = sb(c, nc, "r_kvh", [P, KC, self.HW])
        self.pt = ps(c, nc, "r_pt", [P, 2, KC, P])
        self.pq = [ps(c, nc, f"r_pq{n}", [P, 512]) for n in range(2)]
        self.pot = ps(c, nc, "r_pot", [P, KC, P])
        self.po = ps(c, nc, "r_po", [P, J, D])
        self.x_in = [sem(c, nc, f"r_x_in{b}") for b in range(2)]
        self.x_out = [sem(c, nc, f"r_x_out{b}") for b in range(2)]
        self.q_in = [sem(c, nc, f"r_q_in{b}") for b in range(2)]
        (self.s_par, self.s_init, self.s_kv, self.s_pt, self.s_tr, self.s_mq, self.s_o, self.s_pot, self.s_ot, self.s_mo,
         self.s_x, self.s_step) = (
            sem(c, nc, "r_s_" + n)
            for n in ("par", "init", "kv", "pt", "tr", "mq", "o", "pot", "ot", "mo", "x", "step"))

    def sync(self, sp):
        T = self.T
        sp.dma_start(self.wo[:, :, :], T["wo"].rearrange("(c p) n -> p c n", p=P)).then_inc(self.s_par, 16)
        sp.dma_start(self.bo[:, :], T["bo"].partition_broadcast(P)).then_inc(self.s_par, 16)

        def load_q(g, b, u):
            sp.wait_ge(self.s_pt, g * J + J - 1)
            sp.dma_start(self.q_t[:, b], rows(T["pq"], g)).then_inc(self.q_in[b], 16)

        def load_x(g, b):
            sp.dma_start(self.x_t[:, b], rows(T["x2"], g)).then_inc(self.x_in[b], 16)

        def begin():
            load_x(0, 0)
            load_x(1, 1)

        def store(g, b, u, used):
            sp.wait_ge(self.s_x, g + 3)
            sp.dma_start(rows(T["x2"], g), self.x_t[:, b]).then_inc(self.x_out[b], 16)

        def next_group(g, b, u, used):
            store(g, b, u, used)
            sp.wait_ge(self.x_out[b], u * 16 + 16)
            load_x(g + 2, b)

        ahead(sp, load_q, next_group, begin, store)
        for b in range(2):
            sp.wait_ge(self.x_out[b], 16 * (G // 2))

    def tensor(self, pe):
        def group(g, b, u, used):
            pe.wait_ge(self.q_in[b], u * 16 + 16)
            for j in range(J + 2):
                i = g * J + j
                if j < J:
                    pe.wait_ge(self.s_tr, i + 2)
                    for k in range(KC):
                        o = pe.transpose(self.pt[:, j % 2, k, :], self.q_t[:, b, j, k * P:(k + 1) * P], self.C["ident"][:, :])
                    o.then_inc(self.s_pt, 1)
                if 0 < j <= J:
                    s = (j - 1) % 2
                    pe.wait_ge(self.s_tr, i + 2)
                    pe.wait_ge(self.s_o, i)
                    for k in range(KC):
                        o = pe.matmul(self.pq[s][:, k * self.HW:(k + 1) * self.HW], self.tr_t[:, s, k, :], self.kvh[:, k, :],
                                      start=True, stop=True)
                    o.then_inc(self.s_mq, 1)
                if j > 1:
                    s = j % 2
                    pe.wait_ge(self.s_o, i + 1)
                    pe.wait_ge(self.s_ot, i - 2)
                    for k in range(KC):
                        o = pe.transpose(self.pot[:, k, :], self.o_t[:, s, k * P:(k + 1) * P], self.C["ident"][:, :])
                    o.then_inc(self.s_pot, 1)
                    pe.wait_ge(self.s_ot, i - 1)
                    if j == 2:
                        pe.wait_ge(self.s_x, g + 2)
                    for k in range(KC):
                        o = pe.matmul(self.po[:, j - 2, :], self.ot_t[:, s, k, :], self.wo[:, k, :], start=(k == 0),
                                      stop=(k == KC - 1))
                    o.then_inc(self.s_mo, 1)

        pe.wait_ge(self.s_par, 32)
        pe.wait_ge(self.s_kv, 1)
        pe.sem_inc(self.s_pot, 2)
        pe.sem_inc(self.s_pt, 2 * J - 1)
        ahead(pe, lambda *a: None, group)

    def scalar_begin(self, act):
        act.sem_inc(self.s_tr, 2)

    def scalar_tile(self, act, g, b, u, k, used):
        i = g * J + k
        if k < J:
            act.wait_ge(self.s_pt, i + 2 * J)
            act.wait_ge(self.s_mq, i + 1)
            act.copy(self.tr_t[:, k % 2], self.pt[:, k % 2, :, :]).then_inc(self.s_tr, 1)
        for j in {2: (0,), 3: (1,), 4: (2, 3)}.get(k, ()):
            act.wait_ge(self.s_pot, g * J + j + 3)
            act.copy(self.ot_t[:, j % 2], self.pot[:, :, :]).then_inc(self.s_ot, 1)

    def vector_begin(self, v):
        C, HW = self.C, self.HW
        for k in range(KC):
            v.tensor_tensor(self.kvh[:, k, 0:P], C["kv"][:, k, 0:P], C["heads"][:, :], ALU.mult)
        for k in range(KC):
            i = v.tensor_scalar(self.kvh[:, k, P:HW], C["heads"][:, 0:P:HC], C["kv"][:, k, P:P + 1], None, ALU.mult)
        i.then_inc(self.s_kv, 1)
        v.wait_ge(self.s_par, 32)
        v.sem_inc(self.s_mq, 2)
        v.sem_inc(self.s_o, 2)
        v.sem_inc(self.s_x, 2)

    def vector_tile(self, v, g, b, u, k, used):
        i, s, n = g * J + k, k % 2, HEADS // KC
        if k < J:
            v.wait_ge(self.s_mq, i + 3)
            sums = self.pq[s][:, 0:KC * self.HW].rearrange("p (k n) -> p k n", k=KC)
            step = Steps(v, self.s_step, i, 2)
            step.then(v.tensor_scalar(self.rc[:, s, :].rearrange("p (k h) -> p k h", k=KC), sums[:, :, P:self.HW], 1e-6, None,
                                      ALU.add))
            step.then(v.reciprocal(self.rc[:, s, :], self.rc[:, s, :]))
            step.end()
            v.wait_ge(self.s_pot, i + 1)
            for c in range(KC):
                o = v.tensor_tensor(self.o_t[:, s, c * P:(c + 1) * P].rearrange("p (h e) -> p h e", h=n),
                                    sums[:, c, 0:P].rearrange("p (h e) -> p h e", h=n),
                                    self.rc[:, s, c * n:(c + 1) * n].unsqueeze(2).to_broadcast([P, n, HC]), ALU.mult)
            o.then_inc(self.s_o, 1)
        else:
            x = self.x_t[:, b]
            v.wait_ge(self.x_in[b], u * 16 + 16)
            v.tensor_tensor(x, x, self.bo[:, :].unsqueeze(1).to_broadcast([P, J, D]), ALU.add).then_inc(self.s_init, 1)
            v.wait_ge(self.s_init, g + 1)
            v.wait_ge(self.s_mo, g * J + J)
            v.tensor_tensor(x, x, self.po[:, :, :], ALU.add).then_inc(self.s_x, 1)

    def vector_end(self, v):
        pass


def edge_softmax(nc, T, C, name, table, h, w_tile, guest=None):
    with Stage(nc) as c:
        ig = sb(c, nc, name + "_ig", [P, EU, 2], I32)
        gs = sb(c, nc, name + "_gs", [P, EU, 2 * h])
        gd = sb(c, nc, name + "_gd", [P, EU, 2 * h])
        e = sb(c, nc, name + "_e", [P, h, ET])
        w = sb(c, nc, name + "_w", [P, h, ET])
        seg = Segments(c, nc, T, C, name + "_seg", h)
        names = weight_buffers(c, nc, name, h)
        g_in = [sem(c, nc, f"{name}_g_in{k}") for k in range(EU)]
        s_ig = sem(c, nc, name + "_s_ig")
        e_free = sem(c, nc, name + "_e_free")
        s_step = sem(c, nc, name + "_step")
        s_arg = sem(c, nc, name + "_s_arg")
        s_exp = sem(c, nc, name + "_s_exp")
        s_w = sem(c, nc, name + "_s_w")
        tick = sem(c, nc, name + "_tick")
        rows_work = guest(c, nc, T, C) if guest else None
        block = c.enter_context(nc.Block())

        def edge_tiles(eng, edge_tile, row_tile):
            if rows_work is None:
                with eng.Fori(0, ET // EU) as t:
                    for k in range(EU):
                        edge_tile(t, k)
                return

            def turn(g, b, u, used):
                for k in range(EU):
                    edge_tile(g, k)
                    row_tile(g, b, u, k, used)

            ahead(eng, lambda *a: None, turn)
            with eng.Fori(G, ET // EU) as t:
                for k in range(EU):
                    edge_tile(t, k)

        load, turn, land = spread_weights(nc, T, C, h, w, w_tile, s_w, names)

        @block.sync
        def _(sp):
            if rows_work:
                rows_work.sync(sp)
            seg.carry(sp, 4)
            load(sp)

        @block.tensor
        def _(pe):
            if rows_work:
                rows_work.tensor(pe)
            turn(pe)

        @block.gpsimd
        def _(pool):
            with pool.Fori(0, ET // EU) as t:
                for k in range(EU):
                    wait_all(pool, tick, (s_ig, t * EU + k + 1), (e_free, t * EU + k + 1))
                    for n, buf in ((0, gs), (1, gd)):
                        pool.indirect_dma_start(buf[:, k, :], None, table,
                                                bass.IndirectOffsetOnAxis(ap=ig[:, k, n:n + 1], axis=0),
                                                bounds_check=NP - 1, oob_is_err=False).then_inc(g_in[k], 16)

        @block.scalar
        def _(act):
            def indices(t, k):
                act.wait_ge(g_in[k], t * 32)
                act.copy(ig[:, k, :], C["lane_i"][:, bass.ds(t * EU + k, 1), :].rearrange("p o n -> p (o n)")).then_inc(s_ig, 1)

            for k in range(EU):
                indices(0, k)
            if rows_work:
                rows_work.scalar_begin(act)
            edge_tiles(act, lambda t, k: indices(t + 1, k), lambda *a: rows_work.scalar_tile(act, *a))
            act.wait_ge(s_arg, 1)
            act.activation(w[:, :, :], w[:, :, :], ACT.Exp).then_inc(s_exp, 1)

        @block.vector
        def _(v):
            v.sem_inc(e_free, EU)

            def sums(t, k):
                v.wait_ge(g_in[k], t * 32 + 32)
                v.tensor_tensor(e[:, :, bass.ds(t * EU + k, 1)].rearrange("p h o -> p (h o)"), gs[:, k, 0:h],
                                gd[:, k, h:2 * h], ALU.add).then_inc(e_free, 1)

            if rows_work:
                rows_work.vector_begin(v)
            edge_tiles(v, sums, lambda *a: rows_work.vector_tile(v, *a))
            if rows_work:
                rows_work.vector_end(v)
            v.wait_ge(e_free, ET + EU)
            step = Steps(v, s_step)
            step.then(v.scalar_tensor_tensor(e[:, :, :], e[:, :, :], 0.2, e[:, :, :], ALU.mult, ALU.max))
            seg.total(v, step, e, True)
            v.tensor_tensor(w[:, :, :], e[:, :, :], seg.g[:, :, :], ALU.subtract).then_inc(s_arg, 1)
            v.wait_ge(s_exp, 1)
            seg.total(v, step, w, False)
            step.then(v.tensor_scalar(seg.g[:, :, :], seg.g[:, :, :], 1e-16, None, ALU.add))
            step.then(v.reciprocal(seg.g[:, :, :], seg.g[:, :, :]))
            v.tensor_tensor(w[:, :, :], w[:, :, :], seg.g[:, :, :], ALU.mult).then_inc(s_w, 1)
            step.then(land(v))


def aggregate(nc, T, C, name, table, h, w_tile, guest=None):
    AHEAD = 3
    with Stage(nc) as c:
        keys = sb(c, nc, name + "_keys", [P, EU, P], I32)
        ig = sb(c, nc, name + "_ig", [P, EU], I32)
        io = sb(c, nc, name + "_io", [P, EU], I32)
        msg = sb(c, nc, name + "_msg", [P, EU, D])
        m = sb(c, nc, name + "_m", [P, EU, P])
        cm = sb(c, nc, name + "_cm", [P, EU, P])
        res = sb(c, nc, name + "_res", [P, EU, D])
        pa = [ps(c, nc, f"{name}_pa{k}", [P, 512]) for k in range(EU)]
        k_in = [sem(c, nc, f"{name}_k_in{k}") for k in range(EU)]
        g_in = [sem(c, nc, f"{name}_g_in{k}") for k in range(EU)]
        r_out = [sem(c, nc, f"{name}_r_out{k}") for k in range(EU)]
        s_ig = sem(c, nc, name + "_s_ig")
        s_m = sem(c, nc, name + "_s_m")
        s_sum = sem(c, nc, name + "_s_sum")
        s_res = sem(c, nc, name + "_s_res")
        s_zero = sem(c, nc, name + "_s_zero")
        tick = sem(c, nc, name + "_tick")
        rows_work = guest(c, nc, T, C) if guest else None
        block = c.enter_context(nc.Block())
        turns = ET // EU

        def edge_tiles(eng, edge_tile, row_step):
            def turn(g, b, u, used, more=True):
                for k in range(EU):
                    edge_tile(g, k)
                    row_step(eng, g, b, u, k, more)

            if rows_work is not None:
                ahead(eng, lambda *a: None, turn, None, lambda *a: turn(*a, more=False))
            with eng.Fori(G if rows_work is not None else 0, turns) as t:
                for k in range(EU):
                    edge_tile(t, k)

        @block.sync
        def _(sp):
            def load_keys(t, k):
                sp.wait_ge(s_m, t * EU + k + 1)
                sp.dma_start(keys[:, k, :], T["keys"][bass.ds((t * EU + k) * P, P)].partition_broadcast(P))\
                    .then_inc(k_in[k], 16)

            sp.wait_ge(s_zero, 1)
            if rows_work:
                rows_work.sync_begin(sp)
            edge_tiles(sp, load_keys, rows_work and rows_work.sync_step)

        @block.gpsimd
        def _(pool):
            def gather(k, i):
                wait_all(pool, tick, (s_ig, i + 1), (s_sum, i + 1))
                pool.indirect_dma_start(msg[:, k, :], None, table, bass.IndirectOffsetOnAxis(ap=ig[:, k:k + 1], axis=0),
                                        bounds_check=NP - 1, oob_is_err=False).then_inc(g_in[k], 16)

            for i in range(AHEAD):
                gather(i, i)
            with pool.Fori(0, turns) as t:
                for k in range(EU):
                    gather((k + AHEAD) % EU, t * EU + k + AHEAD)
                    wait_all(pool, tick, (s_res, t * EU + k + 1))
                    pool.indirect_dma_start(T["agg"], bass.IndirectOffsetOnAxis(ap=io[:, k:k + 1], axis=0), res[:, k, :], None,
                                            bounds_check=NP - 1, oob_is_err=False).then_inc(r_out[k], 16)
            for k in range(EU):
                pool.wait_ge(r_out[k], 16 * turns)
                pool.wait_ge(g_in[k], 16 * (turns + (k < AHEAD)))

        @block.scalar
        def _(act):
            def sources(k, i, uses):
                act.wait_ge(g_in[k], uses)
                act.copy(ig[:, k:k + 1], C["src_i"][:, bass.ds(i, 1)]).then_inc(s_ig, 1)

            for i in range(AHEAD):
                sources(i, i, 0)

            def results(t, k):
                sources((k + AHEAD) % EU, t * EU + k + AHEAD, (t + (k + AHEAD) // EU) * 16)
                act.wait_ge(r_out[k], t * 16)
                act.copy(io[:, k:k + 1], C["out_i"][:, bass.ds(t * EU + k, 1)])
                act.wait_ge(s_sum, t * EU + k + 1 + EU)
                act.copy(res[:, k, :], pa[k][:, 0:D]).then_inc(s_res, 1)

            edge_tiles(act, results, rows_work and rows_work.scalar_step)

        @block.tensor
        def _(pe):
            pe.wait_ge(s_zero, 1)
            pe.sem_inc(s_sum, EU)

            def products(t, k):
                i = t * EU + k
                pe.wait_ge(g_in[k], t * 16 + 16)
                pe.wait_ge(s_m, i + 1 + EU)
                pe.matmul(pa[k][:, 0:D], m[:, k, :], msg[:, k, :], start=True, stop=False)
                pe.wait_ge(s_res, i)
                pe.matmul(pa[k][:, 0:D], cm[:, k, :], res[:, (k - 1) % EU, :], start=False, stop=True).then_inc(s_sum, 1)

            if rows_work:
                rows_work.tensor_begin(pe)
            edge_tiles(pe, products, rows_work and rows_work.tensor_step)
            if rows_work:
                rows_work.tensor_end(pe)

        @block.vector
        def _(v):
            v.memset(res[:, EU - 1, :], 0.0).then_inc(s_zero, 1)
            v.sem_inc(s_m, EU)

            def matrices(t, k):
                i = t * EU + k
                v.wait_ge(k_in[k], t * 16 + 16)
                v.wait_ge(s_sum, i + 1)
                if h == 1:
                    v.tensor_scalar(m[:, k, :], keys[:, k, :], C["dst_f"][:, bass.ds(i, 1)],
                                    w_tile[:, bass.ds(i, 1), :].rearrange("p o h -> p (o h)"), ALU.is_equal, ALU.mult)
                else:
                    v.tensor_scalar(m[:, k, :], keys[:, k, :], C["dst_f"][:, bass.ds(i, 1)], None, ALU.is_equal)
                    v.wait_ge(g_in[k], t * 16 + 16)
                    rows_k = msg[:, k, :].rearrange("p (h f) -> p h f", h=h)
                    v.tensor_tensor(rows_k, rows_k, w_tile[:, bass.ds(i, 1), :].rearrange("p o h -> p (o h)")
                                    .unsqueeze(2).to_broadcast([P, h, D // h]), ALU.mult)
                v.tensor_scalar(cm[:, k, :], keys[:, k, :], C["carry_f"][:, bass.ds(i, 1)], None, ALU.is_equal)\
                    .then_inc(s_m, 1)

            if rows_work:
                rows_work.vector_begin(v)
            edge_tiles(v, matrices, rows_work and rows_work.vector_step)
            if rows_work:
                rows_work.vector_end(v)


def ahead(eng, start, body, begun=None, last=None):
    start(0, 0, 0)
    start(1, 1, 0)
    if begun is not None:
        begun()
    with eng.Fori(0, G // 2 - 1) as u:
        for b in range(2):
            start(u * 2 + b + 2, b, u + 1)
            body(u * 2 + b, b, u, P)
    for b in range(2):
        (last or body)(G - 2 + b, b, G // 2 - 1, (P, LAST_P)[b])


def staggered(update, middle, finish, eng):
    update(0, 0, 0)
    update(1, 1, 0)
    middle(0, 0)
    with eng.Fori(0, G // 2 - 1) as u:
        for b in range(2):
            g = u * 2 + b
            update(g + 2, b, u + 1, g)
            middle(g + 1, 1 - b)
    finish(G - 2)
    middle(G - 1, 1)
    finish(G - 1)


def cols(tile, g):
    return tile[:, bass.ds(g * J, J)]


def update_and_gate(nc, T, C):
    with Stage(nc) as c:
        x_t = sb(c, nc, "b_x", [P, 2, J, D])
        xn_t = sb(c, nc, "b_xn", [P, 2, J, D])
        ag_t = sb(c, nc, "b_ag", [P, 2, J, D])
        x1_t = sb(c, nc, "b_x1", [P, 2, J, D])
        xl_t = sb(c, nc, "b_xl", [P, 2, J, D])
        tr_t = sb(c, nc, "b_tr", [P, 2, 4, P])
        lt_t = sb(c, nc, "b_lt", [P, 2, 4, P])
        gate = sb(c, nc, "b_gate", [P, KC, EXPERTS])
        gb = sb(c, nc, "b_gb", [P, EXPERTS])
        br = sb(c, nc, "b_br", [P, D])
        ev = sb(c, nc, "b_ev", [P, 2, EXPERTS])
        stats = sb(c, nc, "b_stats", [P, J, 6])
        mv = sb(c, nc, "b_mv", [P, J, 2])
        ve = sb(c, nc, "b_ve", [P, J])
        nt = sb(c, nc, "b_nt", [P, J])
        rs = sb(c, nc, "b_rs", [P, J])
        lg = sb(c, nc, "b_lg", [P, J, EXPERTS])
        rk = sb(c, nc, "b_rk", [P, J, EXPERTS])
        oh = sb(c, nc, "b_oh", [P, J, EXPERTS])
        cum = sb(c, nc, "b_cum", [P, J + 1, EXPERTS])
        run = sb(c, nc, "b_run", [P, EXPERTS])
        m4 = sb(c, nc, "b_m4", [P, 5, J])
        io = sb(c, nc, "b_io", [P, 2, J], I32)
        pt = [ps(c, nc, f"b_pt{n}", [P, 4, P]) for n in range(2)]
        px = [ps(c, nc, f"b_px{b}", [P, J, D]) for b in range(2)]
        pl = ps(c, nc, "b_pl", [P, 4, P])
        pg = ps(c, nc, "b_pg", [P, 512])
        pgate = pg[:, 0:J * EXPERTS].rearrange("p (j e) -> p j e", e=EXPERTS)
        ppre = pg[:, 64:64 + EXPERTS]
        ins = [sem(c, nc, f"b_ins{b}") for b in range(2)]
        outs = [sem(c, nc, f"b_outs{b}") for b in range(2)]
        sent = [sem(c, nc, f"b_sent{b}") for b in range(2)]
        s_par = sem(c, nc, "b_par")
        s_pt = sem(c, nc, "b_s_pt")
        s_tr = sem(c, nc, "b_s_tr")
        s_mm = sem(c, nc, "b_s_mm")
        s_x1 = sem(c, nc, "b_s_x1")
        s_xl = sem(c, nc, "b_s_xl")
        s_pl = sem(c, nc, "b_s_pl")
        s_lt = sem(c, nc, "b_s_lt")
        s_gate = sem(c, nc, "b_s_gate")
        s_tot = sem(c, nc, "b_s_tot")
        s_pre = sem(c, nc, "b_s_pre")
        s_io = sem(c, nc, "b_s_io")
        s_init = sem(c, nc, "b_s_init")
        st1 = sem(c, nc, "b_step1")
        st2 = sem(c, nc, "b_step2")
        st3 = sem(c, nc, "b_step3")
        tick = sem(c, nc, "b_tick")
        block = c.enter_context(nc.Block())

        @block.sync
        def _(sp):
            sp.dma_start(gate[:, :, :], T["gate_w"].rearrange("(c p) e -> p c e", p=P)).then_inc(s_par, 16)
            sp.dma_start(gb[:, :], T["gate_b"].partition_broadcast(P)).then_inc(s_par, 16)
            sp.dma_start(br[:, :], T["b_r"].partition_broadcast(P)).then_inc(s_par, 16)
            sp.dma_start(ev[:, :, :], T["c_experts"]).then_inc(s_par, 16)

            def load(g, b, u):
                sp.wait_ge(s_x1, g + 1)
                for t, name in ((x_t, "x"), (xn_t, "xn"), (ag_t, "agg")):
                    sp.dma_start(t[:, b], rows(T[name], g)).then_inc(ins[b], 16)

            def store(g, b, u, used):
                sp.wait_ge(s_x1, g + 3)
                sp.dma_start(rows(T["x1"], g), x1_t[:, b]).then_inc(outs[b], 16)

            ahead(sp, load, store)
            for b in range(2):
                sp.wait_ge(outs[b], 16 * (G // 2))

        @block.gpsimd
        def _(pool):
            def scatter(g, b, u, used):
                wait_all(pool, tick, (s_io, g + 1))
                for j in range(J):
                    pool.indirect_dma_start(T["slots"], bass.IndirectOffsetOnAxis(ap=io[:, b, j:j + 1], axis=0),
                                            xl_t[:, b, j, :], None, bounds_check=EXPERTS * MROWS - 1,
                                            oob_is_err=False).then_inc(sent[b], 16)

            ahead(pool, lambda *a: None, scatter)
            for b in range(2):
                pool.wait_ge(sent[b], 16 * J * (G // 2))

        @block.tensor
        def _(pe):
            pe.wait_ge(s_par, 64)
            pe.sem_inc(s_mm, 2)

            def update(g, b, u, counted=None):
                pe.wait_ge(ins[b], u * 48 + 48)
                pe.wait_ge(s_x1, g + 1)
                for j in range(J + 1):
                    if j < J:
                        pe.wait_ge(s_tr, g * J + j + 1)
                        for k in range(4):
                            src = (xn_t, ag_t)[k // 2]
                            i = pe.transpose(pt[j % 2][:, k, :], src[:, b, j, (k % 2) * P:(k % 2 + 1) * P],
                                             C["ident"][:, :])
                        i.then_inc(s_pt, 1)
                    if j > 0:
                        pe.wait_ge(s_tr, g * J + j + 2)
                        for k in range(4):
                            w = (C["wr"], C["wl"])[k // 2]
                            i = pe.matmul(px[b][:, j - 1, :], tr_t[:, (j - 1) % 2, k, :], w[:, k % 2, :],
                                          start=(k == 0), stop=(k == 3))
                        i.then_inc(s_mm, 1)
                    if j == 2 and counted is not None:
                        before(counted)

            def before(g):
                pe.wait_ge(s_tot, g + 1)
                pe.matmul(ppre, C["tri"][:, :], cum[:, J, :], start=True, stop=False)
                pe.matmul(ppre, C["ones"][:, :], run[:, :], start=False, stop=True).then_inc(s_pre, 1)

            def logits(g, b):
                pe.wait_ge(s_xl, g + 1)
                pe.wait_ge(s_io, g)
                for h in range(2):
                    pe.wait_ge(s_lt, g * 2 + h + 1)
                    for k in range(4):
                        i = pe.transpose(pl[:, k, :], xl_t[:, b, 2 * h + k // 2, (k % 2) * P:(k % 2 + 1) * P],
                                         C["ident"][:, :])
                    i.then_inc(s_pl, 1)
                    pe.wait_ge(s_lt, g * 2 + h + 2)
                    for k in range(4):
                        i = pe.matmul(pgate[:, 2 * h + k // 2, :], lt_t[:, h, k, :], gate[:, k % 2, :],
                                      start=(k % 2 == 0), stop=(k % 2 == 1))
                i.then_inc(s_gate, 1)

            staggered(update, logits, before, pe)
            pe.wait_ge(s_io, G)
            pe.matmul(ppre, C["ones"][:, :], run[:, :], start=True, stop=True).then_inc(s_pre, 1)

        @block.scalar
        def _(act):
            act.sem_inc(s_tr, 2)
            act.sem_inc(s_lt, 1)

            def update(g, b, u, counted=None):
                for j in range(J):
                    act.wait_ge(s_pt, g * J + j + 1)
                    act.wait_ge(s_mm, g * J + j + 1)
                    act.copy(tr_t[:, j % 2], pt[j % 2][:, :, :]).then_inc(s_tr, 1)

            def logits(g, b):
                for h in range(2):
                    act.wait_ge(s_pl, g * 2 + h + 1)
                    act.copy(lt_t[:, h], pl[:, :, :]).then_inc(s_lt, 1)

            staggered(update, logits, lambda g: None, act)

        @block.vector
        def _(v):
            step = Steps(v, s_init)
            step.then(v.memset(cum[:, :, :], 0.0))
            step.then(v.memset(run[:, :], 0.0))
            v.wait_ge(s_par, 64)
            v.sem_inc(s_x1, 2)

            def update(g, b, u, counted=None):
                if counted is not None:
                    places(counted, b)
                step = Steps(v, st1, g, 4 + 10)
                x1, xl = x1_t[:, b], xl_t[:, b]
                v.wait_ge(s_mm, g * J + J + 2)
                v.wait_ge(outs[b], u * 16)
                step.then(v.tensor_tensor(x1, px[b][:, :, :], x_t[:, b], ALU.add))
                v.tensor_tensor(x1, x1, br[:, :].unsqueeze(1).to_broadcast([P, J, D]), ALU.add).then_inc(s_x1, 1)
                v.wait_ge(s_x1, g + 3)
                step.then(row_mean_var(v, step, tick, x1, stats, mv, ve[:, :]))
                inverse_root(v, step, rs, ve, nt)
                v.wait_ge(sent[b], u * 16 * J)
                for j in range(J):
                    i = v.tensor_scalar(xl[:, j, :], x1[:, j, :], mv[:, j, 0:1], rs[:, j:j + 1],
                                        ALU.subtract, ALU.mult)
                i.then_inc(s_xl, 1)
                step.end()

            wide = [P, J, EXPERTS]
            pos, base, kept, slot, far = (m4[:, n, :] for n in range(5))

            def choose(g, b):
                step = Steps(v, st2, g, 10)
                v.wait_ge(s_gate, g + 1)
                step.then(v.tensor_tensor(lg[:, :, :], pgate, gb[:, :].unsqueeze(1).to_broadcast(wide), ALU.add))
                step.then(v.tensor_reduce(pos, lg[:, :, :], AX.X, ALU.max))
                step.then(v.tensor_tensor(lg[:, :, :], lg[:, :, :], pos.unsqueeze(2).to_broadcast(wide), ALU.subtract))
                v.tensor_copy(C["gap"][:, bass.ds(g * J, J), :], lg[:, :, :])
                step.then(v.scalar_tensor_tensor(rk[:, :, :], lg[:, :, :], 0.0, ev[:, 0, :].unsqueeze(1).to_broadcast(wide),
                                                 ALU.is_equal, ALU.mult))
                step.then(v.tensor_reduce(base, rk[:, :, :], AX.X, ALU.max))
                step.then(v.tensor_tensor(oh[:, :, :], rk[:, :, :], base.unsqueeze(2).to_broadcast(wide), ALU.is_equal))
                step.then(v.tensor_scalar(oh[:, :, :], oh[:, :, :], C["valid"][:, bass.ds(g, 1)], None, ALU.mult))
                for j in range(J - 1):
                    step.then(v.tensor_tensor(cum[:, j + 1, :], cum[:, j, :], oh[:, j, :], ALU.add))
                v.tensor_tensor(cum[:, J, :], cum[:, J - 1, :], oh[:, J - 1, :], ALU.add).then_inc(s_tot, 1)
                step.end()

            def places(g, b):
                step = Steps(v, st3, g, 6)
                v.wait_ge(s_pre, g + 1)
                v.tensor_tensor(run[:, :], run[:, :], cum[:, J, :], ALU.add)
                step.then(v.tensor_tensor(rk[:, :, :], cum[:, 0:J, :], ppre.unsqueeze(1).to_broadcast(wide), ALU.add))
                step.then(v.tensor_tensor(rk[:, :, :], rk[:, :, :], oh[:, :, :], ALU.mult))
                v.tensor_reduce(pos, rk[:, :, :], AX.X, ALU.add)
                step.then(v.tensor_tensor(lg[:, :, :], oh[:, :, :], ev[:, 1, :].unsqueeze(1).to_broadcast(wide), ALU.mult))
                step.then(v.tensor_reduce(base, lg[:, :, :], AX.X, ALU.add))
                step.then(v.tensor_scalar(kept, pos, float(CAP), C["valid"][:, bass.ds(g, 1)], ALU.is_lt, ALU.mult))
                v.tensor_tensor(slot, pos, base, ALU.add)
                v.tensor_copy(cols(C["kept"], g), kept)
                step.then(v.tensor_scalar(far, kept, -FAR, FAR, ALU.mult, ALU.add))
                v.tensor_tensor(cols(C["from"], g), slot, kept, ALU.mult)
                v.tensor_tensor(io[:, b, :], slot, far, ALU.add).then_inc(s_io, 1)
                step.end()

            staggered(update, choose, lambda g: places(g, g % 2), v)
            v.wait_ge(s_pre, G + 1)
            v.tensor_copy(C["tokens"][:, :], ppre)


def two_layers(nc, T, C, name, experts, pairs, tail_block, r, width, source, w1_d, b1_d, w2_d, b2_d, func, store, out_d):
    n_blocks = 2 * pairs + tail_block
    total = experts * n_blocks
    assert total % 2 == 0
    slots_w = min(experts, 2)
    FC = FF // P
    with Stage(nc) as c:
        xe = sb(c, nc, name + "_xe", [r, 2, J, width])
        w1 = sb(c, nc, name + "_w1", [P, slots_w, KC, FF])
        w2 = sb(c, nc, name + "_w2", [P, slots_w, FC, D])
        b1 = sb(c, nc, name + "_b1", [P, slots_w, FC])
        b2 = sb(c, nc, name + "_b2", [P, slots_w, D])
        xt = sb(c, nc, name + "_xt", [P, KC, J * r])
        ht = sb(c, nc, name + "_ht", [P, FC, J * r])
        yt = sb(c, nc, name + "_yt", [r, 2, J, D])
        io = sb(c, nc, name + "_io", [r, 2, J], I32)
        pxt = ps(c, nc, name + "_pxt", [P, KC, 512])
        ph = [ps(c, nc, f"{name}_ph{n}", [P, 512]) for n in range(2)]
        py = [ps(c, nc, f"{name}_py{b}", [P, J, D]) for b in range(2)]
        w_in = [sem(c, nc, f"{name}_w_in{n}") for n in range(slots_w)]
        x_in = [sem(c, nc, f"{name}_x_in{b}") for b in range(2)]
        y_out = [sem(c, nc, f"{name}_y_out{b}") for b in range(2)]
        s_pt = sem(c, nc, name + "_s_pt")
        s_xt = sem(c, nc, name + "_s_xt")
        s_h = sem(c, nc, name + "_s_h")
        s_ht = sem(c, nc, name + "_s_ht")
        s_y = sem(c, nc, name + "_s_y")
        s_yt = sem(c, nc, name + "_s_yt")
        s_go = sem(c, nc, name + "_s_go")
        s_step = sem(c, nc, name + "_step")
        tick = sem(c, nc, name + "_tick")
        block = c.enter_context(nc.Block())
        block_rows = J * r

        def blocks(eng, body):
            if experts == 1:
                with eng.Fori(0, pairs) as i:
                    for s in range(2):
                        body(i * 2 + s, s, i, 0, 0, i * 2 + s)
                return
            with eng.Fori(0, experts // 2) as ep:
                for par in range(2):
                    def at(i, s):
                        k = n_blocks * par + s
                        body(ep * (2 * n_blocks) + i * 2 + k, k % 2, ep * n_blocks + i + k // 2, par, ep, i * 2 + s)
                    with eng.Fori(0, pairs) as i:
                        for s in range(2):
                            at(i, s)
                    if tail_block:
                        at(pairs, 0)

        def source_rows(n):
            return source[bass.ds(n * block_rows, block_rows), :].rearrange("(p j) d -> p j d", j=J)

        def load_weights(eng, e, slot):
            for out, in_ in ((w1[:, slot], w1_d[e].rearrange("(c p) f -> p c f", p=P)),
                             (w2[:, slot], w2_d[e].rearrange("(c p) d -> p c d", p=P)),
                             (b1[:, slot], b1_d[e]), (b2[:, slot], b2_d[e].partition_broadcast(P))):
                eng.dma_start(out, in_).then_inc(w_in[slot], 16)

        @block.sync
        def _(sp):
            sp.dma_start(xe[:, 0], source_rows(0)).then_inc(x_in[0], 16)

            def body(n, b, u, slot, e, w):
                if store:
                    sp.wait_ge(s_pt, n)
                else:
                    sp.wait_ge(s_yt, n + 2)
                o = 1 - b
                sp.dma_start(xe[:, o], source_rows(n + 1)).then_inc(x_in[o], 16)
                if store:
                    sp.wait_ge(s_yt, n + 3)
                    sp.dma_start(out_d[bass.ds(n * block_rows, block_rows), :].rearrange("(p j) d -> p j d", j=J), yt[:, b])\
                        .then_inc(y_out[b], 16)

            blocks(sp, body)
            sp.wait_ge(x_in[0], 16 * (total // 2 + 1))
            if store:
                for b in range(2):
                    sp.wait_ge(y_out[b], 16 * (total // 2))

        @block.gpsimd
        def _(pool):
            for n in range(slots_w):
                load_weights(pool, n, n)
            if experts > 1:
                with pool.Fori(0, experts // 2 - 1) as ep:
                    for par in range(2):
                        done = ep * (2 * n_blocks) + n_blocks * (par + 1)
                        wait_all(pool, tick, (s_y, done), (s_yt, done + 2))
                        e = ep * 2 + par + 2
                        for out, in_ in ((w1[:, par], w1_d[bass.ds(e, 1)].rearrange("o (c p) f -> p (o c) f", p=P)),
                                         (w2[:, par], w2_d[bass.ds(e, 1)].rearrange("o (c p) d -> p (o c) d", p=P)),
                                         (b1[:, par], b1_d[bass.ds(e, 1)].rearrange("o p f -> p (o f)")),
                                         (b2[:, par], b2_d[bass.ds(e, 1)].rearrange("o d -> (o d)").partition_broadcast(P))):
                            pool.dma_start(out, in_).then_inc(w_in[par], 16)
            if not store:
                def body(n, b, u, slot, e, w):
                    wait_all(pool, tick, (s_yt, n + 3))
                    for j in range(J):
                        pool.indirect_dma_start(out_d, bass.IndirectOffsetOnAxis(ap=io[:, b, j:j + 1], axis=0), yt[:, b, j, :],
                                                None, bounds_check=NP - 1, oob_is_err=False).then_inc(y_out[b], 16)

                blocks(pool, body)
                for b in range(2):
                    pool.wait_ge(y_out[b], 16 * J * (total // 2))

        @block.tensor
        def _(pe):
            def turn(b):
                for k in range(KC):
                    for j in range(J):
                        i = pe.transpose(pxt[:, k, j * r:(j + 1) * r], xe[:, b, j, k * P:(k + 1) * P], C["ident"][0:r, 0:r])
                i.then_inc(s_pt, 1)

            def first_layer(n, slot):
                for f in range(FC):
                    pe.wait_ge(s_ht, n * FC + f + 1)
                    for k in range(KC):
                        i = pe.matmul(ph[f % 2][:, 0:J * r], w1[:, slot, k, f * P:(f + 1) * P], xt[:, k, :],
                                      start=(k == 0), stop=(k == KC - 1))
                    i.then_inc(s_h, 1)

            def second_layer(n, b, slot):
                for j in range(J):
                    for f in range(FC):
                        if j == 0:
                            pe.wait_ge(s_ht, n * FC + f + 3)
                        i = pe.matmul(py[b][0:r, j, :], ht[:, f, j * r:(j + 1) * r], w2[:, slot, f, :],
                                      start=(f == 0), stop=(f == FC - 1))
                i.then_inc(s_y, 1)

            pe.wait_ge(x_in[0], 16)
            turn(0)
            pe.wait_ge(s_go, 1)

            def body(n, b, u, slot, e, w):
                wait_all(pe, tick, (s_xt, n + 1), (w_in[slot], e * 64 + 64 if experts > 1 else 64))
                if experts > 1:
                    tokens = pe.value_load(C["tokens"][0:1, bass.ds(e * 2 + slot, 1)], min_val=0, max_val=N)
                    with pe.If(w * block_rows < tokens):
                        first_layer(n, slot)
                    with pe.Else():
                        for f in range(FC):
                            pe.wait_ge(s_ht, n * FC + f + 1)
                            pe.sem_inc(s_h, 1)
                else:
                    first_layer(n, slot)
                pe.wait_ge(x_in[1 - b], (u + b) * 16 + 16)
                turn(1 - b)
                pe.wait_ge(s_yt, n + 1)
                if experts > 1:
                    with pe.If(w * block_rows < tokens):
                        second_layer(n, b, slot)
                    with pe.Else():
                        pe.wait_ge(s_ht, n * FC + FC + 2)
                        pe.sem_inc(s_y, 1)
                else:
                    second_layer(n, b, slot)

            blocks(pe, body)

        @block.scalar
        def _(act):
            act.sem_inc(s_ht, 2)

            def body(n, b, u, slot, e, w):
                act.wait_ge(s_pt, n + 1)
                act.copy(xt[:, :, :], pxt[:, :, 0:J * r]).then_inc(s_xt, 1)
                for f in range(FC):
                    act.wait_ge(s_h, n * FC + f + 1)
                    if f == 0:
                        act.wait_ge(s_y, n)
                    act.activation(ht[:, f, :], ph[f % 2][:, 0:J * r], func, bias=b1[:, slot, f:f + 1]).then_inc(s_ht, 1)

            blocks(act, body)

        @block.vector
        def _(v):
            for t in (*ph, *py):
                i = v.memset(t[:, :] if t in ph else t[:, :, :], 0.0)
            i.then_inc(s_go, 1)
            v.sem_inc(s_yt, 2)

            def body(n, b, u, slot, e, w):
                y = yt[:, b]
                v.wait_ge(s_y, n + 1)
                v.wait_ge(y_out[b], u * 16 * (1 if store else J))
                bias = b2[0:r, slot, :].unsqueeze(1).to_broadcast([r, J, D])
                if store:
                    v.tensor_tensor(y, py[b][0:r, :, :], bias, ALU.add).then_inc(s_yt, 1)
                else:
                    step = Steps(v, s_step, n, 1)
                    step.then(v.tensor_tensor(y, py[b][0:r, :, :], bias, ALU.add))
                    for j in range(J):
                        v.scalar_tensor_tensor(y[:, j, :], y[:, j, :], xe[:, b, j, 2 * D:2 * D + 1], xe[:, b, j, D:2 * D],
                                               ALU.mult, ALU.add)
                    v.tensor_copy(io[:, b, :], xe[:, b, :, 2 * D + 1].bitcast(I32)).then_inc(s_yt, 1)

            blocks(v, body)


def combine_and_project(nc, T, C):
    SC = 2 * GH
    with Stage(nc) as c:
        x1_t = sb(c, nc, "d_x1", [P, 2, J, D])
        yg_t = sb(c, nc, "d_yg", [P, 2, J, D])
        xl_t = sb(c, nc, "d_xl", [P, 2, J, D])
        fin = sb(c, nc, "d_fin", [P, J, D], I32)
        sg = sb(c, nc, "d_sg", [P, J, D])
        neg = sb(c, nc, "d_neg", [P, J, D])
        io = sb(c, nc, "d_io", [P, 2, J], I32)
        tr_t = sb(c, nc, "d_tr", [P, 2, KC, P])
        wh = sb(c, nc, "d_wh", [P, KC, D + SC])
        w1n = sb(c, nc, "d_w1n", [P, KC, D])
        aa = sb(c, nc, "d_aa", [P, KC, SC])
        hp_t = sb(c, nc, "d_hp", [P, 2, J, D])
        sc_t = sb(c, nc, "d_sc", [P, 2, J, SC])
        gap = C["gap"]
        stats = sb(c, nc, "d_stats", [P, J, 6])
        mv = sb(c, nc, "d_mv", [P, J, 2])
        ve = sb(c, nc, "d_ve", [P, J])
        rs = sb(c, nc, "d_rs", [P, J])
        nt = sb(c, nc, "d_nt", [P, J])
        nb = sb(c, nc, "d_nb", [P, J])
        pt = ps(c, nc, "d_pt", [P, KC, P])
        php = [ps(c, nc, f"d_php{n}", [P, 512]) for n in range(2)]
        ins = [sem(c, nc, f"d_ins{b}") for b in range(2)]
        got = [sem(c, nc, f"d_got{b}") for b in range(2)]
        x2o = [sem(c, nc, f"d_x2o{b}") for b in range(2)]
        xno = [sem(c, nc, f"d_xno{b}") for b in range(2)]
        pro = [sem(c, nc, f"d_pro{b}") for b in range(2)]
        s_par = sem(c, nc, "d_par")
        s_init = sem(c, nc, "d_init")
        s_aw = sem(c, nc, "d_s_aw")
        s_wh = sem(c, nc, "d_s_wh")
        s_ex = sem(c, nc, "d_s_ex")
        s_wt = sem(c, nc, "d_s_wt")
        s_io = sem(c, nc, "d_s_io")
        s_z = sem(c, nc, "d_s_z")
        s_x2 = sem(c, nc, "d_s_x2")
        s_rs = sem(c, nc, "d_s_rs")
        s_xl = sem(c, nc, "d_s_xl")
        s_pt = sem(c, nc, "d_s_pt")
        s_tr = sem(c, nc, "d_s_tr")
        s_mm = sem(c, nc, "d_s_mm")
        s_hp = sem(c, nc, "d_s_hp")
        st1 = sem(c, nc, "d_step1")
        st2 = sem(c, nc, "d_step2")
        tick = sem(c, nc, "d_tick")
        block = c.enter_context(nc.Block())
        n_par = 3

        @block.sync
        def _(sp):
            for out, in_ in ((wh[:, :, 0:D], T["W1_t"].rearrange("(c p) n -> p c n", p=P)),
                             (w1n[:, :, :], T["W1"].rearrange("(c p) n -> p c n", p=P)),
                             (aa[:, :, :], T["a1"].rearrange("(c p) n -> p c n", p=P))):
                sp.dma_start(out, in_).then_inc(s_par, 16)

            def load(g, b, u):
                wait_all(sp, tick, (x2o[b], u * 16))
                sp.wait_ge(s_xl, g + 1)
                sp.dma_start(x1_t[:, b], rows(T["x1"], g)).then_inc(ins[b], 16)

            def store_x2(g, b):
                sp.wait_ge(s_x2, g + 3)
                sp.dma_start(rows(T["x2"], g), x1_t[:, b]).then_inc(x2o[b], 16)

            def store(g, b, u, used):
                sp.wait_ge(s_xl, g + 3)
                sp.dma_start(rows(T["xn"], g), xl_t[:, b]).then_inc(xno[b], 16)
                if used == P:
                    store_x2(g + 1, 1 - b)
                sp.wait_ge(s_hp, g * J + J + 2)
                sp.dma_start(rows(T["hp"], g), hp_t[:, b]).then_inc(pro[b], 16)
                sp.dma_start(rows(T["sc1"], g), sc_t[:, b]).then_inc(pro[b], 16)

            ahead(sp, load, store, lambda: store_x2(0, 0))
            for b in range(2):
                sp.wait_ge(x2o[b], 16 * (G // 2))
                sp.wait_ge(xno[b], 16 * (G // 2))
                sp.wait_ge(pro[b], 32 * (G // 2))

        @block.gpsimd
        def _(pool):
            def gather(g, b, u):
                wait_all(pool, tick, (s_io, g + 1), (s_x2, g + 1))
                for j in range(J):
                    pool.indirect_dma_start(yg_t[:, b, j, :], None, T["y"],
                                            bass.IndirectOffsetOnAxis(ap=io[:, b, j:j + 1], axis=0),
                                            bounds_check=EXPERTS * MROWS - 1, oob_is_err=False).then_inc(got[b], 16)

            ahead(pool, gather, lambda *a: None)

        @block.tensor
        def _(pe):
            pe.wait_ge(s_par, 16 * n_par)
            for k in range(KC):
                for n in range(KC):
                    i = pe.matmul(php[k][:, 0:SC], w1n[:, n, k * P:(k + 1) * P], aa[:, n, :], start=(n == 0), stop=(n == KC - 1))
            i.then_inc(s_aw, 1)
            pe.wait_ge(s_wh, 1)
            pe.sem_inc(s_mm, 2)

            def turn(i, g, b, j):
                if j == 0:
                    pe.wait_ge(s_xl, g + 3)
                pe.wait_ge(s_tr, i + 1)
                for k in range(KC):
                    o = pe.transpose(pt[:, k, :], xl_t[:, b, j, k * P:(k + 1) * P], C["ident"][:, :])
                o.then_inc(s_pt, 1)

            turn(0, 0, 0, 0)

            def project(g, b, u, used):
                for j in range(J):
                    i, s = g * J + j, j % 2
                    if j < J - 1:
                        turn(i + 1, g, b, j + 1)
                    pe.wait_ge(s_tr, i + 2)
                    pe.wait_ge(s_hp, i + 1)
                    for k in range(KC):
                        o = pe.matmul(php[s][:, 0:D + SC], tr_t[:, s, k, :], wh[:, k, :], start=(k == 0), stop=(k == KC - 1))
                    o.then_inc(s_mm, 1)
                    if j == J - 1 and used == P:
                        turn(i + 1, g + 1, 1 - b, 0)

            ahead(pe, lambda *a: None, project)

        @block.scalar
        def _(act):
            act.activation(gap[:, :, :], gap[:, :, :], ACT.Exp).then_inc(s_ex, 1)
            act.sem_inc(s_tr, 1)
            act.sem_inc(s_hp, 2)
            act.sem_inc(s_xl, 2)

            def first(g, b, u):
                act.wait_ge(got[b], u * 16 * J)
                act.copy(io[:, b, :], cols(C["from"], g)).then_inc(s_io, 1)

            def scale(g, b, u):
                act.wait_ge(got[b], u * 16 * J + 16 * J)
                for j in range(J):
                    o = act.mul(yg_t[:, b, j], yg_t[:, b, j], C["w"][:, bass.ds(g * J + j, 1)])
                o.then_inc(s_z, 1)

            def norm(g, b, u):
                act.wait_ge(xno[b], u * 16)
                act.wait_ge(s_rs, g + 1)
                for j in range(J):
                    o = act.activation(xl_t[:, b, j], x1_t[:, b, j], ACT.Identity, bias=nb[:, j:j + 1], scale=rs[:, j:j + 1])
                o.then_inc(s_xl, 1)

            def turned(i, s):
                act.wait_ge(s_pt, i + 1)
                act.wait_ge(s_mm, i + 1)
                act.copy(tr_t[:, s], pt[:, :, :]).then_inc(s_tr, 1)

            def begin():
                act.wait_ge(s_wt, 1)
                scale(0, 0, 0)
                scale(1, 1, 0)
                norm(0, 0, 0)
                turned(0, 0)

            def project(g, b, u, used, more=False):
                act.wait_ge(pro[b], u * 32)
                for j in range(J):
                    i, s = g * J + j, j % 2
                    if j < J - 1:
                        turned(i + 1, 1 - s)
                    act.wait_ge(s_mm, i + 3)
                    act.copy(hp_t[:, b, j], php[s][:, 0:D])
                    act.copy(sc_t[:, b, j], php[s][:, D:D + SC]).then_inc(s_hp, 1)
                if more:
                    scale(g + 2, b, u + 1)
                if used == P:
                    norm(g + 1, 1 - b, u + b)
                    turned(g * J + J, 0)

            ahead(act, first, lambda g, b, u, used: project(g, b, u, used, True), begin, project)

        @block.vector
        def _(v):
            step = Steps(v, s_init)
            v.wait_ge(s_aw, 1)
            for k in range(KC):
                i = v.tensor_copy(wh[:, k, D:D + SC], php[k][:, 0:SC])
            i.then_inc(s_wh, 1)
            v.wait_ge(s_ex, 1)
            step.then(v.tensor_reduce(C["w"][:, :], gap[:, :, :], AX.X, ALU.add))
            step.then(v.reciprocal(C["w"][:, :], C["w"][:, :]))
            v.tensor_tensor(C["w"][:, :], C["w"][:, :], C["kept"][:, :], ALU.mult).then_inc(s_wt, 1)
            v.sem_inc(s_x2, 2)

            def update(g, b, u):
                step = Steps(v, st1, g, 3)
                x, y = x1_t[:, b], yg_t[:, b]
                v.wait_ge(s_z, g + 1)
                v.tensor_scalar(neg[:, :, :], y, 0.0, -1.0e4, ALU.is_lt, ALU.mult)
                v.tensor_scalar(sg[:, :, :], y, 0.0, 1.0e4, ALU.is_gt, ALU.mult)
                step.then(v.tensor_scalar(fin[:, :, :], y, 0.0, 0.0, ALU.mult, ALU.is_equal))
                step.then(v.tensor_tensor(sg[:, :, :], sg[:, :, :], neg[:, :, :], ALU.add), tick)
                step.then(v.copy_predicated(sg[:, :, :], fin[:, :, :], y))
                v.wait_ge(ins[b], u * 16 + 16)
                v.tensor_tensor(x, x, sg[:, :, :], ALU.add).then_inc(s_x2, 1)
                step.end()

            def scales(g, b, u):
                step = Steps(v, st2, g, 2 + 1 + 1 + 9)
                v.wait_ge(s_x2, g + 3)
                v.wait_ge(s_xl, g + 2)
                step.then(row_mean_var(v, step, tick, x1_t[:, b], stats, mv, ve[:, :]))
                inverse_root(v, step, rs, ve, nt)
                v.scalar_tensor_tensor(nb[:, :], mv[:, :, 0], -1.0, rs[:, :], ALU.mult, ALU.mult).then_inc(s_rs, 1)
                step.end()

            with v.Fori(0, G // 2) as u:
                for b in range(2):
                    update(u * 2 + b, b, u)
                    scales(u * 2 + b, b, u)


def second_features(nc, T, C):
    SC = 2
    with Stage(nc) as c:
        ag_t = sb(c, nc, "f_ag", [P, 2, J, D])
        tr_t = sb(c, nc, "f_tr", [P, 2, KC, P])
        wh = sb(c, nc, "f_wh", [P, KC, D + SC])
        wn = sb(c, nc, "f_wn", [P, KC, D])
        aa = sb(c, nc, "f_aa", [P, KC, SC])
        hp_t = sb(c, nc, "f_hp", [P, 2, J, D])
        sc_t = sb(c, nc, "f_sc", [P, 2, J, SC])
        pt = [ps(c, nc, f"f_pt{n}", [P, KC, P]) for n in range(2)]
        php = [ps(c, nc, f"f_php{n}", [P, 512]) for n in range(2)]
        ins = [sem(c, nc, f"f_ins{b}") for b in range(2)]
        outs = [sem(c, nc, f"f_outs{b}") for b in range(2)]
        s_par = sem(c, nc, "f_par")
        s_aw = sem(c, nc, "f_s_aw")
        s_wh = sem(c, nc, "f_s_wh")
        s_pt = sem(c, nc, "f_s_pt")
        s_tr = sem(c, nc, "f_s_tr")
        s_mm = sem(c, nc, "f_s_mm")
        s_hp = sem(c, nc, "f_s_hp")
        block = c.enter_context(nc.Block())

        def groups(eng, body):
            with eng.Fori(0, G // 2) as u:
                for b in range(2):
                    body(u * 2 + b, b, u)

        @block.sync
        def _(sp):
            for out, in_ in ((wh[:, :, 0:D], T["W2_t"].rearrange("(c p) n -> p c n", p=P)),
                             (wn[:, :, :], T["W2"].rearrange("(c p) n -> p c n", p=P)),
                             (aa[:, :, :], T["a2"].rearrange("(c p) n -> p c n", p=P))):
                sp.dma_start(out, in_).then_inc(s_par, 16)

            def load(g, b, u):
                sp.wait_ge(s_hp, g * J + 1)
                sp.dma_start(ag_t[:, b], rows(T["agg"], g)).then_inc(ins[b], 16)

            def save(g, b, u):
                sp.wait_ge(s_hp, g * J + 3 * J)
                sp.dma_start(rows(T["hp"], g), hp_t[:, b]).then_inc(outs[b], 16)
                sp.dma_start(rows(T["sc2"], g), sc_t[:, b]).then_inc(outs[b], 16)

            load(0, 0, 0)
            load(1, 1, 0)
            with sp.Fori(0, G // 2 - 1) as u:
                for b in range(2):
                    save(u * 2 + b, b, u)
                    load(u * 2 + b + 2, b, u + 1)
            for b in range(2):
                save(G - 2 + b, b, G // 2 - 1)
            for b in range(2):
                sp.wait_ge(outs[b], 32 * (G // 2))

        @block.tensor
        def _(pe):
            pe.wait_ge(s_par, 48)
            for k in range(KC):
                for n in range(KC):
                    i = pe.matmul(php[k][:, 0:SC], wn[:, n, k * P:(k + 1) * P], aa[:, n, :], start=(n == 0), stop=(n == KC - 1))
            i.then_inc(s_aw, 1)
            pe.wait_ge(s_wh, 1)

            def body(g, b, u):
                pe.wait_ge(ins[b], u * 16 + 16)
                for j in range(J + 1):
                    i = g * J + j
                    if j < J:
                        pe.wait_ge(s_tr, i + 1)
                        for k in range(KC):
                            o = pe.transpose(pt[j % 2][:, k, :], ag_t[:, b, j, k * P:(k + 1) * P], C["ident"][:, :])
                        o.then_inc(s_pt, 1)
                    if j > 0:
                        s = (j - 1) % 2
                        pe.wait_ge(s_tr, i + 2)
                        pe.wait_ge(s_hp, i - 1 + 7)
                        for k in range(KC):
                            o = pe.matmul(php[s][:, 0:D + SC], tr_t[:, s, k, :], wh[:, k, :], start=(k == 0), stop=(k == KC - 1))
                        o.then_inc(s_mm, 1)

            groups(pe, body)

        @block.scalar
        def _(act):
            act.sem_inc(s_tr, 2)

            def body(g, b, u):
                for j in range(J):
                    i = g * J + j
                    act.wait_ge(s_pt, i + 1)
                    act.wait_ge(s_mm, i + 1)
                    act.activation(tr_t[:, j % 2], pt[j % 2][:, :, :], ACT.Relu).then_inc(s_tr, 1)

            groups(act, body)

        @block.vector
        def _(v):
            v.wait_ge(s_aw, 1)
            for k in range(KC):
                i = v.tensor_copy(wh[:, k, D:D + SC], php[k][:, 0:SC])
            i.then_inc(s_wh, 1)
            v.sem_inc(s_mm, 2)
            v.sem_inc(s_hp, 2 * J)

            def body(g, b, u):
                v.wait_ge(outs[b], u * 32)
                for j in range(J):
                    i = g * J + j
                    v.wait_ge(s_mm, i + 3)
                    v.tensor_copy(hp_t[:, b, j], php[j % 2][:, 0:D])
                    v.tensor_copy(sc_t[:, b, j], php[j % 2][:, D:D + SC]).then_inc(s_hp, 1)

            groups(v, body)


def second_update(nc, T, C):
    NB = 4
    assert G % NB == 0
    with Stage(nc) as c:
        x2_t = sb(c, nc, "g_x2", [P, NB, J, D])
        ag_t = sb(c, nc, "g_ag", [P, NB, J, D])
        row_t = sb(c, nc, "g_row", [P, NB, J, SW])
        wr = sb(c, nc, "g_wr", [P, D])
        br = sb(c, nc, "g_br", [P, 1])
        junk = sb(c, nc, "g_junk", [P, J, D])
        stats = sb(c, nc, "g_stats", [P, J, 6])
        mv = sb(c, nc, "g_mv", [P, 2, J, 2])
        ve = sb(c, nc, "g_ve", [P, 2, J])
        sd = sb(c, nc, "g_sd", [P, 2, J])
        rs = sb(c, nc, "g_rs", [P, J])
        wt = sb(c, nc, "g_wt", [P, J])
        ins = [sem(c, nc, f"g_ins{b}") for b in range(NB)]
        outs = [sem(c, nc, f"g_outs{b}") for b in range(NB)]
        names = ("par", "var", "std", "row", "st1", "st2")
        S = {n: sem(c, nc, "g_s_" + n) for n in names}
        tick = sem(c, nc, "g_tick")
        block = c.enter_context(nc.Block())

        @block.sync
        def _(sp):
            sp.dma_start(wr[:, :], T["ffn_wr"].rearrange("d o -> (d o)").partition_broadcast(P)).then_inc(S["par"], 16)
            sp.dma_start(br[:, :], T["ffn_br"].partition_broadcast(P)).then_inc(S["par"], 16)

            def load(g, b):
                for t, name in ((x2_t, "x2"), (ag_t, "agg")):
                    sp.dma_start(t[:, b], rows(T[name], g)).then_inc(ins[b], 16)

            def store(g, b):
                sp.wait_ge(S["row"], g + 1)
                sp.dma_start(rows(T["sel"], g), row_t[:, b]).then_inc(outs[b], 16)
                sp.dma_start(rows(T["out"], g), row_t[:, b, :, D:2 * D]).then_inc(outs[b], 16)

            for b in range(NB):
                load(b, b)
            with sp.Fori(0, G // NB - 1) as u:
                for b in range(NB):
                    store(u * NB + b, b)
                    load(u * NB + b + NB, b)
            for b in range(NB):
                store(G - NB + b, b)
            for b in range(NB):
                sp.wait_ge(outs[b], 32 * (G // NB))

        @block.scalar
        def _(act):
            with act.Fori(0, G // 2) as u:
                for b in range(2):
                    act.wait_ge(S["var"], u * 2 + b + 1)
                    act.activation(sd[:, b], ve[:, b], ACT.Sqrt).then_inc(S["std"], 1)

        @block.vector
        def _(v):
            v.wait_ge(S["par"], 32)

            def variance(g, b, u):
                step = Steps(v, S["st1"], g, 1 + 2)
                x = x2_t[:, b]
                v.wait_ge(ins[b], u * 32 + 32)
                step.then(v.tensor_tensor(x, x, ag_t[:, b], ALU.add))
                row_mean_var(v, step, tick, x, stats, mv[:, b % 2], ve[:, b % 2]).then_inc(S["var"], 1)
                step.end()

            def write(g, b, u):
                step = Steps(v, S["st2"], g, 4)
                x, row = x2_t[:, b], row_t[:, b]
                v.wait_ge(S["std"], g + 1)
                v.wait_ge(S["row"], g)
                step.then(v.reciprocal(rs[:, :], sd[:, b % 2]))
                v.wait_ge(outs[b], u * 32)
                for j in range(J):
                    i = v.tensor_scalar(row[:, j, 0:D], x[:, j, :], mv[:, b % 2, j, 0:1], rs[:, j:j + 1], ALU.subtract, ALU.mult)
                step.then(i)
                v.tensor_tensor(row[:, :, D:2 * D], x, row[:, :, 0:D], ALU.add)
                for j in range(J):
                    i = v.scalar_tensor_tensor(junk[:, j, :], row[:, j, 0:D], 1.0, wr[:, :], ALU.mult, ALU.mult,
                                               accum_out=wt[:, j:j + 1])
                step.then(i)
                step.then(v.tensor_scalar(wt[:, :], wt[:, :], br[:, 0:1], None, ALU.add))
                v.tensor_copy(cols(C["wsel"], g), wt[:, :])
                v.tensor_copy(row[:, :, 2 * D + 1].bitcast(I32), cols(C["ids"], g))
                v.tensor_copy(row[:, :, 2 * D], wt[:, :]).then_inc(S["row"], 1)
                step.end()

            variance(0, 0, 0)
            with v.Fori(0, G // NB - 1) as u:
                for b in range(NB):
                    variance(u * NB + b + 1, (b + 1) % NB, u + (b + 1) // NB)
                    write(u * NB + b, b, u)
            for b in range(NB):
                if b < NB - 1:
                    variance(G - NB + b + 1, b + 1, G // NB - 1)
                write(G - NB + b, b, G // NB - 1)


def select_rows(nc, T, C):
    COLS = NP // P
    NB = 4
    assert G % NB == 0
    with Stage(nc) as c:
        u_t = sb(c, nc, "s_u", [P, COLS])
        junk = sb(c, nc, "s_junk", [P, COLS])
        eq = sb(c, nc, "s_eq", [P, COLS])
        pre = sb(c, nc, "s_pre", [P, COLS])
        sel = sb(c, nc, "s_sel", [P, COLS])
        egs = sb(c, nc, "s_egs", [P, G])
        tot = sb(c, nc, "s_tot", [P, G])
        one = sb(c, nc, "s_one", [P, COLS])
        cnt = sb(c, nc, "s_cnt", [P, 1])
        sg = sb(c, nc, "s_sg", [P, 1])
        want = sb(c, nc, "s_want", [P, 1])
        bit = sb(c, nc, "s_bit", [P, 2])
        thr = sb(c, nc, "s_thr", [P, 1], I32)
        cand = sb(c, nc, "s_cand", [P, 1], I32)
        add = sb(c, nc, "s_add", [P, 1], I32)
        rows_t = sb(c, nc, "s_rows", [P, NB, J, SW])
        io = sb(c, nc, "s_io", [P, NB, J], I32)
        pad = sb(c, nc, "s_pad", [P, SW])
        pc = ps(c, nc, "s_pc", [P, 512])
        pp = ps(c, nc, "s_pp", [P, 512])
        names = ("init", "cnt", "tot", "loop", "go", "io", "step", "pad", "padded")
        S = {n: sem(c, nc, "s_s_" + n) for n in names}
        r_in = [sem(c, nc, f"s_r_in{b}") for b in range(NB)]
        sent = [sem(c, nc, f"s_sent{b}") for b in range(NB)]
        tick = sem(c, nc, "s_tick")
        block = c.enter_context(nc.Block())
        BITS = 31
        last = SB * GROUP + GROUP

        @block.sync
        def _(sp):
            sp.wait_ge(S["pad"], 1)
            for n, a in enumerate(range(SEL, last, P)):
                k = min(P, last - a)
                sp.dma_start(T["packed"][a:a + k, :], pad[0:k, :]).then_inc(S["padded"], 16)
            sp.wait_ge(S["padded"], 16 * (n + 1))
            with sp.Fori(0, G // NB) as u:
                for b in range(NB):
                    sp.wait_ge(sent[b], u * (16 * J))
                    sp.dma_start(rows_t[:, b], rows(T["sel"], u * NB + b)).then_inc(r_in[b], 16)

        @block.gpsimd
        def _(pool):
            with pool.Fori(0, G // NB) as u:
                for b in range(NB):
                    wait_all(pool, tick, (S["io"], u * NB + b + 1), (r_in[b], u * 16 + 16))
                    for j in range(J):
                        pool.indirect_dma_start(T["packed"], bass.IndirectOffsetOnAxis(ap=io[:, b, j:j + 1], axis=0),
                                                rows_t[:, b, j, :], None, bounds_check=SEL - 1, oob_is_err=False).then_inc(sent[b], 16)
            for b in range(NB):
                pool.wait_ge(sent[b], 16 * J * (G // NB))

        @block.tensor
        def _(pe):
            with pe.Fori(0, BITS + 2) as n:
                pe.wait_ge(S["cnt"], n + 1)
                pe.matmul(pc[:, 0:1], C["ones"][:, :], cnt[:, :], start=True, stop=True).then_inc(S["tot"], 1)
            pe.wait_ge(S["cnt"], BITS + 3)
            pe.matmul(pp[:, 0:G], C["tri"][:, :], egs[:, :], start=True, stop=True)
            pe.matmul(pp[:, 256:256 + G], C["ones"][:, :], egs[:, :], start=True, stop=True).then_inc(S["tot"], 1)
            pe.wait_ge(S["cnt"], BITS + 4)
            pe.matmul(pc[:, 0:1], C["tri"][:, :], cnt[:, :], start=True, stop=True).then_inc(S["tot"], 1)

        @block.scalar
        def _(act):
            act.wait_ge(S["go"], 1)
            with act.Fori(0, G // NB) as u:
                for b in range(NB):
                    act.wait_ge(sent[b], u * (16 * J))
                    act.copy(io[:, b, :], cols(pre, u * NB + b)).then_inc(S["io"], 1)

        @block.vector
        def _(v):
            step = Steps(v, S["step"])
            valid = C["valid_cols"]
            w = C["wsel"]
            step.then(v.memset(pad[:, :], 0.0))
            step.then(v.memset(cnt[:, :], FAR))
            v.tensor_copy(pad[:, 2 * D + 1:2 * D + 2].bitcast(I32), cnt[:, :]).then_inc(S["pad"], 1)
            v.memset(one[:, :], 1.0)
            step.then(v.tensor_scalar(junk[:, :], w[:, :], 0.0, None, ALU.is_ge))
            step.then(v.tensor_tensor(junk[:, :], junk[:, :], valid[:, :], ALU.mult))
            v.tensor_reduce(cnt[:, :], junk[:, :], AX.X, ALU.add).then_inc(S["cnt"], 1)
            v.wait_ge(S["tot"], 1)
            step.then(v.tensor_scalar(sg[:, :], pc[:, 0:1], float(SEL), None, ALU.is_ge))
            step.then(v.tensor_scalar(want[:, :], sg[:, :], float(SEL - (N - SEL + 1)), float(N - SEL + 1), ALU.mult, ALU.add))
            step.then(v.tensor_scalar(sg[:, :], sg[:, :], 2.0, -1.0, ALU.mult, ALU.add))
            step.then(v.tensor_scalar(u_t[:, :], w[:, :], sg[:, 0:1], None, ALU.mult))
            step.then(v.tensor_tensor(u_t[:, :], u_t[:, :], valid[:, :], ALU.mult))
            step.then(v.tensor_scalar(junk[:, :], valid[:, :], 1.0, 3.0e38, ALU.subtract, ALU.mult))
            step.then(v.tensor_tensor(u_t[:, :], u_t[:, :], junk[:, :], ALU.add))
            step.then(v.memset(thr[:, :], 0))
            step.then(v.memset(bit[:, 0:1], float(1 << 30)))
            per = 6
            with v.Fori(0, BITS) as n:
                turn = Steps(v, S["loop"], n, per)
                turn.then(v.tensor_copy(add[:, :], bit[:, 0:1]))
                turn.then(v.tensor_tensor(cand[:, :], thr[:, :], add[:, :], ALU.bitwise_or))
                turn.then(v.tensor_scalar(junk[:, :], u_t[:, :], cand[:, 0:1].bitcast(F32), None, ALU.is_ge))
                v.tensor_reduce(cnt[:, :], junk[:, :], AX.X, ALU.add).then_inc(S["cnt"], 1)
                v.wait_ge(S["tot"], n + 2)
                turn.then(v.tensor_scalar(bit[:, 1:2], pc[:, 0:1], want[:, 0:1], bit[:, 0:1], ALU.is_ge, ALU.mult))
                turn.then(v.tensor_copy(add[:, :], bit[:, 1:2]))
                v.tensor_scalar(bit[:, 0:1], bit[:, 0:1], 0.5, None, ALU.mult)
                turn.then(v.tensor_tensor(thr[:, :], thr[:, :], add[:, :], ALU.bitwise_or))
                turn.end()
            step.then(v.tensor_tensor(bit[:, 0:1], thr[:, :].bitcast(F32), sg[:, :], ALU.mult))
            step.then(v.tensor_scalar(sel[:, :], w[:, :], bit[:, 0:1], None, ALU.is_gt))
            step.then(v.tensor_tensor(sel[:, :], sel[:, :], valid[:, :], ALU.mult))
            v.tensor_reduce(cnt[:, :], sel[:, :], AX.X, ALU.add).then_inc(S["cnt"], 1)
            step.then(v.tensor_scalar(eq[:, :], w[:, :], bit[:, 0:1], None, ALU.is_equal))
            step.then(v.tensor_tensor(eq[:, :], eq[:, :], valid[:, :], ALU.mult))
            v.wait_ge(S["tot"], BITS + 2)
            step.then(v.tensor_scalar(want[:, :], pc[:, 0:1], -1.0, float(SEL), ALU.mult, ALU.add))
            v.tensor_reduce(egs[:, :], eq[:, :].rearrange("p (g j) -> p g j", j=J), AX.X, ALU.add).then_inc(S["cnt"], 1)
            v.wait_ge(S["tot"], BITS + 3)
            step.then(v.tensor_copy(tot[:, :], pp[:, 256:256 + G]))
            step.then(v.tensor_tensor_scan(egs[:, :], one[:, 0:G], tot[:, :], 0.0, ALU.mult, ALU.add))
            step.then(v.tensor_tensor(egs[:, :], egs[:, :], tot[:, :], ALU.subtract))
            step.then(v.tensor_tensor(egs[:, :], egs[:, :], pp[:, 0:G], ALU.add))
            p4, e4 = pre[:, :].rearrange("p (g j) -> p g j", j=J), eq[:, :].rearrange("p (g j) -> p g j", j=J)
            step.then(v.tensor_copy(p4[:, :, 0], egs[:, :]))
            for j in range(1, J):
                step.then(v.tensor_tensor(p4[:, :, j], p4[:, :, j - 1], e4[:, :, j - 1], ALU.add))
            step.then(v.scalar_tensor_tensor(pre[:, :], pre[:, :], want[:, 0:1], eq[:, :], ALU.is_lt, ALU.mult))
            step.then(v.tensor_tensor(sel[:, :], sel[:, :], pre[:, :], ALU.add))
            v.tensor_reduce(cnt[:, :], sel[:, :], AX.X, ALU.add).then_inc(S["cnt"], 1)
            step.then(v.tensor_tensor_scan(pre[:, :], one[:, :], sel[:, :], 0.0, ALU.mult, ALU.add))
            v.wait_ge(S["tot"], BITS + 4)
            step.then(v.tensor_scalar(pre[:, :], pre[:, :], pc[:, 0:1], -1.0, ALU.add, ALU.add))
            step.then(v.tensor_scalar(junk[:, :], sel[:, :], -FAR, FAR, ALU.mult, ALU.add))
            v.tensor_tensor(pre[:, :], pre[:, :], junk[:, :], ALU.add).then_inc(S["go"], 1)


def build(nc, T):
    def scratch(name, shape):
        T[name] = nc.dram_tensor("t_" + name, shape, F32).ap()

    for name in ("xn", "agg", "x1", "x2", "hp", "pq"):
        scratch(name, (NP, D))
    scratch("slots", ((EXPERTS * MB + 1) * MT * J, D))
    scratch("y", (EXPERTS * MROWS, D))
    scratch("sc1", (NP, 2 * GH))
    scratch("sc2", (NP, 2))
    scratch("sel", (NP, SW))
    scratch("packed", ((SB + 1) * GROUP, SW))
    scratch("w_edges", (GH, EP))
    scratch("ends", (2 * GH, P))
    scratch("starts", (GH, P + 1))
    with ExitStack() as c:
        C = {}
        for name, shape, dt in (
            ("ident", [P, P], F32), ("tri", [P, P], F32), ("ones", [P, P], F32), ("heads", [P, P], F32),
            ("valid", [P, G], F32), ("valid_cols", [P, NP // P], F32), ("ids", [P, NP // P], I32),
            ("wl", [P, KC, D], F32), ("wr", [P, KC, D], F32), ("kv", [P, KC, P + 1], F32),
            ("src_i", [P, ET + EU], I32), ("out_i", [P, ET], I32), ("dst_f", [P, ET], F32), ("carry_f", [P, ET], F32),
            ("lane_i", [P, ET + EU, 2], I32), ("same_prev", [P, ET], F32), ("same_next", [P, ET], F32),
            ("cut_prev", [P, ET], F32), ("cut_next", [P, ET], F32), ("all_prev", [P, 1], F32), ("all_next", [P, 1], F32),
            ("cut_whole", [P, 1], F32), ("gap", [P, NP // P, EXPERTS], F32), ("kept", [P, NP // P], F32),
            ("from", [P, NP // P], F32), ("w", [P, NP // P], F32), ("wsel", [P, NP // P], F32),
            ("tokens", [P, EXPERTS], I32), ("edge_w", [P, ET, GH], F32), ("edge_w1", [P, ET, 1], F32),
        ):
            C[name] = sb(c, nc, "k_" + name, shape, dt)
        stages = (
            lambda: load_constants(nc, T, C),
            lambda: norm_rows(nc, T, C),
            lambda: mean_weights(nc, T, C, C["edge_w1"]),
            lambda: aggregate(nc, T, C, "e0", T["xn"], 1, C["edge_w1"], HeadGram),
            lambda: update_and_gate(nc, T, C),
            lambda: two_layers(nc, T, C, "m0", EXPERTS, MB // 2, MB % 2, MT, D, T["slots"], T["moe_w1"], T["moe_b1"], T["moe_w2"],
                               T["moe_b2"], ACT.Relu, True, T["y"]),
            lambda: combine_and_project(nc, T, C),
            lambda: edge_softmax(nc, T, C, "e1", T["sc1"], GH, C["edge_w"], AttentionSums),
            lambda: aggregate(nc, T, C, "e2", T["hp"], GH, C["edge_w"]),
            lambda: second_features(nc, T, C),
            lambda: edge_softmax(nc, T, C, "e3", T["sc2"], 1, C["edge_w1"], AttentionRows),
            lambda: aggregate(nc, T, C, "e4", T["hp"], 1, C["edge_w1"]),
            lambda: second_update(nc, T, C),
            lambda: select_rows(nc, T, C),
            lambda: two_layers(nc, T, C, "m1", 1, SB // 2, 0, P, SW, T["packed"], T["ffn_w1"], T["ffn_b1"], T["ffn_w2"],
                               T["ffn_b2"], ACT.Gelu_apprx_tanh, False, T["out"]),
        )
        for stage in stages:
            stage()


def layout(i):
    def f(name):
        return np.ascontiguousarray(i[name])

    x = np.zeros((NP, D), np.float32)
    x[:N] = f("x")
    src, dst = f("src").astype(np.int32, copy=False), f("dst").astype(np.int32, copy=False)

    def edges(a, before, after, shift):
        out = np.full(EP + 2, after, np.int32)
        out[0] = out[EP + 1] = before
        out[1:E + 1] = a
        return out[1 + shift:1 + shift + EP]

    far = 32767
    key, prev, nxt = (edges(dst, -1, far, s) for s in (0, -1, 1))
    src_p, dst_p = edges(src, 0, 0, 0), edges(dst, 0, 0, 0)

    def tile(a):
        return np.ascontiguousarray(a.reshape(ET, P).T)

    def lane(a):
        return np.ascontiguousarray(a.reshape(P, ET))

    def scores(a_src, a_dst):
        h, n = a_src.shape
        out = np.zeros((h * n, 2 * h), np.float32)
        for k in range(h):
            out[k * n:(k + 1) * n, k] = a_src[k]
            out[k * n:(k + 1) * n, h + k] = a_dst[k]
        return out

    p, q = np.arange(P)[:, None], np.arange(P)[None, :]
    row = (np.arange(G)[None, :, None] * GROUP + np.arange(P)[:, None, None] * J + np.arange(J)[None, None, :])
    last = np.zeros((P, 2), np.float32)
    last[:, 1] = -5.0
    last[P - 1] = (1.0, 0.0)
    ev = np.stack([np.arange(EXPERTS, 0, -1), np.arange(EXPERTS) * MROWS]).astype(np.float32)
    src_tile = np.zeros((P, ET + EU), np.int32)
    src_tile[:, :ET] = tile(src_p)
    return {
        "x": x,
        "W_l_t": np.ascontiguousarray(f("L0_gnn_W_l").T), "W_r_t": np.ascontiguousarray(f("L0_gnn_W_r").T), "b_r": f("L0_gnn_b_r"),
        "kln_weight": np.ascontiguousarray(f("L0_mix_kln_weight").reshape(KC, P).T),
        "kln_bias": np.ascontiguousarray(f("L0_mix_kln_bias").reshape(KC, P).T),
        "vln_weight": f("L0_mix_vln_weight").reshape(-1), "vln_bias": f("L0_mix_vln_bias").reshape(-1),
        "gate_w": f("L0_ffn_gate_w"), "gate_b": f("L0_ffn_gate_b"),
        "moe_w1": f("L0_ffn_w1"), "moe_w2": f("L0_ffn_w2"), "moe_b2": f("L0_ffn_b2"),
        "moe_b1": np.ascontiguousarray(f("L0_ffn_b1").reshape(EXPERTS, FF // P, P).transpose(0, 2, 1)),
        "W1_t": np.ascontiguousarray(f("L1_gnn_W1").T), "W1": f("L1_gnn_W1"), "a1": scores(f("L1_gnn_a1_src"), f("L1_gnn_a1_dst")),
        "W2_t": np.ascontiguousarray(f("L1_gnn_W2").T), "W2": f("L1_gnn_W2"), "a2": scores(f("L1_gnn_a2_src"), f("L1_gnn_a2_dst")),
        "wq": f("L1_mix_wq"), "wk": f("L1_mix_wk"), "wv": f("L1_mix_wv"), "wo": f("L1_mix_wo"),
        "b_qk": np.concatenate([f("L1_mix_bq"), f("L1_mix_bk")]), "bv": f("L1_mix_bv"), "bo": f("L1_mix_bo"),
        "ffn_wr": f("L1_ffn_wr"), "ffn_br": f("L1_ffn_br"), "ffn_w1": f("L1_ffn_w1")[None], "ffn_w2": f("L1_ffn_w2")[None],
        "ffn_b1": np.ascontiguousarray(f("L1_ffn_b1").reshape(1, FF // P, P).transpose(0, 2, 1)), "ffn_b2": f("L1_ffn_b2")[None],
        "keys": key, "dst_tile": tile(key), "next_tile": tile(nxt), "src_tile": src_tile,
        "lane_i": np.pad(np.stack([lane(src_p), lane(dst_p)], axis=2), ((0, 0), (0, EU), (0, 0))),
        "key_lane": lane(key), "prev_lane": lane(prev), "next_lane": lane(nxt),
        "c_ident": np.eye(P, dtype=np.float32), "c_tri": (p < q).astype(np.float32),
        "c_heads": (p // HC == q // HC).astype(np.float32), "c_last": last,
        "c_valid": (row[:, :, 0] < N).astype(np.float32), "c_valid_cols": (row < N).reshape(P, -1).astype(np.float32),
        "c_ids": np.where(row < N, row, int(FAR)).reshape(P, -1).astype(np.int32),
        "c_experts": np.ascontiguousarray(np.broadcast_to(ev, (P, 2, EXPERTS))),
    }


def kernel(**inputs):
    import concourse.bacc as bacc
    from concourse.bass_utils import run_bass_kernel_spmd

    nc = bacc.Bacc("TRN2", target_bir_lowering=False, num_devices=1)
    arrays, T = {}, {}
    for name, a in layout(inputs).items():
        arrays["in_" + name] = a
        T[name] = nc.dram_tensor("in_" + name, a.shape, mybir.dt.from_np(a.dtype), kind="ExternalInput").ap()
    T["out"] = nc.dram_tensor("out", (NP, D), F32, kind="ExternalOutput").ap()
    build(nc, T)
    r = run_bass_kernel_spmd(nc, [arrays], core_ids=[0])
    return r.results[0]["out"][:N]
```
